# Optimizing a Trainium2 kernel written in Bass

```python
import numpy as np
import jax
import jax.numpy as jnp

def _softmax(x, axis=-1):
    return jax.nn.softmax(x, axis=axis)

def _gelu(x):
    return jax.nn.gelu(x, approximate=True)

def _silu(x):
    return jax.nn.silu(x)

def _sigmoid(x):
    return jax.nn.sigmoid(x)

def _layernorm(x, axis=-1, eps=1e-05):
    m = jnp.mean(x, axis=axis, keepdims=True)
    v = jnp.var(x, axis=axis, keepdims=True)
    return (x - m) / jnp.sqrt(v + eps)

def _scatter_add(tgt, idx, src, axis=0):
    return tgt.at[idx].add(src)

def _segment_sum(src, seg, n):
    return jax.ops.segment_sum(src, seg, n)
kernel_name = 'mk_gps_d1_gnn_r8_1de4e1'

def setup_inputs(seed: int=0):
    np.random.seed(seed)
    _w = jnp.asarray

    def _rec_inputs():
        import jax
        import jax.numpy as jnp
        _gk = jax.random.key(seed)
        x = -0.000125 + 0.9999 * jax.random.normal(jax.random.fold_in(_gk, 1), (8192, 512), jnp.float32)
        _s = jax.random.randint(jax.random.fold_in(_gk, 2), (65536,), 0, 8192, jnp.int32)
        _d = jax.random.randint(jax.random.fold_in(_gk, 3), (65536,), 0, 8192, jnp.int32)
        _loop = jnp.arange(8192, dtype=jnp.int32)
        src = jnp.concatenate([_s, _d, _loop])
        dst = jnp.concatenate([_d, _s, _loop])
        _o = jnp.argsort(dst, stable=True)
        src = src[_o]
        dst = dst[_o]
        edge_weight = jax.random.uniform(jax.random.fold_in(_gk, 12), (139264,), jnp.float32, 0.0, 0.999998)
        return (x, src, dst, edge_weight)
    x, src, dst, edge_weight = _rec_inputs()

    def _L0_gnn_setup():
        import jax, jax.numpy as jnp
        import numpy as np
        N_NODES = 8192
        N_EDGES = 65536
        FEAT_DIM = 512
        EMBED_DIM = 512
        key = jax.random.key(seed)
        k1, k2, k3, k4, k5 = jax.random.split(key, 5)
        x = jax.random.normal(k1, (N_NODES, FEAT_DIM), dtype=jnp.float32)
        limit = float(np.sqrt(6.0 / (EMBED_DIM + FEAT_DIM)))
        weight = jax.random.uniform(k2, (EMBED_DIM, FEAT_DIM), dtype=jnp.float32, minval=-limit, maxval=limit)
        row = jax.random.randint(k3, (N_EDGES,), 0, N_NODES, dtype=jnp.int64)
        col = jax.random.randint(k4, (N_EDGES,), 0, N_NODES, dtype=jnp.int64)
        vals = jax.random.uniform(k5, (N_EDGES,), dtype=jnp.float32)
        return {'x': x, 'weight': weight, 'row': row, 'col': col, 'vals': vals}
    _L0_gnn_all = _L0_gnn_setup()
    _L0_gnn_in = {k: v for k, v in _L0_gnn_all.items() if k in ('weight',)}
    del _L0_gnn_all

    def _L0_mix_setup():
        import jax, jax.numpy as jnp
        import numpy as np
        NUM_HEADS = 8
        key = jax.random.key(seed)
        k1, k2, k3 = jax.random.split(key, 3)
        B, N, C = (4, 512, 512)
        x = jax.random.normal(k1, (B, N, C), dtype=jnp.float32)
        w_qkv = jax.random.normal(k2, (C, 3 * C), dtype=jnp.float32) * (1.0 / np.sqrt(C))
        w_proj = jax.random.normal(k3, (C, C), dtype=jnp.float32) * (1.0 / np.sqrt(C))
        b_proj = jnp.zeros((C,), dtype=jnp.float32)
        return {'x': x, 'w_qkv': w_qkv, 'w_proj': w_proj, 'b_proj': b_proj}
    _L0_mix_all = _L0_mix_setup()
    _L0_mix_in = {k: v for k, v in _L0_mix_all.items() if k in ('w_qkv', 'w_proj', 'b_proj')}
    del _L0_mix_all

    def _L0_ffn_setup():
        import jax, jax.numpy as jnp
        import numpy as np
        B, S, D, F, E, NS, K = (2, 256, 512, 256, 8, 2, 2)
        key = jax.random.key(seed)
        ks = jax.random.split(key, 6)
        scale = 0.02

        def p(k, shape):
            return jax.random.normal(k, shape, jnp.float32) * scale
        return {'x': jax.random.normal(ks[0], (B, S, D), jnp.float32), 'gate_w': p(ks[1], (E, D)), 'gate_b': jnp.zeros((E,), jnp.float32), 'sw1': p(ks[2], (NS, F, D)), 'sb1': jnp.zeros((NS, F), jnp.float32), 'sw2': p(ks[3], (NS, D, F)), 'sb2': jnp.zeros((NS, D), jnp.float32), 'rw1': p(ks[4], (E, F, D)), 'rb1': jnp.zeros((E, F), jnp.float32), 'rw2': p(ks[5], (E, D, F)), 'rb2': jnp.zeros((E, D), jnp.float32)}
    _L0_ffn_all = _L0_ffn_setup()
    _L0_ffn_in = {k: v for k, v in _L0_ffn_all.items() if k in ('gate_w', 'gate_b', 'sw1', 'sb1', 'sw2', 'sb2', 'rw1', 'rb1', 'rw2', 'rb2')}
    del _L0_ffn_all
    return {'x': x, 'src': src, 'dst': dst, 'edge_weight': edge_weight, 'L0_gnn_weight': _L0_gnn_in['weight'], 'L0_mix_w_qkv': _L0_mix_in['w_qkv'], 'L0_mix_w_proj': _L0_mix_in['w_proj'], 'L0_mix_b_proj': _L0_mix_in['b_proj'], 'L0_ffn_gate_w': _L0_ffn_in['gate_w'], 'L0_ffn_gate_b': _L0_ffn_in['gate_b'], 'L0_ffn_sw1': _L0_ffn_in['sw1'], 'L0_ffn_sb1': _L0_ffn_in['sb1'], 'L0_ffn_sw2': _L0_ffn_in['sw2'], 'L0_ffn_sb2': _L0_ffn_in['sb2'], 'L0_ffn_rw1': _L0_ffn_in['rw1'], 'L0_ffn_rb1': _L0_ffn_in['rb1'], 'L0_ffn_rw2': _L0_ffn_in['rw2'], 'L0_ffn_rb2': _L0_ffn_in['rb2']}

def reference(x, src, dst, edge_weight, L0_gnn_weight, L0_mix_w_qkv, L0_mix_w_proj, L0_mix_b_proj, L0_ffn_gate_w, L0_ffn_gate_b, L0_ffn_sw1, L0_ffn_sb1, L0_ffn_sw2, L0_ffn_sb2, L0_ffn_rw1, L0_ffn_rb1, L0_ffn_rw2, L0_ffn_rb2):
    import jax
    import jax.numpy as jnp

    def _L0_gnn_ref(x, weight, row, col, vals):
        import jax, jax.numpy as jnp
        import numpy as np
        N_NODES = 8192
        N_EDGES = 65536
        FEAT_DIM = 512
        EMBED_DIM = 512
        h = jnp.einsum('nf,ef->ne', x, weight)
        msgs = vals[:, None] * h[col]
        out = jax.ops.segment_sum(msgs, row, num_segments=N_NODES)
        return out

    def _L0_mix_ref(x, w_qkv, w_proj, b_proj):
        import jax, jax.numpy as jnp
        import numpy as np
        NUM_HEADS = 8
        B, N, C = x.shape
        H = NUM_HEADS
        D = C // H
        qkv = (x @ w_qkv).reshape(B, N, 3, H, D)
        qkv = jnp.transpose(qkv, (2, 0, 3, 1, 4))
        q, k, v = (qkv[0], qkv[1], qkv[2])
        q = jax.nn.softmax(q, axis=-1)
        k = jax.nn.softmax(jax.nn.elu(k) + 1.0, axis=-2)
        context = jnp.einsum('bhnd,bhne->bhde', k, v)
        out = jnp.einsum('bhnd,bhde->bhne', q, context)
        out = jnp.transpose(out, (0, 2, 1, 3)).reshape(B, N, C)
        return out @ w_proj + b_proj

    def _L0_ffn_ref(x, gate_w, gate_b, sw1, sb1, sw2, sb2, rw1, rb1, rw2, rb2):
        import jax, jax.numpy as jnp
        import numpy as np
        B, S, D, F, E, NS, K = (2, 256, 512, 256, 8, 2, 2)
        b, s, d = x.shape
        t = x.reshape(-1, d)
        T = t.shape[0]
        hs = jax.nn.gelu(jnp.einsum('td,nfd->ntf', t, sw1) + sb1[:, None, :], approximate=False)
        shared = jnp.einsum('ntf,ndf->td', hs, sw2) + sb2.sum(axis=0)
        logits = t @ gate_w.T + gate_b
        probs = jax.nn.softmax(logits, axis=-1)
        top_v, top_i = jax.lax.top_k(probs, K)
        cw = jnp.zeros_like(probs).at[jnp.arange(T)[:, None], top_i].add(top_v)
        hr = jax.nn.gelu(jnp.einsum('td,efd->etf', t, rw1) + rb1[:, None, :], approximate=False)
        oe = jnp.einsum('etf,edf->etd', hr, rw2) + rb2[:, None, :]
        routed = jnp.einsum('etd,te->td', oe, cw)
        return (shared + routed).reshape(b, s, d)
    xn = _layernorm(x, axis=-1)
    x = x + _L0_gnn_ref(xn, L0_gnn_weight, src, dst, edge_weight) + _L0_mix_ref(xn[None], L0_mix_w_qkv, L0_mix_w_proj, L0_mix_b_proj)[0]
    x = x + _L0_ffn_ref(_layernorm(x, axis=-1)[None], L0_ffn_gate_w, L0_ffn_gate_b, L0_ffn_sw1, L0_ffn_sb1, L0_ffn_sw2, L0_ffn_sb2, L0_ffn_rw1, L0_ffn_rb1, L0_ffn_rw2, L0_ffn_rb2)[0]
    return x

_drawn_inputs = setup_inputs


def setup_inputs(seed=0):
    import zlib

    import numpy as np

    out = dict(_drawn_inputs(seed))
    spreads = {'L0_mix_b_proj': (0.0, 2.0),
     'L0_ffn_gate_b': (0.0, 0.8),
     'L0_ffn_sb1': (0.0, 2.0),
     'L0_ffn_sb2': (0.0, 2.0),
     'L0_ffn_rb1': (0.0, 2.0),
     'L0_ffn_rb2': (0.0, 2.0)}
    factors = {'L0_mix_w_qkv': 8.0,
     'L0_mix_w_proj': 8.0,
     'L0_ffn_gate_w': 4.647,
     'L0_ffn_rw1': 6.564,
     'L0_ffn_rw2': 6.13,
     'L0_ffn_sw1': 8.0,
     'L0_ffn_sw2': 7.585}
    for name, (base, spread) in spreads.items():
        noise = np.random.default_rng([zlib.crc32(name.encode()), seed]).standard_normal(out[name].shape)
        drawn = base * np.exp(spread * noise) if base else spread * noise
        out[name] = jnp.asarray(drawn.astype(out[name].dtype))
    for name, factor in factors.items():
        out[name] = (out[name] * factor).astype(out[name].dtype)
    return out
```

```python
from contextlib import ExitStack

import concourse.bass as bass
import numpy as np
from concourse import mybir

F32 = mybir.dt.float32
I32 = mybir.dt.int32
U32 = mybir.dt.uint32
F16 = mybir.dt.float16
ALU = mybir.AluOpType
ACT = mybir.ActivationFunctionType
AX = mybir.AxisListType

P = 128
N, D = 8192, 512
E = 139264
K = D // P
TILES = N // P
BLK = 4
BLOCKS = TILES // BLK
ROWS = E // P
FULL = ROWS // P
REST = ROWS - FULL * P
GROUPS = FULL + (REST > 0)
MACRO = ROWS // 2
STEPS = 10
ALL_STEPS = STEPS * TILES
assert ALL_STEPS >= MACRO + TILES - 1
CHUNKS = 2 * STEPS
COLS = CHUNKS * TILES
HEADS, HD = 8, 64
SHARED, ROUTED, FF = 2, 8, 256
EXPERTS = SHARED + ROUTED
FC = FF // P
EPS = 1e-5
GATHERS = 10
MRING = 8
ARING = 4


def wait_apart(eng, passed, sem, value):
    eng.wait_ge(sem, value)
    eng.sem_inc(passed, 1)


def turns(eng, count):
    yield 0
    with eng.Fori(1, count) as it:
        yield it


def ranks_stage(nc, A, T, S):
    ctx = ExitStack()
    sb = lambda name, shape, dt=F32: ctx.enter_context(nc.sbuf_tensor(name, shape, dt))
    pb = lambda name, shape: ctx.enter_context(nc.psum_tensor(name, shape, F32))
    UNIT = 32
    UNITS = ROWS // UNIT
    UW = UNIT * TILES
    assert UW == 4 * 512 and UNITS % 2 == 0
    with ctx:
        raw_i = sb("raw_i", [P, 2, GROUPS, P], I32)
        raw = sb("raw", [P, 3, GROUPS, P])
        src_i = sb("src_i", [P, ROWS], I32)
        tile_c = sb("tile_c", [P, ROWS])
        hot = sb("hot_tiles", [P, ROWS, TILES], F16)
        ones = sb("ones_r", [P, P], F16)
        onesf = sb("onesf_r", [1, 1])
        before = sb("before", [P, P], F16)
        weigh = sb("weigh", [2, P], F16)
        cnt = sb("cnt", [P, GROUPS, TILES], F16)
        total = sb("total", [P, TILES])
        upto = sb("upto", [P, TILES])
        start = sb("start", [P, TILES])
        zeros = sb("zeros_r", [P, TILES])
        carry = sb("carry", [P, TILES])
        carry_i = sb("carry_i", [P, GROUPS, TILES], I32)
        part_i = sb("part_i", [P, 2, GROUPS, TILES], I32)
        part = sb("part", [P, 2, GROUPS, TILES], F16)
        aux = sb("aux", [2, 2, UW], F16)
        cnt_row = aux[0:1, :, :]
        flat = raw[:, :, :, :].rearrange("p a g c -> p (a g c)")
        prod = flat[:, 0:UW]
        place = flat[:, UW:UW + ROWS]
        ps = pb("ps_r", [P, 2, UW])

        with nc.Block() as block:
            @block.sync
            def _(sp):
                for a, name in enumerate(("src", "dst")):
                    v = A[name].rearrange("(r c) -> r c", c=P)
                    sp.dma_start(raw_i[:, a, 0:FULL, :], v[0:FULL * P, :].rearrange("(g p) c -> p g c", p=P)).then_inc(S["e_load"], 16)
                    sp.dma_start(raw_i[0:REST, a, FULL, :], v[FULL * P:ROWS, :]).then_inc(S["e_load"], 16)
                v = A["edge_weight"].rearrange("(r c) -> r c", c=P)
                sp.dma_start(raw[:, 2, 0:FULL, :], v[0:FULL * P, :].rearrange("(g p) c -> p g c", p=P)).then_inc(S["e_load"], 16)
                sp.dma_start(raw[0:REST, 2, FULL, :], v[FULL * P:ROWS, :]).then_inc(S["e_load"], 16)
                for it in turns(sp, UNITS // 2):
                    for u in range(2):
                        n = it * 2 + u
                        sp.wait_ge(S["r_cnt"], n + 3)
                        sp.dma_start(A["cnt"][bass.ds(n, 1), :], cnt_row[:, u, :]).then_inc(S["r_cst"][u], 16)
                for u in range(2):
                    sp.wait_ge(S["r_cst"][u], 16 * (UNITS // 2))
                cv = A["cnt"].rearrange("n (c t) -> (n c) t", t=TILES)
                sp.dma_start(cnt[:, 0:FULL, :], cv[0:FULL * P, :].rearrange("(g p) t -> p g t", p=P)).then_inc(S["r_cld"], 16)
                sp.dma_start(cnt[0:REST, FULL, :], cv[FULL * P:ROWS, :]).then_inc(S["r_cld"], 16)
                sp.wait_ge(S["r_part"], 1)
                for h in range(2):
                    av = A["aux"][h].rearrange("n (c t) -> (n c) t", t=TILES)
                    sp.dma_start(av[0:FULL * P, :].rearrange("(g p) t -> p g t", p=P), part[:, h, 0:FULL, :]).then_inc(S["r_ast"], 16)
                    sp.dma_start(av[FULL * P:ROWS, :], part[0:REST, h, FULL, :]).then_inc(S["r_ast"], 16)
                sp.wait_ge(S["r_ast"], 64)
                for it in turns(sp, UNITS // 2):
                    for u in range(2):
                        n = it * 2 + u
                        sp.wait_ge(S["r_rank"], n + 1)
                        sp.dma_start(aux[:, u, :], A["aux"][:, bass.ds(n, 1), :].rearrange("h o w -> h (o w)")).then_inc(S["r_ald"][u], 16)

            @block.gpsimd
            def _(pool):
                nc.gpsimd.iota(T.iota_i[:, :], pattern=[[1, P]], base=0, channel_multiplier=0).then_inc(S["e_iota"], 1)
                nc.gpsimd.memset(ones[:, :], 1.0).then_inc(S["e_iota"], 1)
                nc.gpsimd.memset(onesf[:, :], 1.0).then_inc(S["e_iota"], 1)
                nc.gpsimd.memset(zeros[:, :], 0.0).then_inc(S["e_iota"], 1)
                nc.gpsimd.memset(before[:, :], 1.0).then_inc(S["e_set"], 1)
                nc.gpsimd.memset(T.ident[:, :], 0.0).then_inc(S["e_set"], 1)
                nc.gpsimd.memset(weigh[:, :], 256.0).then_inc(S["e_set"], 1)
                pool.wait_ge(S["e_set"], 3)
                nc.gpsimd.affine_select(out=before[:, :], in_=before[:, :], compare_op=ALU.is_gt, fill=0.0, base=0,
                                        pattern=[[1, P]], channel_multiplier=-1).then_inc(S["e_iota"], 1)
                nc.gpsimd.affine_select(out=T.ident[:, :], in_=T.ident[:, :], compare_op=ALU.not_equal, fill=1.0, base=0,
                                        pattern=[[-1, P]], channel_multiplier=1).then_inc(S["e_iota"], 1)
                nc.gpsimd.affine_select(out=weigh[:, :], in_=weigh[:, :], compare_op=ALU.not_equal, fill=1.0, base=-1,
                                        pattern=[[0, P]], channel_multiplier=1).then_inc(S["e_iota"], 1)

            @block.scalar
            def _(act):
                for it in turns(act, UNITS // 2):
                    for u in range(2):
                        n = it * 2 + u
                        act.wait_ge(S["r_cps"], n + 1)
                        act.wait_ge(S["r_cst"][u], it * 16)
                        nc.scalar.copy(cnt_row[:, u, :], ps[0:1, u, :]).then_inc(S["r_cnt"], 1)

            @block.vector
            def _(dve):
                done = [0]

                def link(ins):
                    done[0] += 1
                    ins.then_inc(S["e_dve"], 1)
                    dve.wait_ge(S["e_dve"], done[0])

                dve.wait_ge(S["e_iota"], 7)
                nc.vector.tensor_copy(T.iota_f[:, :], T.iota_i[:, :])
                dve.wait_ge(S["e_load"], 16 * 6)
                for a in range(2):
                    nc.vector.tensor_copy(raw[:, a, 0:FULL, :], raw_i[:, a, 0:FULL, :])
                    link(nc.vector.tensor_copy(raw[0:REST, a, FULL, :], raw_i[0:REST, a, FULL, :]))
                nc.vector.sem_inc(S["r_raw"], 1)
                for a in range(3):
                    dve.wait_ge(S["r_tr"], a + 1)
                    link(nc.vector.tensor_copy(T.rec[:, :, a], ps[:, a % 2, 0:ROWS]))
                    nc.vector.sem_inc(S["r_trfree"], 1)
                link(nc.vector.tensor_copy(src_i[:, :], T.rec[:, :, 0]))
                link(nc.vector.tensor_scalar(src_i[:, :], src_i[:, :], 7, None, ALU.arith_shift_right))
                link(nc.vector.tensor_copy(tile_c[:, :], src_i[:, :]))
                with dve.Fori(0, UNITS) as n:
                    nc.vector.tensor_tensor(hot[:, bass.ds(n * UNIT, UNIT), :],
                                            tile_c[:, bass.ds(n * UNIT, UNIT)].unsqueeze(2).broadcast_to([P, UNIT, TILES]),
                                            T.iota_f[:, 0:TILES].unsqueeze(1).broadcast_to([P, UNIT, TILES]),
                                            ALU.is_equal).then_inc(S["r_hot"], 1)
                dve.wait_ge(S["r_tot"], 1)
                link(nc.vector.tensor_copy(total[:, :], ps[:, 0, 0:TILES]))
                link(nc.vector.tensor_tensor_scan(upto[:, :], total[:, :], zeros[:, :], 0.0, ALU.add, ALU.add))
                link(nc.vector.tensor_tensor(start[:, :], upto[:, :], total[:, :], ALU.subtract))
                nc.vector.sem_inc(S["r_start"], 1)
                dve.wait_ge(S["r_carry"], GROUPS)
                for g in range(GROUPS):
                    r = P if g < FULL else REST
                    link(nc.vector.tensor_tensor(carry[0:r, :], start[0:r, :], ps[0:r, 1, g * TILES:(g + 1) * TILES], ALU.add))
                    link(nc.vector.tensor_copy(carry_i[0:r, g, :], carry[0:r, :]))
                    link(nc.vector.tensor_scalar(part_i[0:r, 0, g, :], carry_i[0:r, g, :], 8, None, ALU.arith_shift_right))
                    link(nc.vector.tensor_scalar(part_i[0:r, 1, g, :], carry_i[0:r, g, :], 255, None, ALU.bitwise_and))
                    link(nc.vector.tensor_copy(part[0:r, :, g, :], part_i[0:r, :, g, :]))
                nc.vector.sem_inc(S["r_part"], 1)
                dve.wait_ge(S["r_bound"], 1)
                link(nc.vector.tensor_copy(T.bounds[:, :], ps[0:TILES, 0, 512:514]))
                nc.vector.sem_inc(S["r_bfree"], 1)
                for it in turns(dve, UNITS // 2):
                    for u in range(2):
                        n = it * 2 + u
                        dve.wait_ge(S["r_rps"], n + 1)
                        dve.wait_ge(S["r_place"], n)
                        nc.vector.tensor_tensor(prod[:, :], ps[:, u, :], hot[:, bass.ds(n * UNIT, UNIT), :].rearrange("p c t -> p (c t)"),
                                                ALU.mult).then_inc(S["r_rank"], 1)
                        dve.wait_ge(S["r_rank"], n + 3)
                        nc.vector.reduce_sum(place[:, bass.ds(n * UNIT, UNIT)], prod[:, :].rearrange("p (c t) -> p c t", t=TILES),
                                             AX.X).then_inc(S["r_place"], 1)
                dve.wait_ge(S["r_place"], UNITS)
                nc.vector.tensor_copy(T.place[:, :], place[:, :])

            @block.tensor
            def _(pe):
                pe.sem_inc(S["r_rank"], 2)
                pe.sem_inc(S["r_cnt"], 2)
                pe.wait_ge(S["e_iota"], 7)
                pe.wait_ge(S["r_raw"], 1)
                for a in range(3):
                    if a == 2:
                        pe.wait_ge(S["r_trfree"], 1)
                    for g in range(GROUPS):
                        r = P if g < FULL else REST
                        ins = nc.tensor.transpose(ps[:, a % 2, g * P:g * P + r], raw[0:r, a, g, :], T.ident[0:r, 0:r])
                    ins.then_inc(S["r_tr"], 1)
                pe.wait_ge(S["r_trfree"], 3)
                for it in turns(pe, UNITS // 2):
                    for u in range(2):
                        n = it * 2 + u
                        pe.wait_ge(S["r_hot"], n + 1)
                        pe.wait_ge(S["r_cnt"], n + 1)
                        for c in range(4):
                            ins = nc.tensor.matmul(ps[:, u, c * 512:(c + 1) * 512], ones[:, :],
                                                   hot[:, bass.ds(n * UNIT + c * 8, 8), :].rearrange("p c t -> p (c t)"),
                                                   start=True, stop=True)
                        ins.then_inc(S["r_cps"], 1)
                pe.wait_ge(S["r_cld"], 32)
                pe.wait_ge(S["r_cnt"], UNITS + 2)
                for g in range(GROUPS):
                    r = P if g < FULL else REST
                    ins = nc.tensor.matmul(ps[:, 0, 0:TILES], ones[0:r, :], cnt[0:r, g, :], start=(g == 0), stop=(g == GROUPS - 1))
                ins.then_inc(S["r_tot"], 1)
                for g in range(GROUPS):
                    r = P if g < FULL else REST
                    ins = nc.tensor.matmul(ps[0:r, 1, g * TILES:(g + 1) * TILES], before[0:r, 0:r], cnt[0:r, g, :],
                                           start=True, stop=(g == 0))
                    for e in range(g):
                        ins = nc.tensor.matmul(ps[0:r, 1, g * TILES:(g + 1) * TILES], ones[:, 0:r], cnt[:, e, :],
                                               start=False, stop=(e == g - 1))
                    ins.then_inc(S["r_carry"], 1)
                pe.wait_ge(S["r_start"], 1)
                nc.tensor.matmul(ps[0:TILES, 0, 512:513], start[0:1, :], onesf[:, :], start=True, stop=True)
                nc.tensor.matmul(ps[0:TILES, 0, 513:514], upto[0:1, :], onesf[:, :], start=True, stop=True).then_inc(S["r_bound"], 1)
                pe.wait_ge(S["r_bfree"], 1)
                for it in turns(pe, UNITS // 2):
                    for u in range(2):
                        n = it * 2 + u
                        pe.wait_ge(S["r_ald"][u], it * 16 + 16)
                        pe.wait_ge(S["r_rank"], n + 1)
                        for c in range(4):
                            w = slice(c * 512, (c + 1) * 512)
                            nc.tensor.matmul(ps[:, u, w], before[:, :], hot[:, bass.ds(n * UNIT + c * 8, 8), :].rearrange("p c t -> p (c t)"),
                                             start=True, stop=False)
                            ins = nc.tensor.matmul(ps[:, u, w], weigh[:, :], aux[:, u, w], start=False, stop=True)
                        ins.then_inc(S["r_rps"], 1)


def edges_stage(nc, A, T, S):
    ctx = ExitStack()
    sb = lambda name, shape, dt=F32: ctx.enter_context(nc.sbuf_tensor(name, shape, dt))
    pb = lambda name, shape: ctx.enter_context(nc.psum_tensor(name, shape, F32))
    with ctx:
        raw = sb("sorted", [P, GROUPS, P, 3])
        step_i = sb("step_i", [P, ALL_STEPS], I32)
        step_f = sb("step_f", [P, ALL_STEPS])
        ones = sb("ones_e", [P, P])
        upper = sb("upper", [TILES, TILES])
        se_i = sb("se_i", [TILES, 3], I32)
        sh_i = sb("sh_i", [TILES, 3], I32)
        sh_f = sb("sh_f", [TILES, 3])
        some = sb("some", [TILES, 1])
        span = sb("span", [TILES, 1])
        past = sb("past", [TILES, ALL_STEPS])
        delta = sb("delta", [TILES, 1])
        delta_w = sb("delta_w", [TILES, P])
        cum = sb("cum", [TILES, 1])
        row_of = sb("row_of", [P, ALL_STEPS, 2])
        chunk = sb("chunk", [P, ALL_STEPS])
        pidx_i = sb("pidx_i", [P, 1], I32)
        pidx = sb("pidx", [P, 1])
        pick = sb("pick", [P, GROUPS, COLS])
        base = sb("base", [P, ALL_STEPS])
        tile_f = sb("tile_f", [1, ALL_STEPS])
        big = pb("big", [P, 3 * 512])
        wide = pb("wide", [P, 4 * 512])
        small = pb("small", [P, 512])

        with nc.Block() as block:
            @block.sync
            def _(sp):
                v = A["recs"].rearrange("(r c) w -> r c w", c=P)
                sp.dma_start(raw[:, 0:FULL, :, :], v[0:FULL * P, :, :].rearrange("(g p) c w -> p g c w", p=P)).then_inc(S["d_load"], 16)
                sp.dma_start(raw[0:REST, FULL, :, :], v[FULL * P:ROWS, :, :]).then_inc(S["d_load"], 16)

            @block.gpsimd
            def _(pool):
                nc.gpsimd.iota(step_i[:, :], pattern=[[1, ALL_STEPS]], base=0, channel_multiplier=0).then_inc(S["d_iota"], 1)
                nc.gpsimd.iota(pidx_i[:, :], pattern=[[1, 1]], base=0, channel_multiplier=1).then_inc(S["d_iota"], 1)
                nc.gpsimd.memset(ones[:, :], 1.0).then_inc(S["d_iota"], 1)
                nc.gpsimd.memset(upper[:, :], 1.0).then_inc(S["d_set"], 1)
                pool.wait_ge(S["d_set"], 1)
                nc.gpsimd.affine_select(out=upper[:, :], in_=upper[:, :], compare_op=ALU.is_ge, fill=0.0, base=0,
                                        pattern=[[1, TILES]], channel_multiplier=-1).then_inc(S["d_iota"], 1)

            @block.vector
            def _(dve):
                done = [0]

                def link(ins):
                    done[0] += 1
                    ins.then_inc(S["d_dve"], 1)
                    dve.wait_ge(S["d_dve"], done[0])

                nc.vector.tensor_copy(se_i[:, 0:2], T.bounds[:, :])
                link(nc.vector.tensor_scalar(se_i[:, 2:3], T.bounds[:, 1:2], 255.0, None, ALU.add))
                link(nc.vector.tensor_scalar(sh_i[:, :], se_i[:, :], 8, None, ALU.arith_shift_right))
                nc.vector.tensor_tensor(some[:, :], T.bounds[:, 1:2], T.bounds[:, 0:1], ALU.is_gt)
                link(nc.vector.tensor_copy(sh_f[:, :], sh_i[:, :]))
                link(nc.vector.tensor_tensor(span[:, :], sh_f[:, 2:3], sh_f[:, 0:1], ALU.subtract))
                link(nc.vector.tensor_tensor(span[:, :], span[:, :], some[:, :], ALU.mult))
                link(nc.vector.tensor_tensor(delta[:, :], sh_f[:, 1:2], sh_f[:, 0:1], ALU.subtract))
                link(nc.vector.tensor_tensor(delta[:, :], delta[:, :], span[:, :], ALU.subtract))
                link(nc.vector.tensor_copy(delta_w[:, :], delta[:, 0:1].broadcast_to([TILES, P])))
                nc.vector.sem_inc(S["d_dv1"], 1)
                dve.wait_ge(S["d_iota"], 4)
                nc.vector.tensor_copy(step_f[:, :], step_i[:, :])
                link(nc.vector.tensor_copy(pidx[:, :], pidx_i[:, :]))
                dve.wait_ge(S["d_pe"], 1)
                link(nc.vector.tensor_copy(cum[:, :], small[0:TILES, 4:5]))
                nc.vector.tensor_scalar(past[:, :], step_f[0:TILES, :], cum[:, 0:1], None, ALU.is_ge).then_inc(S["d_dv2"], 1)
                dve.wait_ge(S["d_pe"], 2)
                link(nc.vector.tensor_scalar(base[:, :], wide[:, 0:ALL_STEPS], float(P), None, ALU.mult))
                link(nc.vector.tensor_tensor(chunk[:, :], step_f[:, :], wide[:, 1024:1024 + ALL_STEPS], ALU.add))
                link(nc.vector.tensor_scalar(chunk[:, :], chunk[:, :], 0.0, float(MACRO - 1), ALU.max, ALU.min))
                link(nc.vector.tensor_scalar(tile_f[:, :], wide[0:1, 0:ALL_STEPS], float(TILES - 1), None, ALU.min))
                nc.vector.tensor_copy(T.tile_of[:, :], tile_f[:, :])
                nc.vector.tensor_scalar(row_of[:, :, 0], chunk[:, :], 2.0, None, ALU.mult)
                link(nc.vector.tensor_scalar(row_of[:, :, 1], chunk[:, :], 2.0, 1.0, ALU.mult, ALU.add))
                rows = row_of[:, :, :].rearrange("p s h -> p (s h)")
                for g in range(GROUPS):
                    nc.vector.tensor_scalar(pick[:, g, :], rows, float(g * P), pidx[:, 0:1], ALU.subtract,
                                            ALU.is_equal).then_inc(S["d_pick"], 1)
                dstw = T.dst_w[:, :].rearrange("p (t x c) -> p t x c", x=2, c=CHUNKS)
                dve.wait_ge(S["d_tab"], 1)
                link(nc.vector.tensor_copy(row_of[:, :, :].rearrange("p s h -> p (s h)"), big[:, 0:COLS]))
                nc.vector.sem_inc(S["d_tfree"], 1)
                for h in range(2):
                    link(nc.vector.tensor_tensor(row_of[:, :, h], row_of[:, :, h], base[:, :], ALU.subtract))
                nc.vector.tensor_copy(dstw[:, :, 0, :], rows.rearrange("p (t c) -> p t c", c=CHUNKS))
                dve.wait_ge(S["d_tab"], 2)
                link(nc.vector.tensor_copy(T.src_t[:, :], big[:, 0:COLS]))
                nc.vector.sem_inc(S["d_tfree"], 1)
                dve.wait_ge(S["d_tab"], 3)
                nc.vector.tensor_copy(dstw[:, :, 1, :], big[:, 0:COLS].rearrange("p (t c) -> p t c", c=CHUNKS))

            @block.tensor
            def _(pe):
                pe.wait_ge(S["d_iota"], 4)
                pe.wait_ge(S["d_dv1"], 1)
                nc.tensor.matmul(small[0:TILES, 4:5], upper[:, :], span[:, :], start=True, stop=True).then_inc(S["d_pe"], 1)
                pe.wait_ge(S["d_dv2"], 1)
                for lhs, off in ((ones[0:TILES, :], 0), (delta_w[:, :], 1024)):
                    for lo in range(0, ALL_STEPS, 512):
                        hi = min(lo + 512, ALL_STEPS)
                        last = nc.tensor.matmul(wide[:, off + lo:off + hi], lhs, past[:, lo:hi], start=True, stop=True)
                last.then_inc(S["d_pe"], 1)
                pe.wait_ge(S["d_load"], 32)
                pe.wait_ge(S["d_pick"], GROUPS)
                for a in range(3):
                    if a:
                        pe.wait_ge(S["d_tfree"], a)
                    for lo in range(0, COLS, 512):
                        hi = min(lo + 512, COLS)
                        for g in range(GROUPS):
                            r = P if g < FULL else REST
                            last = nc.tensor.matmul(big[:, lo:hi], raw[0:r, g, :, a], pick[0:r, g, lo:hi],
                                                    start=(g == 0), stop=(g == GROUPS - 1))
                    last.then_inc(S["d_tab"], 1)


def norm_tiles(nc, dve, rows, stat, mv, n_done, sem, passed):
    for a in range(BLK):
        nc.vector.bn_stats(stat[:, a, :], rows(a)).then_inc(sem, 1)
    wait_apart(dve, passed, sem, n_done + BLK)
    for a in range(BLK):
        nc.vector.bn_aggr(mv[:, a, :], stat[:, a, :]).then_inc(sem, 1)
    dve.wait_ge(sem, n_done + 2 * BLK)


def keys_stage(nc, A, T, S):
    ctx = ExitStack()
    sb = lambda name, shape, dt=F32: ctx.enter_context(nc.sbuf_tensor(name, shape, dt))
    pb = lambda name, shape: ctx.enter_context(nc.psum_tensor(name, shape, F32))
    with ctx:
        w_k = sb("w_k", [P, K, D])
        w_v = sb("w_v", [P, K, D])
        w_g = sb("w_g", [P, K, D])
        xin = sb("xin", [P, 2, BLK, D])
        xn = sb("xn", [P, BLK, D])
        xnT = sb("xnT", [P, 2, K, BLK * P])
        neg = sb("neg", [P, K, BLK * P])
        kf = sb("kf", [P, K, BLK * P])
        prob = sb("prob", [P, K, BLK * P])
        probT = sb("probT", [P, BLK, D])
        v_sb = sb("v_sb", [P, BLK, D])
        h_sb = sb("h_sb", [P, 2, BLK, D])
        stat = sb("stat", [P, BLK, 6])
        mv = sb("mv", [P, BLK, 2])
        rstd = sb("rstd", [P, BLK])
        half = sb("half", [P, BLK])
        bmax = sb("bmax", [P, K])
        top = sb("top", [P, 2, K])
        dtop = sb("dtop", [P, K])
        ntop = sb("ntop", [P, K])
        corr = sb("corr", [P, K])
        bsum = sb("bsum", [P, K])
        BATCH = ROWS // (2 * BLOCKS)
        ring_i = sb("ring_i", [P, 2, BATCH], I32)
        ring_r = sb("ring_r", [P, 2, BATCH, 3])
        mm = pb("mm", [P, 4, 512])
        tr = pb("tr", [P, 2, 512])
        cps = pb("cps", [P, 512])

        x4 = A["x"].rearrange("(b a p) d -> b p a d", a=BLK, p=P)
        h4 = A["h"].rearrange("(b a p) d -> b p a d", a=BLK, p=P)

        with nc.Block() as block:
            @block.sync
            def _(sp):
                wq = A["w_qkv"].rearrange("(k p) n -> p k n", p=P)
                sp.dma_start(xin[:, 0, :, :], x4[0, :, :, :]).then_inc(S["x_ld"][0], 16)
                sp.dma_start(w_k[:, :, :], wq[:, :, D:2 * D]).then_inc(S["kw"], 16)
                sp.dma_start(w_v[:, :, :], wq[:, :, 2 * D:3 * D]).then_inc(S["kw"], 16)
                sp.dma_start(w_g[:, :, :], A["w_gnn"].rearrange("(k p) n -> p k n", p=P)).then_inc(S["kw"], 16)
                for it in turns(sp, BLOCKS // 2):
                    for u in range(2):
                        n = it * 2 + u
                        nxt = (n + 1) % BLOCKS
                        sp.wait_ge(S["xn_done"], n * BLK)
                        sp.dma_start(xin[:, 1 - u, :, :], x4[bass.ds(nxt, 1), :, :, :].rearrange("o p a d -> p (o a) d")).then_inc(S["x_ld"][1 - u], 16)
                        sp.wait_ge(S["tr_free"], n * 8 + 4)
                        sp.dma_start(A["xT"][bass.ds(n, 1), :, :].rearrange("o p f -> p (o f)"), xnT[:, u, :, :].rearrange("p k t -> p (k t)")).then_inc(S["xt_st"][u], 16)
                for u in range(2):
                    sp.wait_ge(S["xt_st"][u], 16 * (BLOCKS // 2))

            @block.gpsimd
            def _(pool):
                def power(count):
                    pool.wait_ge(S["var"], count)
                    nc.gpsimd.tensor_tensor(rstd[:, :], mv[:, :, 1], half[:, :], ALU.pow).then_inc(S["rstd"], 1)

                nc.gpsimd.memset(half[:, :], -0.5).then_inc(S["half"], 1)
                pool.wait_ge(S["half"], 1)
                power(1)
                for it in turns(pool, BLOCKS // 2):
                    for u in range(2):
                        n = it * 2 + u
                        for h in range(2):
                            wait_apart(pool, S["pool_passed"], S["scat"][h], n * (16 * BATCH))
                            at = (n * 2 + h) * BATCH
                            nc.gpsimd.tensor_copy(ring_i[:, h, :], T.place[:, bass.ds(at, BATCH)])
                            nc.gpsimd.tensor_copy(ring_r[:, h, :, :], T.rec[:, bass.ds(at, BATCH), :]).then_inc(S["ring"], 1)
                            wait_apart(pool, S["pool_passed"], S["ring"], n * 2 + h + 1)
                            for c in range(BATCH):
                                pool.indirect_dma_start(out=A["recs"][:, :],
                                                        out_offset=bass.IndirectOffsetOnAxis(ap=ring_i[:, h, c:c + 1], axis=0),
                                                        in_=ring_r[:, h, c, :], in_offset=None).then_inc(S["scat"][h], 16)
                            if h == 0:
                                power(n + 2)
                        pool.wait_ge(S["act_free"], n * 8 + 16)
                        pool.dma_start(h4[bass.ds(n, 1), :, :, :].rearrange("o p a d -> p (o a) d"), h_sb[:, u, :, :]).then_inc(S["h_st"][u], 16)
                for u in range(2):
                    pool.wait_ge(S["h_st"][u], 16 * (BLOCKS // 2))
                    pool.wait_ge(S["scat"][u], 16 * BATCH * BLOCKS)

            @block.scalar
            def _(act):
                act.sem_inc(S["act_free"], 8)
                for it in turns(act, BLOCKS // 2):
                    for u in range(2):
                        n = it * 2 + u
                        for j in range(K):
                            act.wait_ge(S["neg_done"], n * K + j + 1)
                            nc.scalar.activation(neg[:, j, :], neg[:, j, :], ACT.Exp).then_inc(S["e_done"], 1)
                        act.wait_ge(S["top_done"], n + 1)
                        nc.scalar.activation(corr[:, :], dtop[:, :], ACT.Exp).then_inc(S["corr_done"], 1)
                        act.wait_ge(S["tr_done"], n * 8 + 4)
                        for j in range(K):
                            nc.scalar.activation(prob[:, j, :], kf[:, j, :], ACT.Exp, bias=ntop[:, j:j + 1],
                                                 accum_out=bsum[:, j:j + 1]).then_inc(S["p_done"], 1)
                        act.wait_ge(S["ctx_done"], n)
                        for a in range(BLK):
                            act.wait_ge(S["vh_done"], n * 8 + a + 1)
                            nc.scalar.copy(v_sb[:, a, :], mm[:, a, :]).then_inc(S["act_free"], 1)
                        act.wait_ge(S["h_st"][u], it * 16)
                        for a in range(BLK):
                            act.wait_ge(S["vh_done"], n * 8 + BLK + a + 1)
                            nc.scalar.copy(h_sb[:, u, a, :], mm[:, a, :]).then_inc(S["act_free"], 1)

            @block.vector
            def _(dve):
                def prep(m, slot, loads, tr0, stores):
                    dve.wait_ge(S["x_ld"][slot], loads)
                    norm_tiles(nc, dve, lambda a: xin[:, slot, a, :], stat, mv, m * 2 * BLK, S["bn"], S["dve_passed"])
                    nc.vector.tensor_scalar(mv[:, :, 1], mv[:, :, 1], EPS, None, ALU.add).then_inc(S["var"], 1)
                    dve.wait_ge(S["rstd"], m + 1)
                    if tr0 is not None:
                        dve.wait_ge(S["tr_done"], tr0 - BLK)
                    for a in range(BLK):
                        nc.vector.tensor_scalar(xn[:, a, :], xin[:, slot, a, :], mv[:, a, 0:1], rstd[:, a:a + 1],
                                                ALU.subtract, ALU.mult).then_inc(S["xn_done"], 1)
                    if stores is not None:
                        dve.wait_ge(S["xt_st"][slot], stores)
                    for k in range(K):
                        dve.wait_ge(S["tr_done"], (0 if tr0 is None else tr0) + k + 1)
                        nc.vector.tensor_copy(xnT[:, slot, k, :], tr[:, k % 2, :]).then_inc(S["tr_free"], 1)

                nc.vector.memset(top[:, :, :], 0.0).then_inc(S["k_init"], 1)
                nc.vector.memset(T.ksum[:, :], 0.0).then_inc(S["k_init"], 1)
                nc.vector.memset(T.ctx[:, :, :], 0.0).then_inc(S["k_init"], 1)
                dve.wait_ge(S["k_init"], 3)
                prep(0, 0, 16, None, None)
                for it in turns(dve, BLOCKS // 2):
                    for u in range(2):
                        n = it * 2 + u

                        def low_half(j):
                            dve.wait_ge(S["k_done"], n * K + j + 1)
                            nc.vector.tensor_scalar(neg[:, j, :], mm[:, j, :], 0.0, None, ALU.min).then_inc(S["neg_done"], 1)

                        def high_half(j):
                            dve.wait_ge(S["e_done"], n * K + j + 1)
                            nc.vector.scalar_tensor_tensor(out=kf[:, j, :], in0=mm[:, j, :], scalar=0.0, in1=neg[:, j, :],
                                                           op0=ALU.max, op1=ALU.add).then_inc(S["kf_done"], 1)
                            dve.wait_ge(S["kf_done"], n * K + j + 1)
                            nc.vector.reduce_max(bmax[:, j:j + 1], kf[:, j, :], AX.X).then_inc(S["bmax_done"], 1)

                        dve.wait_ge(S["p_done"], n * K)
                        low_half(0)
                        low_half(1)
                        high_half(0)
                        low_half(2)
                        high_half(1)
                        low_half(3)
                        high_half(2)
                        high_half(3)
                        dve.wait_ge(S["bmax_done"], n * K + K)
                        nc.vector.tensor_tensor(top[:, 1 - u, :], top[:, u, :], bmax[:, :], ALU.max).then_inc(S["tmax"], 1)
                        dve.wait_ge(S["tmax"], n + 1)
                        nc.vector.tensor_tensor(dtop[:, :], top[:, u, :], top[:, 1 - u, :], ALU.subtract)
                        nc.vector.tensor_scalar(ntop[:, :], top[:, 1 - u, :], -1.0, None, ALU.mult).then_inc(S["top_done"], 1)
                        prep(n + 1, 1 - u, (it + 1 + u) * 16, n * 8 + 4, (it + u) * 16)
                        dve.wait_ge(S["corr_done"], n + 1)
                        dve.wait_ge(S["p_done"], n * K + K)
                        dve.wait_ge(S["ks"], n * 2)
                        nc.vector.tensor_tensor(T.ksum[:, :], T.ksum[:, :], corr[:, :], ALU.mult).then_inc(S["ks"], 1)
                        dve.wait_ge(S["ks"], n * 2 + 1)
                        nc.vector.tensor_tensor(T.ksum[:, :], T.ksum[:, :], bsum[:, :], ALU.add).then_inc(S["ks"], 1)
                        dve.wait_ge(S["ctx_done"], n)
                        for a in range(BLK):
                            dve.wait_ge(S["tr_done"], n * 8 + 8 + a + 1)
                            nc.vector.tensor_copy(probT[:, a, :], tr[:, a % 2, :]).then_inc(S["tr_free"], 1)
                        dve.wait_ge(S["ctx_done"], n + 1)
                        for j in range(K):
                            ins = nc.vector.scalar_tensor_tensor(out=T.ctx[:, j, :], in0=T.ctx[:, j, :], scalar=corr[:, j:j + 1],
                                                                 in1=cps[:, j * P:(j + 1) * P], op0=ALU.mult, op1=ALU.add)
                        ins.then_inc(S["ctx_free"], 1)
                        dve.wait_ge(S["ctx_free"], n + 1)

            @block.tensor
            def _(pe):
                def transposes(m, q0):
                    pe.wait_ge(S["xn_done"], m * BLK + BLK)
                    for k in range(K):
                        if q0 is not None:
                            pe.wait_ge(S["tr_free"], q0 + k - 1)
                        elif k >= 2:
                            pe.wait_ge(S["tr_free"], k - 1)
                        for a in range(BLK):
                            ins = nc.tensor.transpose(tr[:, k % 2, a * P:(a + 1) * P], xn[:, a, k * P:(k + 1) * P], T.ident[:, :])
                        ins.then_inc(S["tr_done"], 1)

                transposes(0, None)
                pe.wait_ge(S["kw"], 48)
                for it in turns(pe, BLOCKS // 2):
                    for u in range(2):
                        n = it * 2 + u
                        pe.wait_ge(S["tr_free"], n * 8 + 4)
                        for j in range(K):
                            pe.wait_ge(S["act_free"], n * 8 + 4 + j + 1)
                            for k in range(K):
                                ins = nc.tensor.matmul(mm[:, j, :], w_k[:, k, j * P:(j + 1) * P], xnT[:, u, k, :],
                                                       start=(k == 0), stop=(k == K - 1))
                            ins.then_inc(S["k_done"], 1)
                        for a in range(BLK):
                            pe.wait_ge(S["kf_done"], n * K + a + 1)
                            for k in range(K):
                                ins = nc.tensor.matmul(mm[:, a, :], xnT[:, u, k, a * P:(a + 1) * P], w_v[:, k, :],
                                                       start=(k == 0), stop=(k == K - 1))
                            ins.then_inc(S["vh_done"], 1)
                        transposes(n + 1, n * 8 + 4)
                        for a in range(BLK):
                            pe.wait_ge(S["act_free"], n * 8 + 8 + a + 1)
                            for k in range(K):
                                ins = nc.tensor.matmul(mm[:, a, :], xnT[:, u, k, a * P:(a + 1) * P], w_g[:, k, :],
                                                       start=(k == 0), stop=(k == K - 1))
                            ins.then_inc(S["vh_done"], 1)
                        pe.wait_ge(S["p_done"], n * K + K)
                        for a in range(BLK):
                            pe.wait_ge(S["tr_free"], n * 8 + 8 + a - 1)
                            for j in range(K):
                                ins = nc.tensor.transpose(tr[:, a % 2, j * P:(j + 1) * P], prob[:, j, a * P:(a + 1) * P], T.ident[:, :])
                            ins.then_inc(S["tr_done"], 1)
                        pe.wait_ge(S["tr_free"], n * 8 + 12)
                        pe.wait_ge(S["ctx_free"], n)
                        for j in range(K):
                            for a in range(BLK):
                                ins = nc.tensor.matmul(cps[:, j * P:(j + 1) * P], probT[:, a, j * P:(j + 1) * P],
                                                       v_sb[:, a, j * P:(j + 1) * P], start=(a == 0), stop=(a == BLK - 1))
                        ins.then_inc(S["ctx_done"], 1)


def context_stage(nc, A, T, S):
    ctx = ExitStack()
    sb = lambda name, shape, dt=F32: ctx.enter_context(nc.sbuf_tensor(name, shape, dt))
    with ctx:
        w_p = sb("w_p", [P, K, D])
        inv = sb("inv", [P, K])
        ctxT = sb("ctxT", [P, K, P])
        t_ps = ctx.enter_context(nc.psum_tensor("t_ps", [P, 512], F32))
        m_ps = ctx.enter_context(nc.psum_tensor("m_ps", [P, K, 512], F32))
        with nc.Block() as block:
            @block.sync
            def _(sp):
                sp.dma_start(w_p[:, :, :], A["w_proj"].rearrange("(k p) n -> p k n", p=P)).then_inc(S["c_load"], 16)
                sp.dma_start(T.w_q[:, :, :], A["w_qkv"].rearrange("(k p) n -> p k n", p=P)[:, :, 0:D]).then_inc(S["c_load"], 16)

            @block.vector
            def _(dve):
                nc.vector.memset(ctxT[:, :, :], 0.0).then_inc(S["c_dve"], 1)
                nc.vector.reciprocal(inv[:, :], T.ksum[:, :]).then_inc(S["c_dve"], 1)
                dve.wait_ge(S["c_dve"], 2)
                for j in range(K):
                    nc.vector.tensor_scalar(T.ctx[:, j, :], T.ctx[:, j, :], inv[:, j:j + 1], None, ALU.mult).then_inc(S["c_dve"], 1)
                dve.wait_ge(S["c_tr"], 1)
                for j in range(K):
                    for h in range(2):
                        s = slice(h * HD, (h + 1) * HD)
                        nc.vector.tensor_copy(ctxT[s, j, s], t_ps[s, j * P + h * HD:j * P + (h + 1) * HD]).then_inc(S["c_dve"], 1)
                for j in range(K):
                    dve.wait_ge(S["c_mm"], j + 1)
                    nc.vector.tensor_copy(T.mix[:, j, :], m_ps[:, j, :]).then_inc(S["c_dve"], 1)

            @block.tensor
            def _(pe):
                pe.wait_ge(S["c_dve"], 2 + K)
                for j in range(K):
                    ins = nc.tensor.transpose(t_ps[:, j * P:(j + 1) * P], T.ctx[:, j, :], T.ident[:, :])
                ins.then_inc(S["c_tr"], 1)
                pe.wait_ge(S["c_load"], 32)
                pe.wait_ge(S["c_dve"], 2 + 3 * K)
                for j in range(K):
                    nc.tensor.matmul(m_ps[:, j, :], ctxT[:, j, :], w_p[:, j, :], start=True, stop=True).then_inc(S["c_mm"], 1)


def nodes_stage(nc, A, T, S):
    ctx = ExitStack()
    sb = lambda name, shape, dt=F32: ctx.enter_context(nc.sbuf_tensor(name, shape, dt))
    pb = lambda name, shape: ctx.enter_context(nc.psum_tensor(name, shape, F32))
    with ctx:
        xT = sb("xT_sb", [P, 2, K, P])
        qs = sb("qs", [P, D])
        qn = sb("qn", [P, D])
        qT = sb("qT", [P, K, P])
        bias = sb("bias", [P, D])
        red = sb("red", [P, 3, HEADS])
        idx = sb("idx", [P, 2, CHUNKS], I32)
        dw = sb("dw", [P, 2, 2 * CHUNKS])
        rows = sb("rows", [P, GATHERS, D])
        onehot = sb("onehot", [P, MRING, P])
        sums = pb("sums", [P, ARING, 512])
        q_ps = pb("q_ps", [P, 512])
        t_ps = pb("qt_ps", [P, 512])
        o_ps = pb("o_ps", [P, 512])
        y = T.y
        xt = A["xT"].rearrange("b p (k a t) -> b a p k t", k=K, a=BLK)

        def chunk_places(c, u):
            return c % GATHERS, c // GATHERS + 1

        with nc.Block() as block:
            @block.sync
            def _(sp):
                sp.dma_start(bias[:, :], A["b_proj"].rearrange("(o d) -> o d", o=1).broadcast_to([P, D])).then_inc(S["n_bias"], 16)
                x3 = A["x"].rearrange("(t p) d -> p t d", p=P)
                for c in range(8):
                    w = TILES // 8
                    sp.dma_start(y[:, c * w:(c + 1) * w, :], x3[:, c * w:(c + 1) * w, :]).then_inc(S["n_x"], 16)
                def load_xt(blk, a):
                    sp.dma_start(xT[:, a % 2, :, :], xt[blk, a, :, :, :].rearrange("o p k t -> p (o k) t")).then_inc(S["n_xt"][a % 2], 16)

                load_xt(slice(0, 1), 0)
                for it in turns(sp, TILES // BLK):
                    for a in range(BLK):
                        sp.wait_ge(S["q_done"], it * BLK + a)
                        if a + 1 < BLK:
                            load_xt(bass.ds(it, 1), a + 1)
                        else:
                            load_xt(bass.ds((it + 1) % BLOCKS, 1), 0)
                sp.wait_ge(S["n_xt"][0], 16 * (TILES // 2 + 1))

            @block.gpsimd
            def _(pool):
                for it in turns(pool, TILES // 2):
                    for u in range(2):
                        n = it * 2 + u
                        nc.gpsimd.tensor_copy(idx[:, u, :], T.src_t[:, bass.ds(n * CHUNKS, CHUNKS)]).then_inc(S["n_idx"], 1)
                        wait_apart(pool, S["pool_passed"], S["n_idx"], n + 1)
                        for c in range(CHUNKS):
                            slot = c % GATHERS
                            if c % 2 == 0:
                                wait_apart(pool, S["pool_passed"], S["agg_done"], n * STEPS + c // 2)
                            pool.indirect_dma_start(out=rows[:, slot, :], out_offset=None, in_=A["h"][:, :],
                                                    in_offset=bass.IndirectOffsetOnAxis(ap=idx[:, u, c:c + 1], axis=0)
                                                    ).then_inc(S["gath"][slot], 16)

            @block.scalar
            def _(act):
                for n in turns(act, TILES):
                    act.wait_ge(S["q_sub"], n + 1)
                    nc.scalar.activation(qs[:, :], qs[:, :], ACT.Exp).then_inc(S["q_exp"], 1)
                    act.wait_ge(S["qt_done"], n + 1)
                    nc.scalar.copy(qT[:, :, :].rearrange("p k t -> p (k t)"), t_ps[:, :]).then_inc(S["qt_sb"], 1)

            @block.vector
            def _(dve):
                dve.wait_ge(S["n_bias"], 16)
                for it in turns(dve, TILES // 2):
                    for u in range(2):
                        n = it * 2 + u
                        per = STEPS + 3

                        def build(s):
                            dve.wait_ge(S["agg_done"], n * STEPS + s + 1)
                            for h in range(2):
                                c = 2 * s + h
                                slot = 2 * ((STEPS * u + s) % ARING) + h
                                ins = nc.vector.tensor_scalar(onehot[:, slot, :], T.iota_f[:, :], dw[:, u, c:c + 1],
                                                              dw[:, u, CHUNKS + c:CHUNKS + c + 1], ALU.is_equal, ALU.mult)
                            ins.then_inc(S["hot"], 1)

                        def add(s):
                            t = dve.value_load(T.tile_of[0:1, bass.ds(n * STEPS + s, 1)], min_val=0, max_val=TILES - 1)
                            dve.wait_ge(S["agg_done"], n * STEPS + s + 5)
                            dve.wait_ge(S["n_y"], n * (STEPS + 1) + s + (1 if s > 5 else 0))
                            nc.vector.tensor_tensor(y[:, t, :], y[:, t, :], sums[:, (STEPS * u + s) % ARING, :],
                                                    ALU.add).then_inc(S["n_y"], 1)

                        nc.vector.tensor_copy(dw[:, u, :], T.dst_w[:, bass.ds(n * 2 * CHUNKS, 2 * CHUNKS)]).then_inc(S["n_dw"], 1)
                        dve.wait_ge(S["n_dw"], n + 1)
                        for s in range(3):
                            build(s)
                        q3 = q_ps[:, :].rearrange("p (h d) -> p h d", h=HEADS)
                        s3 = qs[:, :].rearrange("p (h d) -> p h d", h=HEADS)
                        dve.wait_ge(S["q_done"], n + 1)
                        nc.vector.reduce_max(red[:, 0, :], q3, AX.X).then_inc(S["q_red"], 1)
                        dve.wait_ge(S["q_red"], n * 3 + 1)
                        nc.vector.tensor_tensor(s3, q3, red[:, 0, :].unsqueeze(2).broadcast_to([P, HEADS, HD]),
                                                ALU.subtract).then_inc(S["q_sub"], 1)
                        build(3)
                        if u == 0:
                            dve.wait_ge(S["n_x"], 16 * 8)
                        add(0)
                        dve.wait_ge(S["q_exp"], n + 1)
                        nc.vector.reduce_sum(red[:, 1, :], s3, AX.X).then_inc(S["q_red"], 1)
                        dve.wait_ge(S["q_red"], n * 3 + 2)
                        nc.vector.reciprocal(red[:, 2, :], red[:, 1, :]).then_inc(S["q_red"], 1)
                        dve.wait_ge(S["q_red"], n * 3 + 3)
                        dve.wait_ge(S["qt_done"], n)
                        nc.vector.tensor_tensor(qn[:, :].rearrange("p (h d) -> p h d", h=HEADS), s3,
                                                red[:, 2, :].unsqueeze(2).broadcast_to([P, HEADS, HD]), ALU.mult).then_inc(S["qn_done"], 1)
                        for s in range(1, 6):
                            add(s)
                            build(s + 3)
                        dve.wait_ge(S["o_done"], n + 1)
                        nc.vector.tensor_tensor(qs[:, :], bias[:, :], o_ps[:, :], ALU.add).then_inc(S["o_sb"], 1)
                        dve.wait_ge(S["o_sb"], n + 1)
                        dve.wait_ge(S["n_y"], n * (STEPS + 1) + 6)
                        yn = y[:, bass.ds(n, 1), :].rearrange("p o d -> p (o d)")
                        nc.vector.tensor_tensor(yn, yn, qs[:, :], ALU.add).then_inc(S["n_y"], 1)
                        add(6)
                        build(9)
                        for s in range(7, STEPS):
                            add(s)

            @block.tensor
            def _(pe):
                pe.sem_inc(S["agg_done"], 4)

                def step(n, u, s):
                    bank = (STEPS * u + s) % ARING
                    pe.wait_ge(S["hot"], n * STEPS + s + 1)
                    if s >= 4:
                        pe.wait_ge(S["n_y"], n * (STEPS + 1) + (s - 3) + (1 if s - 4 > 5 else 0))
                    for h in range(2):
                        c = 2 * s + h
                        slot, use = chunk_places(c, u)
                        pe.wait_ge(S["gath"][slot], n * 32 + 16 * use)
                        ins = nc.tensor.matmul(sums[:, bank, :], onehot[:, 2 * bank + h, :], rows[:, slot, :],
                                               start=(h == 0), stop=(h == 1))
                    ins.then_inc(S["agg_done"], 1)

                for it in turns(pe, TILES // 2):
                    for u in range(2):
                        n = it * 2 + u
                        pe.wait_ge(S["n_xt"][u], it * 16 + 16)
                        for k in range(K):
                            ins = nc.tensor.matmul(q_ps[:, :], xT[:, u, k, :], T.w_q[:, k, :], start=(k == 0), stop=(k == K - 1))
                        ins.then_inc(S["q_done"], 1)
                        for s in range(4):
                            if s == 0:
                                pe.wait_ge(S["n_y"], n * (STEPS + 1))
                            step(n, u, s)
                        pe.wait_ge(S["qn_done"], n + 1)
                        pe.wait_ge(S["qt_sb"], n)
                        for k in range(K):
                            ins = nc.tensor.transpose(t_ps[:, k * P:(k + 1) * P], qn[:, k * P:(k + 1) * P], T.ident[:, :])
                        ins.then_inc(S["qt_done"], 1)
                        step(n, u, 4)
                        step(n, u, 5)
                        pe.wait_ge(S["qt_sb"], n + 1)
                        for k in range(K):
                            ins = nc.tensor.matmul(o_ps[:, :], qT[:, k, :], T.mix[:, k, :], start=(k == 0), stop=(k == K - 1))
                        ins.then_inc(S["o_done"], 1)
                        for s in range(6, STEPS):
                            step(n, u, s)


def experts_stage(nc, A, T, S):
    ctx = ExitStack()
    sb = lambda name, shape, dt=F32: ctx.enter_context(nc.sbuf_tensor(name, shape, dt))
    pb = lambda name, shape: ctx.enter_context(nc.psum_tensor(name, shape, F32))
    with ctx:
        yn = sb("yn", [P, 2, D])
        tT = sb("tT", [P, 2, K, BLK * P])
        hT = sb("hT", [P, 2, FC, BLK * P])
        w1 = T.w_q[:, :, :].rearrange("p k d -> p (k d)").rearrange("p (s k f) -> p s k f", s=2, k=K)
        w2 = T.mix[:, :, :].rearrange("p k d -> p (k d)").rearrange("p (s c d) -> p s c d", s=2, c=FC)
        b1 = sb("b1", [P, EXPERTS, FC])
        b2 = sb("b2", [EXPERTS, D])
        gw = sb("gw", [P, K, ROUTED])
        gb = sb("gb", [P, ROUTED])
        cw = sb("cw", [P, 2, BLK, EXPERTS])
        cwT = sb("cwT", [EXPERTS, 2, BLK * P])
        stat = sb("stat2", [P, BLK, 6])
        mv = sb("mv2", [P, BLK, 2])
        rstd = sb("rstd2", [P, BLK])
        half = sb("half2", [P, BLK])
        logit = sb("logit", [P, BLK, ROUTED])
        pr = sb("pr", [P, BLK, ROUTED])
        mx = sb("mx", [P, BLK])
        ssum = sb("ssum", [P, BLK])
        best = sb("best", [P, BLK, 8])
        where = sb("where", [P, BLK, 8], U32)
        where_f = sb("where_f", [P, BLK, 8])
        one = sb("one", [P, 2, BLK, ROUTED])
        up = pb("up", [P, 2, 512])
        down = pb("down", [P, 3, 512])
        tr = pb("tr2", [P, 2, 512])
        gp = pb("gp", [P, 512])
        y = T.y
        out3 = A["out"].rearrange("(t p) d -> p t d", p=P)
        LINKS = 10
        UPS = EXPERTS * FC
        GROUPS_D = (1 + ROUTED) * BLK

        with nc.Block() as block:
            @block.sync
            def _(sp):
                sp.dma_start(b1[:, :, :], A["b1"][:, :, :]).then_inc(S["x_par"], 16)
                sp.dma_start(b2[0:ROUTED, :], A["rb2"][:, :]).then_inc(S["x_par"], 16)
                sp.dma_start(b2[ROUTED:EXPERTS, :], A["sb2"][:, :]).then_inc(S["x_par"], 16)
                sp.dma_start(gw[:, :, :], A["gate_wT"].rearrange("(k p) e -> p k e", p=P)).then_inc(S["x_par"], 16)
                sp.dma_start(gb[:, :], A["gate_b"].rearrange("(o d) -> o d", o=1).broadcast_to([P, ROUTED])).then_inc(S["x_par"], 16)
                for it in turns(sp, BLOCKS // 2):
                    for u in range(2):
                        n = it * 2 + u
                        for e in range(EXPERTS):
                            s = e % 2
                            sp.wait_ge(S["x_used"], n * EXPERTS + e)
                            sp.dma_start(w1[:, s, :, :], A["w1"][e, :, :, :]).then_inc(S["x_w"][s], 16)
                            sp.dma_start(w2[:, s, :, :], A["w2"][e, :, :, :]).then_inc(S["x_w"][s], 16)
                        sp.wait_ge(S["y_done"], n * GROUPS_D + GROUPS_D)
                        sp.dma_start(out3[:, bass.ds(n * BLK, BLK), :], y[:, bass.ds(n * BLK, BLK), :]).then_inc(S["x_out"], 16)
                sp.wait_ge(S["x_out"], 16 * BLOCKS)

            @block.gpsimd
            def _(pool):
                nc.gpsimd.memset(half[:, :], -0.5).then_inc(S["half2"], 1)
                pool.wait_ge(S["half2"], 1)
                with pool.Fori(0, BLOCKS + 1) as n:
                    pool.wait_ge(S["var2"], n + 1)
                    nc.gpsimd.tensor_tensor(rstd[:, :], mv[:, :, 1], half[:, :], ALU.pow).then_inc(S["rstd2"], 1)

            @block.scalar
            def _(act):
                def router(m):
                    act.wait_ge(S["nm"], m + 1)
                    nc.scalar.activation(pr[:, :, :], logit[:, :, :], ACT.Exp).then_inc(S["pr"], 1)

                router(0)
                act.wait_ge(S["x_par"], 80)
                for it in turns(act, BLOCKS // 2):
                    for u in range(2):
                        n = it * 2 + u
                        for e in range(EXPERTS):
                            act.wait_ge(S["x_used"], n * EXPERTS + e)
                            for c in range(FC):
                                act.wait_ge(S["up_done"], n * UPS + e * FC + c + 1)
                                nc.scalar.activation(hT[:, e % 2, c, :], up[:, c, :], ACT.Gelu,
                                                     bias=b1[:, e, c:c + 1]).then_inc(S["hT"], 1)
                            if e == 5:
                                router(n + 1)

            @block.vector
            def _(dve):
                def prep(m, slot, blk, first):
                    norm_tiles(nc, dve, lambda a: y[:, bass.ds(blk * BLK + a, 1), :].rearrange("p o d -> p (o d)"),
                               stat, mv, m * 2 * BLK, S["bn2"], S["dve_passed"])
                    nc.vector.tensor_scalar(mv[:, :, 1], mv[:, :, 1], EPS, None, ALU.add).then_inc(S["var2"], 1)
                    dve.wait_ge(S["rstd2"], m + 1)
                    for a in range(BLK):
                        if not (first and a < 2):
                            dve.wait_ge(S["tr2_done"], m * BLK + a - 1)
                        nc.vector.tensor_scalar(yn[:, a % 2, :], y[:, bass.ds(blk * BLK + a, 1), :].rearrange("p o d -> p (o d)"),
                                                mv[:, a, 0:1], rstd[:, a:a + 1], ALU.subtract, ALU.mult).then_inc(S["yn"], 1)
                        dve.wait_ge(S["tr2_done"], m * BLK + a + 1)
                        nc.vector.tensor_copy(tT[:, slot, :, a * P:(a + 1) * P],
                                              tr[:, a % 2, :].rearrange("p (k t) -> p k t", k=K)).then_inc(S["tT"], 1)
                    route(m, slot)

                def route(m, slot):
                    count = [0]

                    def link(ins):
                        count[0] += 1
                        ins.then_inc(S["r_dve"], 1)
                        wait_apart(dve, S["dve_passed"], S["r_dve"], m * LINKS + count[0])

                    def wide(t):
                        return t.broadcast_to([P, BLK, ROUTED])

                    dve.wait_ge(S["logit"], m + 1)
                    link(nc.vector.tensor_tensor(logit[:, :, :], gp[:, 0:BLK * ROUTED].rearrange("p (a e) -> p a e", e=ROUTED),
                                                 wide(gb[:, :].unsqueeze(1)), ALU.add))
                    link(nc.vector.reduce_max(mx[:, :], logit[:, :, :], AX.X))
                    nc.vector.tensor_tensor(logit[:, :, :], logit[:, :, :], wide(mx[:, :].unsqueeze(2)), ALU.subtract).then_inc(S["nm"], 1)
                    dve.wait_ge(S["pr"], m + 1)
                    link(nc.vector.reduce_sum(mx[:, :], pr[:, :, :], AX.X))
                    link(nc.vector.reciprocal(ssum[:, :], mx[:, :]))
                    link(nc.vector.tensor_tensor(pr[:, :, :], pr[:, :, :], wide(ssum[:, :].unsqueeze(2)), ALU.mult))
                    for a in range(BLK):
                        ins = nc.vector.max(best[:, a, :], pr[:, a, :])
                    link(ins)
                    for a in range(BLK):
                        ins = nc.vector.max_index(where[:, a, :], best[:, a, :], pr[:, a, :])
                    link(ins)
                    link(nc.vector.tensor_copy(where_f[:, :, :], where[:, :, :]))
                    for i in range(2):
                        ins = nc.vector.tensor_tensor(one[:, i, :, :], wide(T.iota_f[:, 0:ROUTED].unsqueeze(1)),
                                                      wide(where_f[:, :, i:i + 1]), ALU.is_equal)
                    link(ins)
                    for i in range(2):
                        ins = nc.vector.tensor_tensor(one[:, i, :, :], one[:, i, :, :], wide(best[:, :, i:i + 1]), ALU.mult)
                    link(ins)
                    nc.vector.tensor_tensor(cw[:, slot, :, 0:ROUTED], one[:, 0, :, :], one[:, 1, :, :], ALU.add).then_inc(S["cw"], 1)
                    assert count[0] == LINKS

                def turned_weights(m, slot):
                    dve.wait_ge(S["cwT_done"], m + 1)
                    nc.vector.tensor_copy(cwT[:, slot, :], gp[0:EXPERTS, :]).then_inc(S["cwT"], 1)

                nc.vector.memset(cw[:, :, :, :], 1.0).then_inc(S["cw_init"], 1)
                dve.wait_ge(S["cw_init"], 1)
                dve.wait_ge(S["x_par"], 80)
                prep(0, 0, 0, True)
                turned_weights(0, 0)
                for it in turns(dve, BLOCKS // 2):
                    for u in range(2):
                        n = it * 2 + u
                        g = 0
                        for e in range(1, EXPERTS):
                            for a in range(BLK):
                                dve.wait_ge(S["down_done"], n * GROUPS_D + g + 1)
                                dve.wait_ge(S["y_done"], n * GROUPS_D + max(g - BLK + 1, 0))
                                yt = y[:, bass.ds(n * BLK + a, 1), :].rearrange("p o d -> p (o d)")
                                bank = down[:, g % 3, :]
                                if e < SHARED:
                                    nc.vector.tensor_tensor(yt, yt, bank, ALU.add).then_inc(S["y_done"], 1)
                                else:
                                    nc.vector.scalar_tensor_tensor(out=yt, in0=bank, scalar=cw[:, u, a, e - SHARED:e - SHARED + 1],
                                                                   in1=yt, op0=ALU.mult, op1=ALU.add).then_inc(S["y_done"], 1)
                                g += 1
                            if e == 4:
                                prep(n + 1, 1 - u, (n + 1) % BLOCKS, False)
                        turned_weights(n + 1, 1 - u)

            @block.tensor
            def _(pe):
                def prep(m, slot, first):
                    for a in range(BLK):
                        pe.wait_ge(S["yn"], m * BLK + a + 1)
                        if not (first and a < 2):
                            pe.wait_ge(S["tT"], m * BLK + a - 1)
                        for k in range(K):
                            ins = nc.tensor.transpose(tr[:, a % 2, k * P:(k + 1) * P], yn[:, a % 2, k * P:(k + 1) * P], T.ident[:, :])
                        ins.then_inc(S["tr2_done"], 1)
                    pe.wait_ge(S["tT"], m * BLK + BLK)
                    pe.wait_ge(S["cwT"], m)
                    for a in range(BLK):
                        for k in range(K):
                            ins = nc.tensor.matmul(gp[:, a * ROUTED:(a + 1) * ROUTED], tT[:, slot, k, a * P:(a + 1) * P], gw[:, k, :],
                                                   start=(k == 0), stop=(k == K - 1))
                    ins.then_inc(S["logit"], 1)

                def turn_weights(m, slot):
                    pe.wait_ge(S["cw"], m + 1)
                    for a in range(BLK):
                        ins = nc.tensor.transpose(gp[0:EXPERTS, a * P:(a + 1) * P], cw[:, slot, a, :], T.ident[:, :])
                    ins.then_inc(S["cwT_done"], 1)

                pe.wait_ge(S["x_par"], 80)
                prep(0, 0, True)
                turn_weights(0, 0)
                pe.sem_inc(S["x_used"], 1)
                for it in turns(pe, BLOCKS // 2):
                    for u in range(2):
                        n = it * 2 + u

                        def ups(e):
                            pe.wait_ge(S["x_w"][e % 2], n * (16 * EXPERTS) + 32 * (e // 2 + 1))
                            for c in range(FC):
                                if e == 0:
                                    pe.wait_ge(S["hT"], n * UPS)
                                else:
                                    pe.wait_ge(S["hT"], n * UPS + (e - 1) * FC + c + 1)
                                for k in range(K):
                                    ins = nc.tensor.matmul(up[:, c, :], w1[:, e % 2, k, c * P:(c + 1) * P], tT[:, u, k, :],
                                                           start=(k == 0), stop=(k == K - 1))
                                ins.then_inc(S["up_done"], 1)

                        def bank_wait(g):
                            if g >= 3:
                                pe.wait_ge(S["y_done"], n * GROUPS_D + g - 2)
                            else:
                                pe.wait_ge(S["y_done"], n * GROUPS_D)

                        ups(0)
                        ups(1)
                        pe.wait_ge(S["hT"], n * UPS + 2 * FC)
                        for a in range(BLK):
                            bank_wait(a)
                            for e in range(SHARED):
                                for c in range(FC):
                                    nc.tensor.matmul(down[:, a % 3, :], hT[:, e, c, a * P:(a + 1) * P], w2[:, e, c, :],
                                                     start=(e == 0 and c == 0), stop=False)
                            pe.wait_ge(S["cwT"], n + 1)
                            ins = nc.tensor.matmul(down[:, a % 3, :], cwT[:, u, a * P:(a + 1) * P], b2[:, :], start=False, stop=True)
                            ins.then_inc(S["down_done"], 1)
                        for e in range(SHARED, EXPERTS):
                            if e == SHARED:
                                pe.wait_ge(S["down_done"], n * GROUPS_D + BLK)
                                pe.sem_inc(S["x_used"], 2)
                            ups(e)
                            if e == 5:
                                prep(n + 1, 1 - u, False)
                            pe.wait_ge(S["hT"], n * UPS + (e + 1) * FC)
                            for a in range(BLK):
                                g = (e - 1) * BLK + a
                                bank_wait(g)
                                for c in range(FC):
                                    ins = nc.tensor.matmul(down[:, g % 3, :], hT[:, e % 2, c, a * P:(a + 1) * P], w2[:, e % 2, c, :],
                                                           start=(c == 0), stop=(c == FC - 1))
                                ins.then_inc(S["down_done"], 1)
                            pe.wait_ge(S["down_done"], n * GROUPS_D + e * BLK)
                            pe.sem_inc(S["x_used"], 1)
                        turn_weights(n + 1, 1 - u)


class Kept:
    pass


def gps_layer(nc, A):
    ctx = ExitStack()
    T, S = Kept(), {}
    with ctx:
        for name in ("dve_passed pool_passed pe_passed e_load e_iota e_set e_dve "
                     "kw xn_done tr_free tr_done var rstd half act_free neg_done e_done top_done corr_done p_done "
                     "ctx_done ctx_free vh_done k_done kf_done bmax_done tmax ks bn k_init "
                     "c_load c_dve c_tr c_mm "
                     "n_bias n_x n_idx n_dw n_y hot agg_done q_done q_red q_sub q_exp qn_done qt_done qt_sb o_done o_sb "
                     "r_cnt r_cld r_part r_ast r_rank r_cps r_raw r_tr r_trfree r_hot r_tot r_start r_carry r_bound r_bfree r_rps r_place d_load d_iota d_set d_dve d_dv1 d_dv2 d_pe d_pick d_tab d_tfree ring "
                     "x_par x_used x_out half2 var2 rstd2 bn2 nm pr up_done hT tr2_done yn tT r_dve logit cw cw_init "
                     "cwT cwT_done down_done y_done").split():
            S[name] = ctx.enter_context(nc.semaphore(name))
        for name, n in (("x_ld", 2), ("r_cst", 2), ("r_ald", 2), ("scat", 2), ("xt_st", 2), ("h_st", 2), ("n_xt", 2), ("gath", GATHERS), ("x_w", 2)):
            S[name] = [ctx.enter_context(nc.semaphore(f"{name}{i}")) for i in range(n)]
        sb = lambda name, shape, dt=F32: ctx.enter_context(nc.sbuf_tensor(name, shape, dt))
        T.ident = sb("ident", [P, P])
        T.iota_i = sb("iota_i", [P, P], I32)
        T.iota_f = sb("iota_f", [P, P])
        T.bounds = sb("bounds", [TILES, 2])
        T.ctx = sb("ctx", [P, K, P])
        T.ksum = sb("ksum", [P, K])
        with nc.sbuf_tensor("rec", [P, ROWS, 3], F32) as T.rec, nc.sbuf_tensor("place_i", [P, ROWS], I32) as T.place:
            ranks_stage(nc, A, T, S)
            keys_stage(nc, A, T, S)
        T.src_t = sb("src_t", [P, COLS], I32)
        T.dst_w = sb("dst_w", [P, 2 * COLS])
        T.tile_of = sb("tile_of", [1, ALL_STEPS], I32)
        T.w_q = sb("w_q", [P, K, D])
        T.mix = sb("mix", [P, K, D])
        edges_stage(nc, A, T, S)
        context_stage(nc, A, T, S)
        T.y = sb("y", [P, TILES, D])
        nodes_stage(nc, A, T, S)
        experts_stage(nc, A, T, S)


def kernel(**inputs):
    import concourse.bacc as _bacc
    import numpy as _np
    from concourse import mybir as _mybir
    from concourse.bass_utils import run_bass_kernel_spmd as _run

    g = {k: _np.asarray(v) for k, v in inputs.items()}
    w1 = _np.concatenate([g["L0_ffn_sw1"], g["L0_ffn_rw1"]])
    w2 = _np.concatenate([g["L0_ffn_sw2"], g["L0_ffn_rw2"]])
    b1 = _np.concatenate([g["L0_ffn_sb1"], g["L0_ffn_rb1"]])
    arrays = {
        "x": g["x"], "src": g["src"], "dst": g["dst"], "edge_weight": g["edge_weight"],
        "w_gnn": g["L0_gnn_weight"].T,
        "w_qkv": g["L0_mix_w_qkv"], "w_proj": g["L0_mix_w_proj"], "b_proj": g["L0_mix_b_proj"],
        "gate_wT": g["L0_ffn_gate_w"].T, "gate_b": g["L0_ffn_gate_b"],
        "w1": w1.transpose(0, 2, 1).reshape(EXPERTS, K, P, FF).transpose(0, 2, 1, 3),
        "w2": w2.transpose(0, 2, 1).reshape(EXPERTS, FC, P, D).transpose(0, 2, 1, 3),
        "b1": b1.reshape(EXPERTS, FC, P).transpose(2, 0, 1),
        "rb2": g["L0_ffn_rb2"], "sb2": g["L0_ffn_sb2"],
    }
    arrays = {k: _np.ascontiguousarray(v) for k, v in arrays.items()}
    nc = _bacc.Bacc("TRN2", target_bir_lowering=False, num_devices=1)
    A = {k: nc.dram_tensor(f"in_{k}", a.shape, _mybir.dt.from_np(a.dtype), kind="ExternalInput").ap() for k, a in arrays.items()}
    A["xT"] = nc.dram_tensor("xT_dram", (BLOCKS, P, K * BLK * P), F32).ap()
    A["h"] = nc.dram_tensor("h_dram", (N, D), F32).ap()
    A["cnt"] = nc.dram_tensor("cnt_dram", (ROWS // 32, 32 * TILES), F16).ap()
    A["aux"] = nc.dram_tensor("aux_dram", (2, ROWS // 32, 32 * TILES), F16).ap()
    A["recs"] = nc.dram_tensor("recs_dram", (E, 3), F32).ap()
    A["out"] = nc.dram_tensor("out_0", (N, D), F32, kind="ExternalOutput").ap()
    gps_layer(nc, A)
    r = _run(nc, [{f"in_{k}": a for k, a in arrays.items()}], core_ids=[0])
    return r.results[0]["out_0"]
```

```python
from contextlib import ExitStack

import concourse.bass as bass
import numpy as np
from concourse import mybir

F32 = mybir.dt.float32
I32 = mybir.dt.int32
U32 = mybir.dt.uint32
F16 = mybir.dt.float16
ALU = mybir.AluOpType
ACT = mybir.ActivationFunctionType
AX = mybir.AxisListType

P = 128
N, D = 8192, 512
E = 139264
K = D // P
TILES = N // P
BLK = 4
BLOCKS = TILES // BLK
ROWS = E // P
FULL = ROWS // P
REST = ROWS - FULL * P
GROUPS = FULL + (REST > 0)
MACRO = ROWS // 2
STEPS = 10
ALL_STEPS = STEPS * TILES
assert ALL_STEPS >= MACRO + TILES - 1
CHUNKS = 2 * STEPS
COLS = CHUNKS * TILES
HEADS, HD = 8, 64
SHARED, ROUTED, FF = 2, 8, 256
EXPERTS = SHARED + ROUTED
FC = FF // P
SLOT_TILES = 2 * TILES + ROUTED
EPS = 1e-5
GATHERS = 10
MRING = 8
ARING = 4


def wait_apart(eng, passed, sem, value):
    eng.wait_ge(sem, value)
    eng.sem_inc(passed, 1)


def turns(eng, count):
    yield 0
    with eng.Fori(1, count) as it:
        yield it


def turns_and_last(eng, count):
    yield 0, False
    with eng.Fori(1, count - 1) as it:
        yield it, False
    yield count - 1, True


def ranks_stage(nc, A, T, S):
    ctx = ExitStack()
    sb = lambda name, shape, dt=F32: ctx.enter_context(nc.sbuf_tensor(name, shape, dt))
    pb = lambda name, shape: ctx.enter_context(nc.psum_tensor(name, shape, F32))
    UNIT = 32
    UNITS = ROWS // UNIT
    UW = UNIT * TILES
    assert UW == 4 * 512 and UNITS % 2 == 0
    with ctx:
        raw_i = sb("raw_i", [P, 2, GROUPS, P], I32)
        raw = sb("raw", [P, 3, GROUPS, P])
        src_i = sb("src_i", [P, ROWS], I32)
        tile_c = sb("tile_c", [P, ROWS])
        hot = sb("hot_tiles", [P, ROWS, TILES], F16)
        ones = sb("ones_r", [P, P], F16)
        onesf = sb("onesf_r", [1, 1])
        before = sb("before", [P, P], F16)
        weigh = sb("weigh", [2, P], F16)
        cnt = sb("cnt", [P, GROUPS, TILES], F16)
        total = sb("total", [P, TILES])
        upto = sb("upto", [P, TILES])
        start = sb("start", [P, TILES])
        zeros = sb("zeros_r", [P, TILES])
        carry = sb("carry", [P, TILES])
        carry_i = sb("carry_i", [P, GROUPS, TILES], I32)
        part_i = sb("part_i", [P, 2, GROUPS, TILES], I32)
        part = sb("part", [P, 2, GROUPS, TILES], F16)
        aux = sb("aux", [2, 2, UW], F16)
        cnt_row = aux[0:1, :, :]
        flat = raw[:, :, :, :].rearrange("p a g c -> p (a g c)")
        prod = flat[:, 0:UW]
        place = flat[:, UW:UW + ROWS]
        ps = pb("ps_r", [P, 2, UW])

        with nc.Block() as block:
            @block.sync
            def _(sp):
                for a, name in enumerate(("src", "dst")):
                    v = A[name].rearrange("(r c) -> r c", c=P)
                    sp.dma_start(raw_i[:, a, 0:FULL, :], v[0:FULL * P, :].rearrange("(g p) c -> p g c", p=P)).then_inc(S["e_load"], 16)
                    sp.dma_start(raw_i[0:REST, a, FULL, :], v[FULL * P:ROWS, :]).then_inc(S["e_load"], 16)
                v = A["edge_weight"].rearrange("(r c) -> r c", c=P)
                sp.dma_start(raw[:, 2, 0:FULL, :], v[0:FULL * P, :].rearrange("(g p) c -> p g c", p=P)).then_inc(S["e_load"], 16)
                sp.dma_start(raw[0:REST, 2, FULL, :], v[FULL * P:ROWS, :]).then_inc(S["e_load"], 16)
                for it in turns(sp, UNITS // 2):
                    for u in range(2):
                        n = it * 2 + u
                        sp.wait_ge(S["r_cnt"], n + 3)
                        sp.dma_start(A["cnt"][bass.ds(n, 1), :], cnt_row[:, u, :]).then_inc(S["r_cst"][u], 16)
                for u in range(2):
                    sp.wait_ge(S["r_cst"][u], 16 * (UNITS // 2))
                cv = A["cnt"].rearrange("n (c t) -> (n c) t", t=TILES)
                sp.dma_start(cnt[:, 0:FULL, :], cv[0:FULL * P, :].rearrange("(g p) t -> p g t", p=P)).then_inc(S["r_cld"], 16)
                sp.dma_start(cnt[0:REST, FULL, :], cv[FULL * P:ROWS, :]).then_inc(S["r_cld"], 16)
                sp.wait_ge(S["r_part"], 1)
                for h in range(2):
                    av = A["aux"][h].rearrange("n (c t) -> (n c) t", t=TILES)
                    sp.dma_start(av[0:FULL * P, :].rearrange("(g p) t -> p g t", p=P), part[:, h, 0:FULL, :]).then_inc(S["r_ast"], 16)
                    sp.dma_start(av[FULL * P:ROWS, :], part[0:REST, h, FULL, :]).then_inc(S["r_ast"], 16)
                sp.wait_ge(S["r_ast"], 64)
                for it in turns(sp, UNITS // 2):
                    for u in range(2):
                        n = it * 2 + u
                        sp.wait_ge(S["r_rank"], n + 1)
                        sp.dma_start(aux[:, u, :], A["aux"][:, bass.ds(n, 1), :].rearrange("h o w -> h (o w)")).then_inc(S["r_ald"][u], 16)

            @block.gpsimd
            def _(pool):
                nc.gpsimd.iota(T.iota_i[:, :], pattern=[[1, P]], base=0, channel_multiplier=0).then_inc(S["consts"], 1)
                nc.gpsimd.memset(ones[:, :], 1.0).then_inc(S["consts"], 1)
                nc.gpsimd.memset(onesf[:, :], 1.0).then_inc(S["consts"], 1)
                nc.gpsimd.memset(zeros[:, :], 0.0).then_inc(S["consts"], 1)
                nc.gpsimd.memset(before[:, :], 1.0).then_inc(S["blank"], 1)
                nc.gpsimd.memset(T.ident[:, :], 0.0).then_inc(S["blank"], 1)
                nc.gpsimd.memset(weigh[:, :], 256.0).then_inc(S["blank"], 1)
                pool.wait_ge(S["blank"], 3)
                nc.gpsimd.affine_select(out=before[:, :], in_=before[:, :], compare_op=ALU.is_gt, fill=0.0, base=0,
                                        pattern=[[1, P]], channel_multiplier=-1).then_inc(S["consts"], 1)
                nc.gpsimd.affine_select(out=T.ident[:, :], in_=T.ident[:, :], compare_op=ALU.not_equal, fill=1.0, base=0,
                                        pattern=[[-1, P]], channel_multiplier=1).then_inc(S["consts"], 1)
                nc.gpsimd.affine_select(out=weigh[:, :], in_=weigh[:, :], compare_op=ALU.not_equal, fill=1.0, base=-1,
                                        pattern=[[0, P]], channel_multiplier=1).then_inc(S["consts"], 1)

            @block.scalar
            def _(act):
                for it in turns(act, UNITS // 2):
                    for u in range(2):
                        n = it * 2 + u
                        act.wait_ge(S["r_cps"], n + 1)
                        act.wait_ge(S["r_cst"][u], it * 16)
                        nc.scalar.copy(cnt_row[:, u, :], ps[0:1, u, :]).then_inc(S["r_cnt"], 1)

            @block.vector
            def _(dve):
                def link(ins):
                    T.linked += 1
                    ins.then_inc(S["linked"], 1)
                    dve.wait_ge(S["linked"], T.linked)

                dve.wait_ge(S["consts"], 7)
                nc.vector.tensor_copy(T.iota_f[:, :], T.iota_i[:, :])
                dve.wait_ge(S["e_load"], 16 * 6)
                for a in range(2):
                    nc.vector.tensor_copy(raw[:, a, 0:FULL, :], raw_i[:, a, 0:FULL, :])
                    link(nc.vector.tensor_copy(raw[0:REST, a, FULL, :], raw_i[0:REST, a, FULL, :]))
                nc.vector.sem_inc(S["r_raw"], 1)
                for a in range(3):
                    dve.wait_ge(S["r_tr"], a + 1)
                    link(nc.vector.tensor_copy(T.rec[:, :, a], ps[:, a % 2, 0:ROWS]))
                    nc.vector.sem_inc(S["r_trfree"], 1)
                link(nc.vector.tensor_copy(src_i[:, :], T.rec[:, :, 0]))
                link(nc.vector.tensor_scalar(src_i[:, :], src_i[:, :], 7, None, ALU.arith_shift_right))
                link(nc.vector.tensor_copy(tile_c[:, :], src_i[:, :]))
                with dve.Fori(0, UNITS) as n:
                    nc.vector.tensor_tensor(hot[:, bass.ds(n * UNIT, UNIT), :],
                                            tile_c[:, bass.ds(n * UNIT, UNIT)].unsqueeze(2).broadcast_to([P, UNIT, TILES]),
                                            T.iota_f[:, 0:TILES].unsqueeze(1).broadcast_to([P, UNIT, TILES]),
                                            ALU.is_equal).then_inc(S["r_hot"], 1)
                dve.wait_ge(S["r_tot"], 1)
                link(nc.vector.tensor_copy(total[:, :], ps[:, 0, 0:TILES]))
                link(nc.vector.tensor_tensor_scan(upto[:, :], total[:, :], zeros[:, :], 0.0, ALU.add, ALU.add))
                link(nc.vector.tensor_tensor(start[:, :], upto[:, :], total[:, :], ALU.subtract))
                nc.vector.sem_inc(S["r_start"], 1)
                dve.wait_ge(S["r_carry"], GROUPS)
                for g in range(GROUPS):
                    r = P if g < FULL else REST
                    link(nc.vector.tensor_tensor(carry[0:r, :], start[0:r, :], ps[0:r, 1, g * TILES:(g + 1) * TILES], ALU.add))
                    link(nc.vector.tensor_copy(carry_i[0:r, g, :], carry[0:r, :]))
                    link(nc.vector.tensor_scalar(part_i[0:r, 0, g, :], carry_i[0:r, g, :], 8, None, ALU.arith_shift_right))
                    link(nc.vector.tensor_scalar(part_i[0:r, 1, g, :], carry_i[0:r, g, :], 255, None, ALU.bitwise_and))
                    link(nc.vector.tensor_copy(part[0:r, :, g, :], part_i[0:r, :, g, :]))
                nc.vector.sem_inc(S["r_part"], 1)
                dve.wait_ge(S["r_bound"], 1)
                link(nc.vector.tensor_copy(T.bounds[:, :], ps[0:TILES, 0, 512:514]))
                nc.vector.sem_inc(S["r_bfree"], 1)
                for it in turns(dve, UNITS // 2):
                    for u in range(2):
                        n = it * 2 + u
                        dve.wait_ge(S["r_rps"], n + 1)
                        dve.wait_ge(S["r_place"], n)
                        nc.vector.tensor_tensor(prod[:, :], ps[:, u, :], hot[:, bass.ds(n * UNIT, UNIT), :].rearrange("p c t -> p (c t)"),
                                                ALU.mult).then_inc(S["r_rank"], 1)
                        dve.wait_ge(S["r_rank"], n + 3)
                        nc.vector.reduce_sum(place[:, bass.ds(n * UNIT, UNIT)], prod[:, :].rearrange("p (c t) -> p c t", t=TILES),
                                             AX.X).then_inc(S["r_place"], 1)
                dve.wait_ge(S["r_place"], UNITS)
                nc.vector.tensor_copy(T.place[:, :], place[:, :])

            @block.tensor
            def _(pe):
                pe.sem_inc(S["r_rank"], 2)
                pe.sem_inc(S["r_cnt"], 2)
                pe.wait_ge(S["consts"], 7)
                pe.wait_ge(S["r_raw"], 1)
                for a in range(3):
                    if a == 2:
                        pe.wait_ge(S["r_trfree"], 1)
                    for g in range(GROUPS):
                        r = P if g < FULL else REST
                        ins = nc.tensor.transpose(ps[:, a % 2, g * P:g * P + r], raw[0:r, a, g, :], T.ident[0:r, 0:r])
                    ins.then_inc(S["r_tr"], 1)
                pe.wait_ge(S["r_trfree"], 3)
                for it in turns(pe, UNITS // 2):
                    for u in range(2):
                        n = it * 2 + u
                        pe.wait_ge(S["r_hot"], n + 1)
                        pe.wait_ge(S["r_cnt"], n + 1)
                        for c in range(4):
                            ins = nc.tensor.matmul(ps[:, u, c * 512:(c + 1) * 512], ones[:, :],
                                                   hot[:, bass.ds(n * UNIT + c * 8, 8), :].rearrange("p c t -> p (c t)"),
                                                   start=True, stop=True)
                        ins.then_inc(S["r_cps"], 1)
                pe.wait_ge(S["r_cld"], 32)
                pe.wait_ge(S["r_cnt"], UNITS + 2)
                for g in range(GROUPS):
                    r = P if g < FULL else REST
                    ins = nc.tensor.matmul(ps[:, 0, 0:TILES], ones[0:r, :], cnt[0:r, g, :], start=(g == 0), stop=(g == GROUPS - 1))
                ins.then_inc(S["r_tot"], 1)
                for g in range(GROUPS):
                    r = P if g < FULL else REST
                    ins = nc.tensor.matmul(ps[0:r, 1, g * TILES:(g + 1) * TILES], before[0:r, 0:r], cnt[0:r, g, :],
                                           start=True, stop=(g == 0))
                    for e in range(g):
                        ins = nc.tensor.matmul(ps[0:r, 1, g * TILES:(g + 1) * TILES], ones[:, 0:r], cnt[:, e, :],
                                               start=False, stop=(e == g - 1))
                    ins.then_inc(S["r_carry"], 1)
                pe.wait_ge(S["r_start"], 1)
                nc.tensor.matmul(ps[0:TILES, 0, 512:513], start[0:1, :], onesf[:, :], start=True, stop=True)
                nc.tensor.matmul(ps[0:TILES, 0, 513:514], upto[0:1, :], onesf[:, :], start=True, stop=True).then_inc(S["r_bound"], 1)
                pe.wait_ge(S["r_bfree"], 1)
                for it in turns(pe, UNITS // 2):
                    for u in range(2):
                        n = it * 2 + u
                        pe.wait_ge(S["r_ald"][u], it * 16 + 16)
                        pe.wait_ge(S["r_rank"], n + 1)
                        for c in range(4):
                            w = slice(c * 512, (c + 1) * 512)
                            nc.tensor.matmul(ps[:, u, w], before[:, :], hot[:, bass.ds(n * UNIT + c * 8, 8), :].rearrange("p c t -> p (c t)"),
                                             start=True, stop=False)
                            ins = nc.tensor.matmul(ps[:, u, w], weigh[:, :], aux[:, u, w], start=False, stop=True)
                        ins.then_inc(S["r_rps"], 1)


def edges_stage(nc, A, T, S):
    ctx = ExitStack()
    sb = lambda name, shape, dt=F32: ctx.enter_context(nc.sbuf_tensor(name, shape, dt))
    pb = lambda name, shape: ctx.enter_context(nc.psum_tensor(name, shape, F32))
    with ctx:
        raw = sb("sorted", [P, GROUPS, P, 3])
        step_i = sb("step_i", [P, ALL_STEPS], I32)
        step_f = sb("step_f", [P, ALL_STEPS])
        ones = sb("ones_e", [P, P])
        upper = sb("upper", [TILES, TILES])
        se_i = sb("se_i", [TILES, 3], I32)
        sh_i = sb("sh_i", [TILES, 3], I32)
        sh_f = sb("sh_f", [TILES, 3])
        some = sb("some", [TILES, 1])
        span = sb("span", [TILES, 1])
        past = sb("past", [TILES, ALL_STEPS])
        delta = sb("delta", [TILES, 1])
        delta_w = sb("delta_w", [TILES, P])
        cum = sb("cum", [TILES, 1])
        row_of = sb("row_of", [P, ALL_STEPS, 2])
        chunk = sb("chunk", [P, ALL_STEPS])
        pidx_i = sb("pidx_i", [P, 1], I32)
        pidx = sb("pidx", [P, 1])
        pick = sb("pick", [P, GROUPS, COLS])
        base = sb("base", [P, ALL_STEPS])
        tile_f = sb("tile_f", [1, ALL_STEPS])
        big = pb("big", [P, 3 * 512])
        wide = pb("wide", [P, 4 * 512])
        small = pb("small", [P, 512])

        with nc.Block() as block:
            @block.sync
            def _(sp):
                v = A["recs"].rearrange("(r c) w -> r c w", c=P)
                sp.dma_start(raw[:, 0:FULL, :, :], v[0:FULL * P, :, :].rearrange("(g p) c w -> p g c w", p=P)).then_inc(S["d_load"], 16)
                sp.dma_start(raw[0:REST, FULL, :, :], v[FULL * P:ROWS, :, :]).then_inc(S["d_load"], 16)

            @block.gpsimd
            def _(pool):
                nc.gpsimd.iota(step_i[:, :], pattern=[[1, ALL_STEPS]], base=0, channel_multiplier=0).then_inc(S["consts"], 1)
                nc.gpsimd.iota(pidx_i[:, :], pattern=[[1, 1]], base=0, channel_multiplier=1).then_inc(S["consts"], 1)
                nc.gpsimd.memset(ones[:, :], 1.0).then_inc(S["consts"], 1)
                nc.gpsimd.memset(upper[:, :], 1.0).then_inc(S["blank"], 1)
                pool.wait_ge(S["blank"], 4)
                nc.gpsimd.affine_select(out=upper[:, :], in_=upper[:, :], compare_op=ALU.is_ge, fill=0.0, base=0,
                                        pattern=[[1, TILES]], channel_multiplier=-1).then_inc(S["consts"], 1)

            @block.vector
            def _(dve):
                def link(ins):
                    T.linked += 1
                    ins.then_inc(S["linked"], 1)
                    dve.wait_ge(S["linked"], T.linked)

                nc.vector.tensor_copy(se_i[:, 0:2], T.bounds[:, :])
                link(nc.vector.tensor_scalar(se_i[:, 2:3], T.bounds[:, 1:2], 255.0, None, ALU.add))
                link(nc.vector.tensor_scalar(sh_i[:, :], se_i[:, :], 8, None, ALU.arith_shift_right))
                nc.vector.tensor_tensor(some[:, :], T.bounds[:, 1:2], T.bounds[:, 0:1], ALU.is_gt)
                link(nc.vector.tensor_copy(sh_f[:, :], sh_i[:, :]))
                link(nc.vector.tensor_tensor(span[:, :], sh_f[:, 2:3], sh_f[:, 0:1], ALU.subtract))
                link(nc.vector.tensor_tensor(span[:, :], span[:, :], some[:, :], ALU.mult))
                link(nc.vector.tensor_tensor(delta[:, :], sh_f[:, 1:2], sh_f[:, 0:1], ALU.subtract))
                link(nc.vector.tensor_tensor(delta[:, :], delta[:, :], span[:, :], ALU.subtract))
                link(nc.vector.tensor_copy(delta_w[:, :], delta[:, 0:1].broadcast_to([TILES, P])))
                nc.vector.sem_inc(S["d_dv1"], 1)
                dve.wait_ge(S["consts"], 11)
                nc.vector.tensor_copy(step_f[:, :], step_i[:, :])
                link(nc.vector.tensor_copy(pidx[:, :], pidx_i[:, :]))
                dve.wait_ge(S["d_pe"], 1)
                link(nc.vector.tensor_copy(cum[:, :], small[0:TILES, 4:5]))
                nc.vector.tensor_scalar(past[:, :], step_f[0:TILES, :], cum[:, 0:1], None, ALU.is_ge).then_inc(S["d_dv2"], 1)
                dve.wait_ge(S["d_pe"], 2)
                link(nc.vector.tensor_scalar(base[:, :], wide[:, 0:ALL_STEPS], float(P), None, ALU.mult))
                link(nc.vector.tensor_tensor(chunk[:, :], step_f[:, :], wide[:, 1024:1024 + ALL_STEPS], ALU.add))
                link(nc.vector.tensor_scalar(chunk[:, :], chunk[:, :], 0.0, float(MACRO - 1), ALU.max, ALU.min))
                link(nc.vector.tensor_scalar(tile_f[:, :], wide[0:1, 0:ALL_STEPS], float(TILES - 1), None, ALU.min))
                nc.vector.tensor_copy(T.tile_of[:, :], tile_f[:, :])
                nc.vector.tensor_scalar(row_of[:, :, 0], chunk[:, :], 2.0, None, ALU.mult)
                link(nc.vector.tensor_scalar(row_of[:, :, 1], chunk[:, :], 2.0, 1.0, ALU.mult, ALU.add))
                rows = row_of[:, :, :].rearrange("p s h -> p (s h)")
                for g in range(GROUPS):
                    nc.vector.tensor_scalar(pick[:, g, :], rows, float(g * P), pidx[:, 0:1], ALU.subtract,
                                            ALU.is_equal).then_inc(S["d_pick"], 1)
                dstw = T.dst_w[:, :].rearrange("p (t x c) -> p t x c", x=2, c=CHUNKS)
                dve.wait_ge(S["d_tab"], 1)
                link(nc.vector.tensor_copy(row_of[:, :, :].rearrange("p s h -> p (s h)"), big[:, 0:COLS]))
                nc.vector.sem_inc(S["d_tfree"], 1)
                for h in range(2):
                    link(nc.vector.tensor_tensor(row_of[:, :, h], row_of[:, :, h], base[:, :], ALU.subtract))
                nc.vector.tensor_copy(dstw[:, :, 0, :], rows.rearrange("p (t c) -> p t c", c=CHUNKS))
                dve.wait_ge(S["d_tab"], 2)
                link(nc.vector.tensor_copy(T.src_t[:, :], big[:, 0:COLS]))
                nc.vector.sem_inc(S["d_tfree"], 1)
                dve.wait_ge(S["d_tab"], 3)
                nc.vector.tensor_copy(dstw[:, :, 1, :], big[:, 0:COLS].rearrange("p (t c) -> p t c", c=CHUNKS))

            @block.tensor
            def _(pe):
                pe.wait_ge(S["consts"], 11)
                pe.wait_ge(S["d_dv1"], 1)
                nc.tensor.matmul(small[0:TILES, 4:5], upper[:, :], span[:, :], start=True, stop=True).then_inc(S["d_pe"], 1)
                pe.wait_ge(S["d_dv2"], 1)
                for lhs, off in ((ones[0:TILES, :], 0), (delta_w[:, :], 1024)):
                    for lo in range(0, ALL_STEPS, 512):
                        hi = min(lo + 512, ALL_STEPS)
                        last = nc.tensor.matmul(wide[:, off + lo:off + hi], lhs, past[:, lo:hi], start=True, stop=True)
                last.then_inc(S["d_pe"], 1)
                pe.wait_ge(S["d_load"], 32)
                pe.wait_ge(S["d_pick"], GROUPS)
                for a in range(3):
                    if a:
                        pe.wait_ge(S["d_tfree"], a)
                    for lo in range(0, COLS, 512):
                        hi = min(lo + 512, COLS)
                        for g in range(GROUPS):
                            r = P if g < FULL else REST
                            last = nc.tensor.matmul(big[:, lo:hi], raw[0:r, g, :, a], pick[0:r, g, lo:hi],
                                                    start=(g == 0), stop=(g == GROUPS - 1))
                    last.then_inc(S["d_tab"], 1)


def norm_tiles(nc, dve, rows, stat, mv, n_done, sem, passed):
    for a in range(BLK):
        nc.vector.bn_stats(stat[:, a, :], rows(a)).then_inc(sem, 1)
    wait_apart(dve, passed, sem, n_done + BLK)
    for a in range(BLK):
        nc.vector.bn_aggr(mv[:, a, :], stat[:, a, :]).then_inc(sem, 1)
    dve.wait_ge(sem, n_done + 2 * BLK)


def keys_stage(nc, A, T, S):
    ctx = ExitStack()
    sb = lambda name, shape, dt=F32: ctx.enter_context(nc.sbuf_tensor(name, shape, dt))
    pb = lambda name, shape: ctx.enter_context(nc.psum_tensor(name, shape, F32))
    with ctx:
        w_k = sb("w_k", [P, K, D])
        w_v = sb("w_v", [P, K, D])
        w_g = sb("w_g", [P, K, D])
        xin = sb("xin", [P, 2, BLK, D])
        xn = sb("xn", [P, BLK, D])
        xnT = sb("xnT", [P, 2, K, BLK * P])
        neg = sb("neg", [P, K, BLK * P])
        kf = sb("kf", [P, K, BLK * P])
        prob = sb("prob", [P, K, BLK * P])
        probT = sb("probT", [P, BLK, D])
        v_sb = sb("v_sb", [P, BLK, D])
        h_sb = sb("h_sb", [P, 2, BLK, D])
        stat = sb("stat", [P, BLK, 6])
        mv = sb("mv", [P, BLK, 2])
        rstd = sb("rstd", [P, BLK])
        half = sb("half", [P, BLK])
        bmax = sb("bmax", [P, K])
        top = sb("top", [P, 2, K])
        dtop = sb("dtop", [P, K])
        ntop = sb("ntop", [P, K])
        corr = sb("corr", [P, K])
        bsum = sb("bsum", [P, K])
        BATCH = ROWS // (2 * BLOCKS)
        ring_i = sb("ring_i", [P, 2, BATCH], I32)
        ring_r = sb("ring_r", [P, 2, BATCH, 3])
        mm = pb("mm", [P, 4, 512])
        tr = pb("tr", [P, 2, 512])
        cps = pb("cps", [P, 512])

        x4 = A["x"].rearrange("(b a p) d -> b p a d", a=BLK, p=P)
        h4 = A["h"].rearrange("(b a p) d -> b p a d", a=BLK, p=P)

        with nc.Block() as block:
            @block.sync
            def _(sp):
                wq = A["w_qkv"].rearrange("(k p) n -> p k n", p=P)
                sp.dma_start(xin[:, 0, :, :], x4[0, :, :, :]).then_inc(S["x_ld"][0], 16)
                sp.dma_start(w_k[:, :, :], wq[:, :, D:2 * D]).then_inc(S["kw"], 16)
                sp.dma_start(w_v[:, :, :], wq[:, :, 2 * D:3 * D]).then_inc(S["kw"], 16)
                sp.dma_start(w_g[:, :, :], A["w_gnn"].rearrange("(k p) n -> p k n", p=P)).then_inc(S["kw"], 16)
                for it in turns(sp, BLOCKS // 2):
                    for u in range(2):
                        n = it * 2 + u
                        nxt = (n + 1) % BLOCKS
                        sp.wait_ge(S["xn_done"], n * BLK)
                        sp.dma_start(xin[:, 1 - u, :, :], x4[bass.ds(nxt, 1), :, :, :].rearrange("o p a d -> p (o a) d")).then_inc(S["x_ld"][1 - u], 16)
                        sp.wait_ge(S["tr_free"], n * 8 + 4)
                        sp.dma_start(A["xT"][bass.ds(n, 1), :, :].rearrange("o p f -> p (o f)"), xnT[:, u, :, :].rearrange("p k t -> p (k t)")).then_inc(S["xt_st"][u], 16)
                for u in range(2):
                    sp.wait_ge(S["xt_st"][u], 16 * (BLOCKS // 2))

            @block.gpsimd
            def _(pool):
                def power(count):
                    pool.wait_ge(S["var"], count)
                    nc.gpsimd.tensor_tensor(rstd[:, :], mv[:, :, 1], half[:, :], ALU.pow).then_inc(S["rstd"], 1)

                nc.gpsimd.memset(half[:, :], -0.5).then_inc(S["half"], 1)
                pool.wait_ge(S["half"], 1)
                power(1)
                for it in turns(pool, BLOCKS // 2):
                    for u in range(2):
                        n = it * 2 + u
                        for h in range(2):
                            wait_apart(pool, S["pool_passed"], S["scat"][h], n * (16 * BATCH))
                            at = (n * 2 + h) * BATCH
                            nc.gpsimd.tensor_copy(ring_i[:, h, :], T.place[:, bass.ds(at, BATCH)])
                            nc.gpsimd.tensor_copy(ring_r[:, h, :, :], T.rec[:, bass.ds(at, BATCH), :]).then_inc(S["ring"], 1)
                            wait_apart(pool, S["pool_passed"], S["ring"], n * 2 + h + 1)
                            for c in range(BATCH):
                                pool.indirect_dma_start(out=A["recs"][:, :],
                                                        out_offset=bass.IndirectOffsetOnAxis(ap=ring_i[:, h, c:c + 1], axis=0),
                                                        in_=ring_r[:, h, c, :], in_offset=None).then_inc(S["scat"][h], 16)
                            if h == 0:
                                power(n + 2)
                        pool.wait_ge(S["act_free"], n * 8 + 16)
                        pool.dma_start(h4[bass.ds(n, 1), :, :, :].rearrange("o p a d -> p (o a) d"), h_sb[:, u, :, :]).then_inc(S["h_st"][u], 16)
                for u in range(2):
                    pool.wait_ge(S["h_st"][u], 16 * (BLOCKS // 2))
                    pool.wait_ge(S["scat"][u], 16 * BATCH * BLOCKS)

            @block.scalar
            def _(act):
                act.sem_inc(S["act_free"], 8)
                for it in turns(act, BLOCKS // 2):
                    for u in range(2):
                        n = it * 2 + u
                        for j in range(K):
                            act.wait_ge(S["neg_done"], n * K + j + 1)
                            nc.scalar.activation(neg[:, j, :], neg[:, j, :], ACT.Exp).then_inc(S["e_done"], 1)
                        act.wait_ge(S["top_done"], n + 1)
                        nc.scalar.activation(corr[:, :], dtop[:, :], ACT.Exp).then_inc(S["corr_done"], 1)
                        act.wait_ge(S["tr_done"], n * 8 + 4)
                        for j in range(K):
                            nc.scalar.activation(prob[:, j, :], kf[:, j, :], ACT.Exp, bias=ntop[:, j:j + 1],
                                                 accum_out=bsum[:, j:j + 1]).then_inc(S["p_done"], 1)
                        act.wait_ge(S["ctx_done"], n)
                        for a in range(BLK):
                            act.wait_ge(S["vh_done"], n * 8 + a + 1)
                            nc.scalar.copy(v_sb[:, a, :], mm[:, a, :]).then_inc(S["act_free"], 1)
                        act.wait_ge(S["h_st"][u], it * 16)
                        for a in range(BLK):
                            act.wait_ge(S["vh_done"], n * 8 + BLK + a + 1)
                            nc.scalar.copy(h_sb[:, u, a, :], mm[:, a, :]).then_inc(S["act_free"], 1)

            @block.vector
            def _(dve):
                def prep(m, slot, loads, tr0, stores):
                    dve.wait_ge(S["x_ld"][slot], loads)
                    norm_tiles(nc, dve, lambda a: xin[:, slot, a, :], stat, mv, m * 2 * BLK, S["bn"], S["dve_passed"])
                    nc.vector.tensor_scalar(mv[:, :, 1], mv[:, :, 1], EPS, None, ALU.add).then_inc(S["var"], 1)
                    dve.wait_ge(S["rstd"], m + 1)
                    if tr0 is not None:
                        dve.wait_ge(S["tr_done"], tr0 - BLK)
                    for a in range(BLK):
                        nc.vector.tensor_scalar(xn[:, a, :], xin[:, slot, a, :], mv[:, a, 0:1], rstd[:, a:a + 1],
                                                ALU.subtract, ALU.mult).then_inc(S["xn_done"], 1)
                    if stores is not None:
                        dve.wait_ge(S["xt_st"][slot], stores)
                    for k in range(K):
                        dve.wait_ge(S["tr_done"], (0 if tr0 is None else tr0) + k + 1)
                        nc.vector.tensor_copy(xnT[:, slot, k, :], tr[:, k % 2, :]).then_inc(S["tr_free"], 1)

                nc.vector.memset(top[:, :, :], 0.0).then_inc(S["k_init"], 1)
                nc.vector.memset(T.ksum[:, :], 0.0).then_inc(S["k_init"], 1)
                nc.vector.memset(T.ctx[:, :, :], 0.0).then_inc(S["k_init"], 1)
                dve.wait_ge(S["k_init"], 3)
                prep(0, 0, 16, None, None)
                for it in turns(dve, BLOCKS // 2):
                    for u in range(2):
                        n = it * 2 + u

                        def low_half(j):
                            dve.wait_ge(S["k_done"], n * K + j + 1)
                            nc.vector.tensor_scalar(neg[:, j, :], mm[:, j, :], 0.0, None, ALU.min).then_inc(S["neg_done"], 1)

                        def high_half(j):
                            dve.wait_ge(S["e_done"], n * K + j + 1)
                            nc.vector.scalar_tensor_tensor(out=kf[:, j, :], in0=mm[:, j, :], scalar=0.0, in1=neg[:, j, :],
                                                           op0=ALU.max, op1=ALU.add).then_inc(S["kf_done"], 1)
                            dve.wait_ge(S["kf_done"], n * K + j + 1)
                            nc.vector.reduce_max(bmax[:, j:j + 1], kf[:, j, :], AX.X).then_inc(S["bmax_done"], 1)

                        dve.wait_ge(S["p_done"], n * K)
                        low_half(0)
                        low_half(1)
                        high_half(0)
                        low_half(2)
                        high_half(1)
                        low_half(3)
                        high_half(2)
                        high_half(3)
                        dve.wait_ge(S["bmax_done"], n * K + K)
                        nc.vector.tensor_tensor(top[:, 1 - u, :], top[:, u, :], bmax[:, :], ALU.max).then_inc(S["tmax"], 1)
                        dve.wait_ge(S["tmax"], n + 1)
                        nc.vector.tensor_tensor(dtop[:, :], top[:, u, :], top[:, 1 - u, :], ALU.subtract)
                        nc.vector.tensor_scalar(ntop[:, :], top[:, 1 - u, :], -1.0, None, ALU.mult).then_inc(S["top_done"], 1)
                        prep(n + 1, 1 - u, (it + 1 + u) * 16, n * 8 + 4, (it + u) * 16)
                        dve.wait_ge(S["corr_done"], n + 1)
                        dve.wait_ge(S["p_done"], n * K + K)
                        dve.wait_ge(S["ks"], n * 2)
                        nc.vector.tensor_tensor(T.ksum[:, :], T.ksum[:, :], corr[:, :], ALU.mult).then_inc(S["ks"], 1)
                        dve.wait_ge(S["ks"], n * 2 + 1)
                        nc.vector.tensor_tensor(T.ksum[:, :], T.ksum[:, :], bsum[:, :], ALU.add).then_inc(S["ks"], 1)
                        dve.wait_ge(S["ctx_done"], n)
                        for a in range(BLK):
                            dve.wait_ge(S["tr_done"], n * 8 + 8 + a + 1)
                            nc.vector.tensor_copy(probT[:, a, :], tr[:, a % 2, :]).then_inc(S["tr_free"], 1)
                        dve.wait_ge(S["ctx_done"], n + 1)
                        for j in range(K):
                            ins = nc.vector.scalar_tensor_tensor(out=T.ctx[:, j, :], in0=T.ctx[:, j, :], scalar=corr[:, j:j + 1],
                                                                 in1=cps[:, j * P:(j + 1) * P], op0=ALU.mult, op1=ALU.add)
                        ins.then_inc(S["ctx_free"], 1)
                        dve.wait_ge(S["ctx_free"], n + 1)

            @block.tensor
            def _(pe):
                def transposes(m, q0):
                    pe.wait_ge(S["xn_done"], m * BLK + BLK)
                    for k in range(K):
                        if q0 is not None:
                            pe.wait_ge(S["tr_free"], q0 + k - 1)
                        elif k >= 2:
                            pe.wait_ge(S["tr_free"], k - 1)
                        for a in range(BLK):
                            ins = nc.tensor.transpose(tr[:, k % 2, a * P:(a + 1) * P], xn[:, a, k * P:(k + 1) * P], T.ident[:, :])
                        ins.then_inc(S["tr_done"], 1)

                transposes(0, None)
                pe.wait_ge(S["kw"], 48)
                for it in turns(pe, BLOCKS // 2):
                    for u in range(2):
                        n = it * 2 + u
                        pe.wait_ge(S["tr_free"], n * 8 + 4)
                        for j in range(K):
                            pe.wait_ge(S["act_free"], n * 8 + 4 + j + 1)
                            for k in range(K):
                                ins = nc.tensor.matmul(mm[:, j, :], w_k[:, k, j * P:(j + 1) * P], xnT[:, u, k, :],
                                                       start=(k == 0), stop=(k == K - 1))
                            ins.then_inc(S["k_done"], 1)
                        for a in range(BLK):
                            pe.wait_ge(S["kf_done"], n * K + a + 1)
                            for k in range(K):
                                ins = nc.tensor.matmul(mm[:, a, :], xnT[:, u, k, a * P:(a + 1) * P], w_v[:, k, :],
                                                       start=(k == 0), stop=(k == K - 1))
                            ins.then_inc(S["vh_done"], 1)
                        transposes(n + 1, n * 8 + 4)
                        for a in range(BLK):
                            pe.wait_ge(S["act_free"], n * 8 + 8 + a + 1)
                            for k in range(K):
                                ins = nc.tensor.matmul(mm[:, a, :], xnT[:, u, k, a * P:(a + 1) * P], w_g[:, k, :],
                                                       start=(k == 0), stop=(k == K - 1))
                            ins.then_inc(S["vh_done"], 1)
                        pe.wait_ge(S["p_done"], n * K + K)
                        for a in range(BLK):
                            pe.wait_ge(S["tr_free"], n * 8 + 8 + a - 1)
                            for j in range(K):
                                ins = nc.tensor.transpose(tr[:, a % 2, j * P:(j + 1) * P], prob[:, j, a * P:(a + 1) * P], T.ident[:, :])
                            ins.then_inc(S["tr_done"], 1)
                        pe.wait_ge(S["tr_free"], n * 8 + 12)
                        pe.wait_ge(S["ctx_free"], n)
                        for j in range(K):
                            for a in range(BLK):
                                ins = nc.tensor.matmul(cps[:, j * P:(j + 1) * P], probT[:, a, j * P:(j + 1) * P],
                                                       v_sb[:, a, j * P:(j + 1) * P], start=(a == 0), stop=(a == BLK - 1))
                        ins.then_inc(S["ctx_done"], 1)


def context_stage(nc, A, T, S):
    ctx = ExitStack()
    sb = lambda name, shape, dt=F32: ctx.enter_context(nc.sbuf_tensor(name, shape, dt))
    with ctx:
        w_p = sb("w_p", [P, K, D])
        inv = sb("inv", [P, K])
        ctxT = sb("ctxT", [P, K, P])
        t_ps = ctx.enter_context(nc.psum_tensor("t_ps", [P, 512], F32))
        m_ps = ctx.enter_context(nc.psum_tensor("m_ps", [P, K, 512], F32))
        with nc.Block() as block:
            @block.sync
            def _(sp):
                sp.dma_start(w_p[:, :, :], A["w_proj"].rearrange("(k p) n -> p k n", p=P)).then_inc(S["c_load"], 16)
                sp.dma_start(T.w_q[:, :, :], A["w_qkv"].rearrange("(k p) n -> p k n", p=P)[:, :, 0:D]).then_inc(S["c_load"], 16)

            @block.vector
            def _(dve):
                nc.vector.memset(ctxT[:, :, :], 0.0).then_inc(S["c_dve"], 1)
                nc.vector.reciprocal(inv[:, :], T.ksum[:, :]).then_inc(S["c_dve"], 1)
                dve.wait_ge(S["c_dve"], 2)
                for j in range(K):
                    nc.vector.tensor_scalar(T.ctx[:, j, :], T.ctx[:, j, :], inv[:, j:j + 1], None, ALU.mult).then_inc(S["c_dve"], 1)
                dve.wait_ge(S["c_tr"], 1)
                for j in range(K):
                    for h in range(2):
                        s = slice(h * HD, (h + 1) * HD)
                        nc.vector.tensor_copy(ctxT[s, j, s], t_ps[s, j * P + h * HD:j * P + (h + 1) * HD]).then_inc(S["c_dve"], 1)
                for j in range(K):
                    dve.wait_ge(S["c_mm"], j + 1)
                    nc.vector.tensor_copy(T.mix[:, j, :], m_ps[:, j, :]).then_inc(S["c_dve"], 1)

            @block.tensor
            def _(pe):
                pe.wait_ge(S["c_dve"], 2 + K)
                for j in range(K):
                    ins = nc.tensor.transpose(t_ps[:, j * P:(j + 1) * P], T.ctx[:, j, :], T.ident[:, :])
                ins.then_inc(S["c_tr"], 1)
                pe.wait_ge(S["c_load"], 32)
                pe.wait_ge(S["c_dve"], 2 + 3 * K)
                for j in range(K):
                    nc.tensor.matmul(m_ps[:, j, :], ctxT[:, j, :], w_p[:, j, :], start=True, stop=True).then_inc(S["c_mm"], 1)


def nodes_stage(nc, A, T, S):
    ctx = ExitStack()
    sb = lambda name, shape, dt=F32: ctx.enter_context(nc.sbuf_tensor(name, shape, dt))
    pb = lambda name, shape: ctx.enter_context(nc.psum_tensor(name, shape, F32))
    with ctx:
        xT = sb("xT_sb", [P, 2, K, P])
        qs = sb("qs", [P, D])
        qn = sb("qn", [P, D])
        qT = sb("qT", [P, K, P])
        bias = sb("bias", [P, D])
        red = sb("red", [P, 3, HEADS])
        idx = sb("idx", [P, 2, CHUNKS], I32)
        dw = sb("dw", [P, 2, 2 * CHUNKS])
        rows = sb("rows", [P, GATHERS, D])
        onehot = sb("onehot", [P, MRING, P])
        sums = pb("sums", [P, ARING, 512])
        q_ps = pb("q_ps", [P, 512])
        t_ps = pb("qt_ps", [P, 512])
        o_ps = pb("o_ps", [P, 512])
        y = T.y
        xt = A["xT"].rearrange("b p (k a t) -> b a p k t", k=K, a=BLK)

        def chunk_places(c, u):
            return c % GATHERS, c // GATHERS + 1

        with nc.Block() as block:
            @block.sync
            def _(sp):
                sp.dma_start(bias[:, :], A["b_proj"].rearrange("(o d) -> o d", o=1).broadcast_to([P, D])).then_inc(S["n_bias"], 16)
                x3 = A["x"].rearrange("(t p) d -> p t d", p=P)
                for c in range(8):
                    w = TILES // 8
                    sp.dma_start(y[:, c * w:(c + 1) * w, :], x3[:, c * w:(c + 1) * w, :]).then_inc(S["n_x"], 16)
                def load_xt(blk, a):
                    sp.dma_start(xT[:, a % 2, :, :], xt[blk, a, :, :, :].rearrange("o p k t -> p (o k) t")).then_inc(S["n_xt"][a % 2], 16)

                load_xt(slice(0, 1), 0)
                for it in turns(sp, TILES // BLK):
                    for a in range(BLK):
                        sp.wait_ge(S["q_done"], it * BLK + a)
                        if a + 1 < BLK:
                            load_xt(bass.ds(it, 1), a + 1)
                        else:
                            load_xt(bass.ds((it + 1) % BLOCKS, 1), 0)
                sp.wait_ge(S["n_xt"][0], 16 * (TILES // 2 + 1))

            @block.gpsimd
            def _(pool):
                for it in turns(pool, TILES // 2):
                    for u in range(2):
                        n = it * 2 + u
                        nc.gpsimd.tensor_copy(idx[:, u, :], T.src_t[:, bass.ds(n * CHUNKS, CHUNKS)]).then_inc(S["n_idx"], 1)
                        wait_apart(pool, S["pool_passed"], S["n_idx"], n + 1)
                        for c in range(CHUNKS):
                            slot = c % GATHERS
                            if c % 2 == 0:
                                wait_apart(pool, S["pool_passed"], S["agg_done"], n * STEPS + c // 2)
                            pool.indirect_dma_start(out=rows[:, slot, :], out_offset=None, in_=A["h"][:, :],
                                                    in_offset=bass.IndirectOffsetOnAxis(ap=idx[:, u, c:c + 1], axis=0)
                                                    ).then_inc(S["gath"][slot], 16)

            @block.scalar
            def _(act):
                for n in turns(act, TILES):
                    act.wait_ge(S["q_sub"], n + 1)
                    nc.scalar.activation(qs[:, :], qs[:, :], ACT.Exp).then_inc(S["q_exp"], 1)
                    act.wait_ge(S["qt_done"], n + 1)
                    nc.scalar.copy(qT[:, :, :].rearrange("p k t -> p (k t)"), t_ps[:, :]).then_inc(S["qt_sb"], 1)

            @block.vector
            def _(dve):
                dve.wait_ge(S["n_bias"], 16)
                for it in turns(dve, TILES // 2):
                    for u in range(2):
                        n = it * 2 + u
                        per = STEPS + 3

                        def build(s):
                            dve.wait_ge(S["agg_done"], n * STEPS + s + 1)
                            for h in range(2):
                                c = 2 * s + h
                                slot = 2 * ((STEPS * u + s) % ARING) + h
                                ins = nc.vector.tensor_scalar(onehot[:, slot, :], T.iota_f[:, :], dw[:, u, c:c + 1],
                                                              dw[:, u, CHUNKS + c:CHUNKS + c + 1], ALU.is_equal, ALU.mult)
                            ins.then_inc(S["hot"], 1)

                        def add(s):
                            t = dve.value_load(T.tile_of[0:1, bass.ds(n * STEPS + s, 1)], min_val=0, max_val=TILES - 1)
                            dve.wait_ge(S["agg_done"], n * STEPS + s + 5)
                            dve.wait_ge(S["n_y"], n * (STEPS + 1) + s + (1 if s > 5 else 0))
                            nc.vector.tensor_tensor(y[:, t, :], y[:, t, :], sums[:, (STEPS * u + s) % ARING, :],
                                                    ALU.add).then_inc(S["n_y"], 1)

                        nc.vector.tensor_copy(dw[:, u, :], T.dst_w[:, bass.ds(n * 2 * CHUNKS, 2 * CHUNKS)]).then_inc(S["n_dw"], 1)
                        dve.wait_ge(S["n_dw"], n + 1)
                        for s in range(3):
                            build(s)
                        q3 = q_ps[:, :].rearrange("p (h d) -> p h d", h=HEADS)
                        s3 = qs[:, :].rearrange("p (h d) -> p h d", h=HEADS)
                        dve.wait_ge(S["q_done"], n + 1)
                        nc.vector.reduce_max(red[:, 0, :], q3, AX.X).then_inc(S["q_red"], 1)
                        dve.wait_ge(S["q_red"], n * 3 + 1)
                        nc.vector.tensor_tensor(s3, q3, red[:, 0, :].unsqueeze(2).broadcast_to([P, HEADS, HD]),
                                                ALU.subtract).then_inc(S["q_sub"], 1)
                        build(3)
                        if u == 0:
                            dve.wait_ge(S["n_x"], 16 * 8)
                        add(0)
                        dve.wait_ge(S["q_exp"], n + 1)
                        nc.vector.reduce_sum(red[:, 1, :], s3, AX.X).then_inc(S["q_red"], 1)
                        dve.wait_ge(S["q_red"], n * 3 + 2)
                        nc.vector.reciprocal(red[:, 2, :], red[:, 1, :]).then_inc(S["q_red"], 1)
                        dve.wait_ge(S["q_red"], n * 3 + 3)
                        dve.wait_ge(S["qt_done"], n)
                        nc.vector.tensor_tensor(qn[:, :].rearrange("p (h d) -> p h d", h=HEADS), s3,
                                                red[:, 2, :].unsqueeze(2).broadcast_to([P, HEADS, HD]), ALU.mult).then_inc(S["qn_done"], 1)
                        for s in range(1, 6):
                            add(s)
                            build(s + 3)
                        dve.wait_ge(S["o_done"], n + 1)
                        nc.vector.tensor_tensor(qs[:, :], bias[:, :], o_ps[:, :], ALU.add).then_inc(S["o_sb"], 1)
                        dve.wait_ge(S["o_sb"], n + 1)
                        dve.wait_ge(S["n_y"], n * (STEPS + 1) + 6)
                        yn = y[:, bass.ds(n, 1), :].rearrange("p o d -> p (o d)")
                        nc.vector.tensor_tensor(yn, yn, qs[:, :], ALU.add).then_inc(S["n_y"], 1)
                        add(6)
                        build(9)
                        for s in range(7, STEPS):
                            add(s)

            @block.tensor
            def _(pe):
                pe.sem_inc(S["agg_done"], 4)

                def step(n, u, s):
                    bank = (STEPS * u + s) % ARING
                    pe.wait_ge(S["hot"], n * STEPS + s + 1)
                    if s >= 4:
                        pe.wait_ge(S["n_y"], n * (STEPS + 1) + (s - 3) + (1 if s - 4 > 5 else 0))
                    for h in range(2):
                        c = 2 * s + h
                        slot, use = chunk_places(c, u)
                        pe.wait_ge(S["gath"][slot], n * 32 + 16 * use)
                        ins = nc.tensor.matmul(sums[:, bank, :], onehot[:, 2 * bank + h, :], rows[:, slot, :],
                                               start=(h == 0), stop=(h == 1))
                    ins.then_inc(S["agg_done"], 1)

                for it in turns(pe, TILES // 2):
                    for u in range(2):
                        n = it * 2 + u
                        pe.wait_ge(S["n_xt"][u], it * 16 + 16)
                        for k in range(K):
                            ins = nc.tensor.matmul(q_ps[:, :], xT[:, u, k, :], T.w_q[:, k, :], start=(k == 0), stop=(k == K - 1))
                        ins.then_inc(S["q_done"], 1)
                        for s in range(4):
                            if s == 0:
                                pe.wait_ge(S["n_y"], n * (STEPS + 1))
                            step(n, u, s)
                        pe.wait_ge(S["qn_done"], n + 1)
                        pe.wait_ge(S["qt_sb"], n)
                        for k in range(K):
                            ins = nc.tensor.transpose(t_ps[:, k * P:(k + 1) * P], qn[:, k * P:(k + 1) * P], T.ident[:, :])
                        ins.then_inc(S["qt_done"], 1)
                        step(n, u, 4)
                        step(n, u, 5)
                        pe.wait_ge(S["qt_sb"], n + 1)
                        for k in range(K):
                            ins = nc.tensor.matmul(o_ps[:, :], qT[:, k, :], T.mix[:, k, :], start=(k == 0), stop=(k == K - 1))
                        ins.then_inc(S["o_done"], 1)
                        for s in range(6, STEPS):
                            step(n, u, s)


def shared_stage(nc, A, T, S):
    ctx = ExitStack()
    sb = lambda name, shape, dt=F32: ctx.enter_context(nc.sbuf_tensor(name, shape, dt))
    pb = lambda name, shape: ctx.enter_context(nc.psum_tensor(name, shape, F32))
    with ctx:
        yn = T.dst_w[:, 0:BLK * D].rearrange("p (a d) -> p a d", a=BLK)
        w1 = T.w_q[:, :, :].rearrange("p k d -> p (k d)").rearrange("p (e k f) -> p e k f", e=SHARED, k=K)
        w2 = T.mix[:, :, :].rearrange("p k d -> p (k d)").rearrange("p (e c d) -> p e c d", e=SHARED, c=FC)
        tT = sb("tT", [P, 2, K, BLK * P])
        hT = sb("hT", [P, SHARED, FC, BLK * P])
        b1 = sb("b1", [P, SHARED, FC])
        b2 = sb("b2", [EXPERTS, D])
        gw = sb("gw", [P, K, ROUTED])
        gb = sb("gb", [P, ROUTED])
        cw = sb("cw", [P, BLK, EXPERTS])
        cwT = sb("cwT", [EXPERTS, BLK * P])
        stat = sb("stat2", [P, BLK, 6])
        mv = sb("mv2", [P, BLK, 2])
        rstd = sb("rstd2", [P, BLK])
        half = sb("half2", [P, BLK])
        logit = sb("logit", [P, BLK, ROUTED])
        pr = sb("pr", [P, BLK, ROUTED])
        mx = sb("mx", [P, BLK])
        ssum = sb("ssum", [P, BLK])
        best = sb("best", [P, BLK, 8])
        where = sb("where", [P, BLK, 8], U32)
        where_f = sb("where_f", [P, BLK, 8])
        one = sb("one", [P, 2, BLK, ROUTED])
        zero = sb("zero_ids", [P, SLOT_TILES])
        up = pb("up", [P, 2, 512])
        down = pb("down", [P, 3, 512])
        tr = pb("tr2", [P, 2, 512])
        gp = pb("gp", [P, 512])
        y = T.y
        y3 = A["y1"].rearrange("(t p) d -> p t d", p=P)
        n3 = A["yn"].rearrange("(t p) d -> p t d", p=P)
        LINKS = 10

        with nc.Block() as block:
            @block.sync
            def _(sp):
                sp.dma_start(w1[:, :, :, :], A["w1"][0:SHARED].rearrange("e p k f -> p e k f")).then_inc(S["x_par"], 16)
                sp.dma_start(w2[:, :, :, :], A["w2"][0:SHARED].rearrange("e p c d -> p e c d")).then_inc(S["x_par"], 16)
                sp.dma_start(b1[:, :, :], A["b1"][:, 0:SHARED, :]).then_inc(S["x_par"], 16)
                sp.dma_start(b2[0:ROUTED, :], A["rb2"][:, :]).then_inc(S["x_par"], 16)
                sp.dma_start(b2[ROUTED:EXPERTS, :], A["sb2"][:, :]).then_inc(S["x_par"], 16)
                sp.dma_start(gw[:, :, :], A["gate_wT"].rearrange("(k p) e -> p k e", p=P)).then_inc(S["x_par"], 16)
                sp.dma_start(gb[:, :], A["gate_b"].rearrange("(o d) -> o d", o=1).broadcast_to([P, ROUTED])).then_inc(S["x_par"], 16)
                sp.wait_ge(S["x_zero"], 1)
                sp.dma_start(A["ids"].rearrange("(p j) o -> p (j o)", p=P), zero[:, :]).then_inc(S["x_zst"], 16)

                def store_rows(m):
                    for a in range(BLK):
                        sp.wait_ge(S["yn"], m * BLK + a + 1)
                        sp.dma_start(n3[:, bass.ds(m * BLK + a, 1), :], yn[:, a:a + 1, :]).then_inc(S["yn_st"][a], 16)

                store_rows(0)
                for it, last in turns_and_last(sp, BLOCKS // 2):
                    for u in range(2):
                        n = it * 2 + u
                        if not (last and u == 1):
                            store_rows(n + 1)
                        sp.wait_ge(S["y_done"], n * BLK + BLK)
                        sp.dma_start(y3[:, bass.ds(n * BLK, BLK), :], y[:, bass.ds(n * BLK, BLK), :]).then_inc(S["x_out"], 16)
                sp.wait_ge(S["x_out"], 16 * BLOCKS)
                sp.wait_ge(S["x_zst"], 16)
                for a in range(BLK):
                    sp.wait_ge(S["yn_st"][a], 16 * BLOCKS)

            @block.gpsimd
            def _(pool):
                nc.gpsimd.memset(zero[:, :], 0.0).then_inc(S["x_zero"], 1)
                nc.gpsimd.memset(half[:, :], -0.5).then_inc(S["half2"], 1)
                pool.wait_ge(S["half2"], 1)
                with pool.Fori(0, BLOCKS) as n:
                    pool.wait_ge(S["var2"], n + 1)
                    nc.gpsimd.tensor_tensor(rstd[:, :], mv[:, :, 1], half[:, :], ALU.pow).then_inc(S["rstd2"], 1)

            @block.scalar
            def _(act):
                act.wait_ge(S["x_par"], 16 * 7)
                for n in turns(act, BLOCKS):
                    act.wait_ge(S["nm"], n + 1)
                    nc.scalar.activation(pr[:, :, :], logit[:, :, :], ACT.Exp).then_inc(S["pr"], 1)
                    act.wait_ge(S["down_done"], n * BLK)
                    for e in range(SHARED):
                        for c in range(FC):
                            act.wait_ge(S["up_done"], n * (SHARED * FC) + e * FC + c + 1)
                            nc.scalar.activation(hT[:, e, c, :], up[:, c, :], ACT.Gelu, bias=b1[:, e, c:c + 1]).then_inc(S["hT"], 1)

            @block.vector
            def _(dve):
                def tile(t):
                    return y[:, bass.ds(t, 1), :].rearrange("p o d -> p (o d)")

                def stats(m):
                    norm_tiles(nc, dve, lambda a: tile(m * BLK + a), stat, mv, m * 2 * BLK, S["bn2"], S["dve_passed"])
                    nc.vector.tensor_scalar(mv[:, :, 1], mv[:, :, 1], EPS, None, ALU.add).then_inc(S["var2"], 1)
                    dve.wait_ge(S["rstd2"], m + 1)

                def norm(m, a):
                    dve.wait_ge(S["yn_st"][a], m * 16)
                    dve.wait_ge(S["tr2_done"], m * BLK + a - 3 if not isinstance(m, int) or m else 0)
                    nc.vector.tensor_scalar(yn[:, a, :], tile(m * BLK + a), mv[:, a, 0:1], rstd[:, a:a + 1],
                                            ALU.subtract, ALU.mult).then_inc(S["yn"], 1)

                def turned(m, slot, a):
                    dve.wait_ge(S["tr2_done"], m * BLK + a + 1)
                    nc.vector.tensor_copy(tT[:, slot, :, a * P:(a + 1) * P],
                                          tr[:, a % 2, :].rearrange("p (k t) -> p k t", k=K)).then_inc(S["tT"], 1)

                def route(m):
                    count = [0]

                    def link(ins):
                        count[0] += 1
                        ins.then_inc(S["r_dve"], 1)
                        wait_apart(dve, S["dve_passed"], S["r_dve"], m * LINKS + count[0])

                    def wide(t):
                        return t.broadcast_to([P, BLK, ROUTED])

                    dve.wait_ge(S["logit"], m + 1)
                    link(nc.vector.tensor_tensor(logit[:, :, :], gp[:, 0:BLK * ROUTED].rearrange("p (a e) -> p a e", e=ROUTED),
                                                 wide(gb[:, :].unsqueeze(1)), ALU.add))
                    link(nc.vector.reduce_max(mx[:, :], logit[:, :, :], AX.X))
                    nc.vector.tensor_tensor(logit[:, :, :], logit[:, :, :], wide(mx[:, :].unsqueeze(2)), ALU.subtract).then_inc(S["nm"], 1)
                    dve.wait_ge(S["pr"], m + 1)
                    link(nc.vector.reduce_sum(mx[:, :], pr[:, :, :], AX.X))
                    link(nc.vector.reciprocal(ssum[:, :], mx[:, :]))
                    link(nc.vector.tensor_tensor(pr[:, :, :], pr[:, :, :], wide(ssum[:, :].unsqueeze(2)), ALU.mult))
                    for a in range(BLK):
                        ins = nc.vector.max(best[:, a, :], pr[:, a, :])
                    link(ins)
                    for a in range(BLK):
                        ins = nc.vector.max_index(where[:, a, :], best[:, a, :], pr[:, a, :])
                    link(ins)
                    link(nc.vector.tensor_copy(where_f[:, :, :], where[:, :, :]))
                    nc.vector.tensor_copy(T.expert[:, bass.ds(m * BLK, BLK), :], where_f[:, :, 0:2])
                    nc.vector.tensor_copy(T.prob[:, bass.ds(m * BLK, BLK), :], best[:, :, 0:2])
                    for i in range(2):
                        ins = nc.vector.tensor_tensor(one[:, i, :, :], wide(T.iota_f[:, 0:ROUTED].unsqueeze(1)),
                                                      wide(where_f[:, :, i:i + 1]), ALU.is_equal)
                    link(ins)
                    for i in range(2):
                        ins = nc.vector.tensor_tensor(one[:, i, :, :], one[:, i, :, :], wide(best[:, :, i:i + 1]), ALU.mult)
                    link(ins)
                    nc.vector.tensor_tensor(cw[:, :, 0:ROUTED], one[:, 0, :, :], one[:, 1, :, :], ALU.add).then_inc(S["cw"], 1)
                    assert count[0] == LINKS
                    dve.wait_ge(S["cwT_done"], m + 1)
                    nc.vector.tensor_copy(cwT[:, :], gp[0:EXPERTS, :]).then_inc(S["cwT"], 1)

                nc.vector.memset(cw[:, :, :], 1.0).then_inc(S["cw_init"], 1)
                dve.wait_ge(S["cw_init"], 1)
                dve.wait_ge(S["x_par"], 16 * 7)
                stats(0)
                for a in range(BLK):
                    norm(0, a)
                    turned(0, 0, a)
                for it, last in turns_and_last(dve, BLOCKS // 2):
                    for u in range(2):
                        n = it * 2 + u
                        more = not (last and u == 1)
                        route(n)
                        if more:
                            stats(n + 1)
                            norm(n + 1, 0)
                            norm(n + 1, 1)
                        for a in range(BLK):
                            if more:
                                turned(n + 1, 1 - u, a)
                                if a + 2 < BLK:
                                    norm(n + 1, a + 2)
                            dve.wait_ge(S["down_done"], n * BLK + a + 1)
                            nc.vector.tensor_tensor(tile(n * BLK + a), tile(n * BLK + a), down[:, a % 2, :], ALU.add).then_inc(S["y_done"], 1)

            @block.tensor
            def _(pe):
                def turn(m, a):
                    pe.wait_ge(S["yn"], m * BLK + a + 1)
                    if not (isinstance(m, int) and m == 0 and a < 2):
                        pe.wait_ge(S["tT"], m * BLK + a - 1)
                    for k in range(K):
                        ins = nc.tensor.transpose(tr[:, a % 2, k * P:(k + 1) * P], yn[:, a, k * P:(k + 1) * P], T.ident[:, :])
                    ins.then_inc(S["tr2_done"], 1)

                def logits(m, slot):
                    pe.wait_ge(S["tT"], m * BLK + BLK)
                    pe.wait_ge(S["cwT"], m)
                    for a in range(BLK):
                        for k in range(K):
                            ins = nc.tensor.matmul(gp[:, a * ROUTED:(a + 1) * ROUTED], tT[:, slot, k, a * P:(a + 1) * P], gw[:, k, :],
                                                   start=(k == 0), stop=(k == K - 1))
                    ins.then_inc(S["logit"], 1)

                pe.wait_ge(S["x_par"], 16 * 7)
                for a in range(BLK):
                    turn(0, a)
                logits(0, 0)
                for it, last in turns_and_last(pe, BLOCKS // 2):
                    for u in range(2):
                        n = it * 2 + u
                        more = not (last and u == 1)
                        for e in range(SHARED):
                            for c in range(FC):
                                pe.wait_ge(S["hT"], n * (SHARED * FC) + max(e * FC + c - 1, 0))
                                for k in range(K):
                                    ins = nc.tensor.matmul(up[:, c, :], w1[:, e, k, c * P:(c + 1) * P], tT[:, u, k, :],
                                                           start=(k == 0), stop=(k == K - 1))
                                ins.then_inc(S["up_done"], 1)
                        pe.wait_ge(S["cw"], n + 1)
                        for a in range(BLK):
                            ins = nc.tensor.transpose(gp[0:EXPERTS, a * P:(a + 1) * P], cw[:, a, :], T.ident[:, :])
                        ins.then_inc(S["cwT_done"], 1)
                        for a in range(BLK):
                            if more:
                                turn(n + 1, a)
                            if a == 0:
                                pe.wait_ge(S["hT"], n * (SHARED * FC) + SHARED * FC)
                                pe.wait_ge(S["cwT"], n + 1)
                            pe.wait_ge(S["y_done"], n * BLK + max(a - 1, 0))
                            for e in range(SHARED):
                                for c in range(FC):
                                    nc.tensor.matmul(down[:, a % 2, :], hT[:, e, c, a * P:(a + 1) * P], w2[:, e, c, :],
                                                     start=(e == 0 and c == 0), stop=False)
                            nc.tensor.matmul(down[:, a % 2, :], cwT[:, a * P:(a + 1) * P], b2[:, :], start=False,
                                             stop=True).then_inc(S["down_done"], 1)
                        if more:
                            logits(n + 1, 1 - u)


def places_stage(nc, A, T, S):
    ctx = ExitStack()
    sb = lambda name, shape, dt=F32: ctx.enter_context(nc.sbuf_tensor(name, shape, dt))
    pb = lambda name, shape: ctx.enter_context(nc.psum_tensor(name, shape, F32))
    C = 2 * TILES
    SENT = 16 * ROWS // 2
    SENDS = 16
    with ctx:
        hot = sb("hot_e", [P, C, ROUTED], F16)
        ones = sb("ones_p", [P, P], F16)
        before = sb("before_p", [P, P], F16)
        col = sb("col", [P, C, ROUTED])
        upto = sb("upto_p", [P, ROUTED, C])
        zeros = sb("zeros_p", [P, C])
        tiles_i = sb("tiles_i", [P, ROUTED], I32)
        tiles = sb("tiles", [P, ROUTED])
        cum = sb("cum_p", [P, ROUTED])
        base = sb("base_p", [P, ROUTED])
        rank = sb("rank", [P, C, ROUTED])
        place = sb("place_f", [P, C])
        node_i = sb("node_i", [P, C], I32)
        node = sb("node", [P, C])
        slot_i = sb("slot_i", [P, SLOT_TILES], I32)
        slot = sb("slot", [P, SLOT_TILES])
        eof = sb("eof", [1, SLOT_TILES])
        ring_i = sb("ring_p", [P, 2, SENDS], I32)
        ring_n = sb("ring_n", [P, 2, SENDS, 1])
        back = sb("back", [P, 2, P])
        ps = pb("ps_p", [P, 2, 2, 512])
        tp = pb("tp", [P, 512])

        with nc.Block() as block:
            @block.gpsimd
            def _(pool):
                nc.gpsimd.memset(ones[:, :], 1.0).then_inc(S["consts"], 1)
                nc.gpsimd.memset(zeros[:, :], 0.0).then_inc(S["consts"], 1)
                nc.gpsimd.memset(before[:, :], 1.0).then_inc(S["blank"], 1)
                nc.gpsimd.iota(node_i[:, :], pattern=[[P, TILES], [0, 2]], base=0, channel_multiplier=1).then_inc(S["consts"], 1)
                nc.gpsimd.iota(slot_i[:, :], pattern=[[1, SLOT_TILES]], base=0, channel_multiplier=0).then_inc(S["consts"], 1)
                pool.wait_ge(S["blank"], 5)
                nc.gpsimd.affine_select(out=before[:, :], in_=before[:, :], compare_op=ALU.is_gt, fill=0.0, base=0,
                                        pattern=[[1, P]], channel_multiplier=-1).then_inc(S["consts"], 1)
                pool.wait_ge(S["p_place"], 1)
                for it in turns(pool, C // (2 * SENDS)):
                    for u in range(2):
                        n = it * 2 + u
                        wait_apart(pool, S["pool_passed"], S["scat"][u], SENT + it * (16 * SENDS))
                        nc.gpsimd.tensor_copy(ring_i[:, u, :], T.spot[:, bass.ds(n * SENDS, SENDS)])
                        nc.gpsimd.tensor_copy(ring_n[:, u, :, 0], node[:, bass.ds(n * SENDS, SENDS)]).then_inc(S["p_ring"], 1)
                        wait_apart(pool, S["pool_passed"], S["p_ring"], n + 1)
                        for c in range(SENDS):
                            pool.indirect_dma_start(out=A["ids"][:, :],
                                                    out_offset=bass.IndirectOffsetOnAxis(ap=ring_i[:, u, c:c + 1], axis=0),
                                                    in_=ring_n[:, u, c, :], in_offset=None).then_inc(S["scat"][u], 16)

            @block.sync
            def _(sp):
                for u in range(2):
                    sp.wait_ge(S["scat"][u], SENT + 16 * C // 2)
                v = A["ids"].rearrange("(j p) o -> j (p o)", p=P)
                sp.dma_start(back[:, 0, :], v[0:P, :]).then_inc(S["p_back"], 16)
                sp.dma_start(back[0:SLOT_TILES - P, 1, :], v[P:SLOT_TILES, :]).then_inc(S["p_back"], 16)

            @block.vector
            def _(dve):
                def link(ins):
                    T.linked += 1
                    ins.then_inc(S["linked"], 1)
                    dve.wait_ge(S["linked"], T.linked)

                nc.vector.tensor_tensor(hot[:, :, :], T.expert[:, :, :].rearrange("p t i -> p (t i)").unsqueeze(2).broadcast_to([P, C, ROUTED]),
                                        T.iota_f[:, 0:ROUTED].unsqueeze(1).broadcast_to([P, C, ROUTED]),
                                        ALU.is_equal).then_inc(S["p_hot"], 1)
                dve.wait_ge(S["consts"], 16)
                nc.vector.tensor_copy(node[:, :], node_i[:, :])
                nc.vector.tensor_copy(slot[:, :], slot_i[:, :])
                dve.wait_ge(S["p_mm"], 1)
                link(nc.vector.tensor_copy(col[:, :, :].rearrange("p c e -> p (c e)"), ps[:, 0, :, :].rearrange("p b w -> p (b w)")))
                for e in range(ROUTED):
                    ins = nc.vector.tensor_tensor_scan(upto[:, e, :], col[:, :, e], zeros[:, :], 0.0, ALU.add, ALU.add)
                link(ins)
                link(nc.vector.tensor_scalar(tiles_i[:, :], upto[:, :, C - 1], float(P - 1), None, ALU.add))
                link(nc.vector.tensor_scalar(tiles_i[:, :], tiles_i[:, :], 7, None, ALU.arith_shift_right))
                link(nc.vector.tensor_copy(tiles[:, :], tiles_i[:, :]))
                link(nc.vector.tensor_tensor_scan(cum[:, :], tiles[:, :], zeros[:, 0:ROUTED], 0.0, ALU.add, ALU.add))
                link(nc.vector.tensor_tensor(base[:, :], cum[:, :], tiles[:, :], ALU.subtract))
                link(nc.vector.tensor_scalar(base[:, :], base[:, :], float(P), None, ALU.mult))
                link(nc.vector.tensor_tensor(rank[:, :, :], upto[:, :, :].rearrange("p e c -> p c e"), col[:, :, :], ALU.subtract))
                link(nc.vector.tensor_tensor(rank[:, :, :], rank[:, :, :], base[:, :].unsqueeze(1).broadcast_to([P, C, ROUTED]), ALU.add))
                link(nc.vector.tensor_tensor(rank[:, :, :].rearrange("p c e -> p (c e)"), rank[:, :, :].rearrange("p c e -> p (c e)"),
                                             ps[:, 1, :, :].rearrange("p b w -> p (b w)"), ALU.add))
                link(nc.vector.tensor_tensor(rank[:, :, :], rank[:, :, :], hot[:, :, :], ALU.mult))
                link(nc.vector.reduce_sum(place[:, :], rank[:, :, :], AX.X))
                nc.vector.tensor_copy(T.spot[:, :], place[:, :]).then_inc(S["p_place"], 1)
                link(nc.vector.tensor_scalar(eof[:, :], slot[0:1, :], cum[0:1, 0:1], None, ALU.is_ge))
                for e in range(1, ROUTED - 1):
                    link(nc.vector.scalar_tensor_tensor(out=eof[:, :], in0=slot[0:1, :], scalar=cum[0:1, e:e + 1], in1=eof[:, :],
                                                        op0=ALU.is_ge, op1=ALU.add))
                nc.vector.tensor_copy(T.expert_of[:, :], eof[:, :])
                dve.wait_ge(S["p_turn"], 1)
                nc.vector.tensor_copy(T.ids[:, :], tp[:, 0:SLOT_TILES])

            @block.tensor
            def _(pe):
                pe.wait_ge(S["consts"], 16)
                pe.wait_ge(S["p_hot"], 1)
                flat = hot[:, :, :].rearrange("p c e -> p (c e)")
                for i, lhs in enumerate((ones, before)):
                    for h in range(2):
                        ins = nc.tensor.matmul(ps[:, i, h, :], lhs[:, :], flat[:, h * 512:(h + 1) * 512], start=True, stop=True)
                ins.then_inc(S["p_mm"], 1)
                pe.wait_ge(S["p_back"], 32)
                nc.tensor.transpose(tp[:, 0:P], back[:, 0, :], T.ident[:, :])
                r = SLOT_TILES - P
                nc.tensor.transpose(tp[:, P:SLOT_TILES], back[0:r, 1, :], T.ident[0:r, 0:r]).then_inc(S["p_turn"], 1)


def routed_stage(nc, A, T, S):
    ctx = ExitStack()
    sb = lambda name, shape, dt=F32: ctx.enter_context(nc.sbuf_tensor(name, shape, dt))
    pb = lambda name, shape: ctx.enter_context(nc.psum_tensor(name, shape, F32))
    with ctx:
        w1 = sb("w1r", [P, ROUTED, K, FF])
        w2 = sb("w2r", [P, ROUTED, FC, D])
        b1 = sb("b1r", [P, ROUTED, FF])
        idx = sb("idx_r", [P, 4], I32)
        rows = sb("rows_r", [P, 4, D])
        rT = sb("rT", [P, 2, K, P])
        pre = sb("pre", [P, 2, FF])
        act_h = sb("act_h", [P, 2, FF])
        hT = sb("hT_r", [P, 2, FC, P])
        ob = sb("ob", [P, 4, D])
        tr = pb("tr_r", [P, 2, 512])
        up = pb("up_r", [P, 2, 512])
        ht = pb("ht_r", [P, 2, 512])
        down = pb("down_r", [P, 2, 512])
        o3 = A["slots"].rearrange("(j p) d -> p j d", p=P)
        LAST = SLOT_TILES - 1

        def four(eng):
            for it, last in turns_and_last(eng, SLOT_TILES // 4):
                for u in range(4):
                    yield it * 4 + u, it, u

        with nc.Block() as block:
            @block.sync
            def _(sp):
                sp.dma_start(b1[:, :, :], A["rb1"].rearrange("(o e) f -> o e f", o=1).broadcast_to([P, ROUTED, FF])).then_inc(S["s_par"], 16)
                for e in range(ROUTED):
                    sp.dma_start(w1[:, e, :, :], A["w1"][SHARED + e]).then_inc(S["s_par"], 16)
                    sp.dma_start(w2[:, e, :, :], A["w2"][SHARED + e]).then_inc(S["s_par"], 16)
                for j, it, u in four(sp):
                    sp.wait_ge(S["s_ob"], j + 1)
                    sp.dma_start(o3[:, bass.ds(j, 1), :], ob[:, u:u + 1, :]).then_inc(S["s_st"][u], 16)
                for u in range(4):
                    sp.wait_ge(S["s_st"][u], 16 * (SLOT_TILES // 4))

            @block.gpsimd
            def _(pool):
                for j, it, u in four(pool):
                    pool.wait_ge(S["s_tr"], it * 4 + u - 3 if not isinstance(it, int) or it else 0)
                    nc.gpsimd.tensor_copy(idx[:, u:u + 1], T.ids[:, bass.ds(j, 1)]).then_inc(S["s_idx"], 1)
                    wait_apart(pool, S["pool_passed"], S["s_idx"], j + 1)
                    pool.indirect_dma_start(out=rows[:, u, :], out_offset=None, in_=A["yn"][:, :],
                                            in_offset=bass.IndirectOffsetOnAxis(ap=idx[:, u:u + 1], axis=0)).then_inc(S["s_rows"][u], 16)

            @block.vector
            def _(dve):
                dve.wait_ge(S["s_par"], 16 * (1 + 2 * ROUTED))

                def rows_out(j, u):
                    dve.wait_ge(S["s_tr"], j + 1)
                    dve.wait_ge(S["s_up"], j - 1 if not isinstance(j, int) or j > 0 else 0)
                    nc.vector.tensor_copy(rT[:, u % 2, :, :].rearrange("p k t -> p (k t)"), tr[:, u % 2, :]).then_inc(S["s_rT"], 1)

                def bias(j, u):
                    e = dve.value_load(T.expert_of[0:1, bass.ds(j, 1)], min_val=0, max_val=ROUTED - 1)
                    dve.wait_ge(S["s_up"], j + 1)
                    dve.wait_ge(S["s_gelu"], j - 1 if not isinstance(j, int) or j > 0 else 0)
                    nc.vector.tensor_tensor(pre[:, u % 2, :], up[:, u % 2, 0:FF], b1[:, bass.ds(e, 1), :].rearrange("p o f -> p (o f)"),
                                            ALU.add).then_inc(S["s_pre"], 1)

                def sums_out(j, u):
                    dve.wait_ge(S["s_down"], j + 1)
                    dve.wait_ge(S["s_st"][u % 4], 16 * (j // 4) if isinstance(j, int) else st_count(j, u))
                    nc.vector.tensor_copy(ob[:, u % 4, :], down[:, u % 2, :]).then_inc(S["s_ob"], 1)

                def st_count(j, u):
                    return (j - (u % 4)) * 4

                rows_out(0, 0)
                for j, it, u in four(dve):
                    if not (isinstance(j, int) and j == LAST):
                        rows_out(j + 1, u + 1)
                    bias(j, u)
                    if not (isinstance(j, int) and j == 0):
                        sums_out(j - 1, u + 3)
                sums_out(LAST, 3)

            @block.scalar
            def _(act):
                def turned(j, u):
                    act.wait_ge(S["s_ht"], j + 1)
                    nc.scalar.copy(hT[:, u % 2, :, :].rearrange("p c t -> p (c t)"), ht[:, u % 2, 0:FF]).then_inc(S["s_hT"], 1)

                for j, it, u in four(act):
                    if not (isinstance(j, int) and j == 0):
                        turned(j - 1, u + 3)
                    act.wait_ge(S["s_pre"], j + 1)
                    nc.scalar.activation(act_h[:, u % 2, :], pre[:, u % 2, :], ACT.Gelu).then_inc(S["s_gelu"], 1)
                turned(LAST, 3)

            @block.tensor
            def _(pe):
                def turn(j, u):
                    pe.wait_ge(S["s_rows"][u % 4], 16 * (j // 4 + 1) if isinstance(j, int) else (j - (u % 4)) * 4 + 16)
                    pe.wait_ge(S["s_rT"], j - 1 if not isinstance(j, int) or j > 0 else 0)
                    for k in range(K):
                        ins = nc.tensor.transpose(tr[:, u % 2, k * P:(k + 1) * P], rows[:, u % 4, k * P:(k + 1) * P], T.ident[:, :])
                    ins.then_inc(S["s_tr"], 1)

                def turn_h(j, u):
                    pe.wait_ge(S["s_gelu"], j + 1)
                    pe.wait_ge(S["s_hT"], j - 1 if not isinstance(j, int) or j > 0 else 0)
                    for c in range(FC):
                        ins = nc.tensor.transpose(ht[:, u % 2, c * P:(c + 1) * P], act_h[:, u % 2, c * P:(c + 1) * P], T.ident[:, :])
                    ins.then_inc(S["s_ht"], 1)

                def expert(j):
                    return pe.value_load(T.expert_of[0:1, bass.ds(j, 1)], min_val=0, max_val=ROUTED - 1)

                def first(j, u):
                    e = expert(j)
                    pe.wait_ge(S["s_rT"], j + 1)
                    pe.wait_ge(S["s_pre"], j - 1 if not isinstance(j, int) or j > 0 else 0)
                    for k in range(K):
                        ins = nc.tensor.matmul(up[:, u % 2, 0:FF], rT[:, u % 2, k, :], w1[:, bass.ds(e, 1), k, :].rearrange("p o f -> p (o f)"),
                                               start=(k == 0), stop=(k == K - 1))
                    ins.then_inc(S["s_up"], 1)

                def second(j, u):
                    e = expert(j)
                    pe.wait_ge(S["s_hT"], j + 1)
                    pe.wait_ge(S["s_ob"], j - 1 if not isinstance(j, int) or j > 0 else 0)
                    for c in range(FC):
                        ins = nc.tensor.matmul(down[:, u % 2, :], hT[:, u % 2, c, :], w2[:, bass.ds(e, 1), c, :].rearrange("p o d -> p (o d)"),
                                               start=(c == 0), stop=(c == FC - 1))
                    ins.then_inc(S["s_down"], 1)

                pe.wait_ge(S["s_par"], 16 * (1 + 2 * ROUTED))
                turn(0, 0)
                for j, it, u in four(pe):
                    if not (isinstance(j, int) and j == 0):
                        turn_h(j - 1, u + 3)
                    if not (isinstance(j, int) and j == LAST):
                        turn(j + 1, u + 1)
                    first(j, u)
                    if not (isinstance(j, int) and j == 0):
                        second(j - 1, u + 3)
                turn_h(LAST, 3)
                second(LAST, 3)


def combine_stage(nc, A, T, S):
    ctx = ExitStack()
    sb = lambda name, shape, dt=F32: ctx.enter_context(nc.sbuf_tensor(name, shape, dt))
    with ctx:
        RING = 4
        GATHERED = 16 * COLS // GATHERS
        STORED = 16 * SLOT_TILES // 4
        idx = sb("idx_c", [P, RING, 2], I32)
        rows = sb("rows_c", [P, RING, 2, D])
        acc = sb("acc_c", [P, RING, D])
        res = sb("res_c", [P, RING, D])
        y3 = A["y1"].rearrange("(t p) d -> p t d", p=P)
        out3 = A["out"].rearrange("(t p) d -> p t d", p=P)

        with nc.Block() as block:
            @block.sync
            def _(sp):
                for it in turns(sp, TILES // RING):
                    for u in range(RING):
                        sp.wait_ge(S["f_acc"], it * RING + u - 3 if not isinstance(it, int) or it else 0)
                        sp.dma_start(acc[:, u:u + 1, :], y3[:, bass.ds(it * RING + u, 1), :]).then_inc(S["f_ld"][u], 16)

            @block.gpsimd
            def _(pool):
                for it in turns(pool, TILES // RING):
                    for u in range(RING):
                        t = it * RING + u
                        pool.wait_ge(S["f_acc"], t - 3 if not isinstance(it, int) or it else 0)
                        nc.gpsimd.tensor_copy(idx[:, u, :], T.spot[:, bass.ds(t * 2, 2)]).then_inc(S["f_idx"], 1)
                        wait_apart(pool, S["pool_passed"], S["f_idx"], t + 1)
                        for i in range(2):
                            pool.indirect_dma_start(out=rows[:, u, i, :], out_offset=None, in_=A["slots"][:, :],
                                                    in_offset=bass.IndirectOffsetOnAxis(ap=idx[:, u, i:i + 1], axis=0)).then_inc(S["gath"][u], 16)

            @block.vector
            def _(dve):
                for it in turns(dve, TILES // RING):
                    for u in range(RING):
                        t = it * RING + u
                        dve.wait_ge(S["f_ld"][u], it * 16 + 16)
                        dve.wait_ge(S["gath"][u], GATHERED + it * 32 + 32)
                        p = T.prob[:, bass.ds(t, 1), :].rearrange("p o i -> p (o i)")
                        nc.vector.scalar_tensor_tensor(out=acc[:, u, :], in0=rows[:, u, 0, :], scalar=p[:, 0:1], in1=acc[:, u, :],
                                                       op0=ALU.mult, op1=ALU.add).then_inc(S["f_half"], 1)
                        dve.wait_ge(S["f_half"], t + 1)
                        dve.wait_ge(S["s_st"][u], STORED + it * 16)
                        nc.vector.scalar_tensor_tensor(out=res[:, u, :], in0=rows[:, u, 1, :], scalar=p[:, 1:2], in1=acc[:, u, :],
                                                       op0=ALU.mult, op1=ALU.add).then_inc(S["f_acc"], 1)

            @block.scalar
            def _(act):
                for it in turns(act, TILES // RING):
                    for u in range(RING):
                        t = it * RING + u
                        act.wait_ge(S["f_acc"], t + 1)
                        act.dma_start(out3[:, bass.ds(t, 1), :], res[:, u:u + 1, :]).then_inc(S["s_st"][u], 16)
                for u in range(RING):
                    act.wait_ge(S["s_st"][u], STORED + 16 * (TILES // RING))


class Kept:
    pass


def gps_layer(nc, A):
    ctx = ExitStack()
    T, S = Kept(), {}
    T.linked = 0
    with ctx:
        for name in ("dve_passed pool_passed linked e_load consts blank "
                     "kw xn_done tr_free tr_done var rstd half act_free neg_done e_done top_done corr_done p_done "
                     "ctx_done ctx_free vh_done k_done kf_done bmax_done tmax ks bn k_init "
                     "c_load c_dve c_tr c_mm "
                     "n_bias n_x n_idx n_dw n_y hot agg_done q_done q_red q_sub q_exp qn_done qt_done qt_sb o_done o_sb "
                     "r_cnt r_cld r_part r_ast r_rank r_cps r_raw r_tr r_trfree r_hot r_tot r_start r_carry r_bound r_bfree r_rps r_place d_load d_dv1 d_dv2 d_pe d_pick d_tab d_tfree ring "
                     "x_par x_out half2 var2 rstd2 bn2 nm pr up_done hT tr2_done yn tT r_dve logit cw cw_init "
                     "cwT cwT_done down_done y_done x_zero x_zst "
                     "p_place p_ring p_back p_hot p_mm p_turn "
                     "s_par s_ob s_tr s_idx s_rT s_up s_gelu s_pre s_down s_ht s_hT f_acc f_idx f_half").split():
            S[name] = ctx.enter_context(nc.semaphore(name))
        for name, n in (("x_ld", 2), ("r_cst", 2), ("r_ald", 2), ("scat", 2), ("yn_st", BLK),
                        ("s_st", 4), ("s_rows", 4), ("f_ld", 4), ("xt_st", 2), ("h_st", 2), ("n_xt", 2), ("gath", GATHERS)):
            S[name] = [ctx.enter_context(nc.semaphore(f"{name}{i}")) for i in range(n)]
        sb = lambda name, shape, dt=F32: ctx.enter_context(nc.sbuf_tensor(name, shape, dt))
        T.ident = sb("ident", [P, P])
        T.iota_i = sb("iota_i", [P, P], I32)
        T.iota_f = sb("iota_f", [P, P])
        T.bounds = sb("bounds", [TILES, 2])
        T.ctx = sb("ctx", [P, K, P])
        T.ksum = sb("ksum", [P, K])
        with nc.sbuf_tensor("rec", [P, ROWS, 3], F32) as T.rec, nc.sbuf_tensor("place_i", [P, ROWS], I32) as T.place:
            ranks_stage(nc, A, T, S)
            keys_stage(nc, A, T, S)
        T.src_t = sb("src_t", [P, COLS], I32)
        T.dst_w = sb("dst_w", [P, 2 * COLS])
        T.tile_of = sb("tile_of", [1, ALL_STEPS], I32)
        T.w_q = sb("w_q", [P, K, D])
        T.mix = sb("mix", [P, K, D])
        edges_stage(nc, A, T, S)
        context_stage(nc, A, T, S)
        T.expert = sb("expert", [P, TILES, 2])
        T.prob = sb("prob2", [P, TILES, 2])
        with nc.sbuf_tensor("y", [P, TILES, D], F32) as T.y:
            nodes_stage(nc, A, T, S)
            shared_stage(nc, A, T, S)
        T.spot = sb("spot", [P, 2 * TILES], I32)
        T.expert_of = sb("expert_of", [1, SLOT_TILES], I32)
        T.ids = sb("ids", [P, SLOT_TILES], I32)
        places_stage(nc, A, T, S)
        routed_stage(nc, A, T, S)
        combine_stage(nc, A, T, S)


def kernel(**inputs):
    import concourse.bacc as _bacc
    import numpy as _np
    from concourse import mybir as _mybir
    from concourse.bass_utils import run_bass_kernel_spmd as _run

    g = {k: _np.asarray(v) for k, v in inputs.items()}
    w1 = _np.concatenate([g["L0_ffn_sw1"], g["L0_ffn_rw1"]])
    w2 = _np.concatenate([g["L0_ffn_sw2"], g["L0_ffn_rw2"]])
    b1 = _np.concatenate([g["L0_ffn_sb1"], g["L0_ffn_rb1"]])
    arrays = {
        "x": g["x"], "src": g["src"], "dst": g["dst"], "edge_weight": g["edge_weight"],
        "w_gnn": g["L0_gnn_weight"].T,
        "w_qkv": g["L0_mix_w_qkv"], "w_proj": g["L0_mix_w_proj"], "b_proj": g["L0_mix_b_proj"],
        "gate_wT": g["L0_ffn_gate_w"].T, "gate_b": g["L0_ffn_gate_b"],
        "w1": w1.transpose(0, 2, 1).reshape(EXPERTS, K, P, FF).transpose(0, 2, 1, 3),
        "w2": w2.transpose(0, 2, 1).reshape(EXPERTS, FC, P, D).transpose(0, 2, 1, 3),
        "b1": b1.reshape(EXPERTS, FC, P).transpose(2, 0, 1),
        "rb1": g["L0_ffn_rb1"], "rb2": g["L0_ffn_rb2"], "sb2": g["L0_ffn_sb2"],
    }
    arrays = {k: _np.ascontiguousarray(v) for k, v in arrays.items()}
    nc = _bacc.Bacc("TRN2", target_bir_lowering=False, num_devices=1)
    A = {k: nc.dram_tensor(f"in_{k}", a.shape, _mybir.dt.from_np(a.dtype), kind="ExternalInput").ap() for k, a in arrays.items()}
    A["xT"] = nc.dram_tensor("xT_dram", (BLOCKS, P, K * BLK * P), F32).ap()
    A["h"] = nc.dram_tensor("h_dram", (N, D), F32).ap()
    A["cnt"] = nc.dram_tensor("cnt_dram", (ROWS // 32, 32 * TILES), F16).ap()
    A["aux"] = nc.dram_tensor("aux_dram", (2, ROWS // 32, 32 * TILES), F16).ap()
    A["recs"] = nc.dram_tensor("recs_dram", (E, 3), F32).ap()
    A["y1"] = nc.dram_tensor("y_dram", (N, D), F32).ap()
    A["yn"] = nc.dram_tensor("yn_dram", (N, D), F32).ap()
    A["ids"] = nc.dram_tensor("ids_dram", (SLOT_TILES * P, 1), F32).ap()
    A["slots"] = nc.dram_tensor("slots_dram", (SLOT_TILES * P, D), F32).ap()
    A["out"] = nc.dram_tensor("out_0", (N, D), F32, kind="ExternalOutput").ap()
    gps_layer(nc, A)
    r = _run(nc, [{f"in_{k}": a for k, a in arrays.items()}], core_ids=[0])
    return r.results[0]["out_0"]
```

```python
from contextlib import ExitStack

import concourse.bass as bass
import numpy as np
from concourse import mybir

F32 = mybir.dt.float32
I32 = mybir.dt.int32
U32 = mybir.dt.uint32
F16 = mybir.dt.float16
F32R = mybir.dt.float32r
ALU = mybir.AluOpType
ACT = mybir.ActivationFunctionType
AX = mybir.AxisListType

P = 128
N, D = 8192, 512
E = 139264
K = D // P
TILES = N // P
BLK = 4
BLOCKS = TILES // BLK
ROWS = E // P
FULL = ROWS // P
REST = ROWS - FULL * P
GROUPS = FULL + (REST > 0)
MACRO = ROWS // 2
PAIRS = TILES // 2
STEPS = 19
ALL_STEPS = STEPS * PAIRS
assert ALL_STEPS >= MACRO + TILES - 1
CHUNKS = 2 * STEPS
COLS = CHUNKS * PAIRS
HEADS, HD = 8, 64
SHARED, ROUTED, FF = 2, 8, 256
EXPERTS = SHARED + ROUTED
FC = FF // P
SLOT_TILES = 2 * TILES + ROUTED
EPS = 1e-5
GRING = 9
GATHERS = GRING + 2
ARING = 6
BANKS = ARING + 1
assert (STEPS - 1) % ARING == 0 and (CHUNKS - 2) % GRING == 0


def wait_apart(eng, passed, sem, value):
    eng.wait_ge(sem, value)
    eng.sem_inc(passed, 1)


def turns(eng, count):
    yield 0
    with eng.Fori(1, count) as it:
        yield it


def turns_and_last(eng, count):
    yield 0, False
    with eng.Fori(1, count - 1) as it:
        yield it, False
    yield count - 1, True


def ranks_stage(nc, A, T, S):
    ctx = ExitStack()
    sb = lambda name, shape, dt=F32: ctx.enter_context(nc.sbuf_tensor(name, shape, dt))
    pb = lambda name, shape: ctx.enter_context(nc.psum_tensor(name, shape, F32))
    UNIT = 32
    UNITS = ROWS // UNIT
    UW = UNIT * TILES
    assert UW == 4 * 512 and UNITS % 2 == 0
    with ctx:
        raw_i = sb("raw_i", [P, 2, GROUPS, P], I32)
        raw = sb("raw", [P, 3, GROUPS, P])
        src_i = sb("src_i", [P, ROWS], I32)
        iota_h = sb("iota_h", [P, TILES], F16)
        tile_c = sb("tile_c", [P, ROWS], F16)
        hot = sb("hot_tiles", [P, ROWS, TILES], F16)
        ones = sb("ones_r", [P, P], F16)
        onesf = sb("onesf_r", [1, 1])
        before = sb("before", [P, P], F16)
        weigh = sb("weigh", [2, P], F16)
        cnt = sb("cnt", [P, GROUPS, TILES], F16)
        total = sb("total", [P, TILES])
        upto = sb("upto", [P, TILES])
        start = sb("start", [P, TILES])
        zeros = sb("zeros_r", [P, TILES])
        carry = sb("carry", [P, TILES])
        carry_i = sb("carry_i", [P, GROUPS, TILES], I32)
        part_i = sb("part_i", [P, 2, GROUPS, TILES], I32)
        part = sb("part", [P, 2, GROUPS, TILES], F16)
        aux = sb("aux", [2, 2, UW], F16)
        cnt_row = aux[0:1, :, :]
        flat = raw[:, :, :, :].rearrange("p a g c -> p (a g c)")
        prod = flat[:, 0:UW]
        place = flat[:, UW:UW + ROWS]
        ps = pb("ps_r", [P, 2, UW])

        with nc.Block() as block:
            @block.sync
            def _(sp):
                for a, name in enumerate(("src", "dst")):
                    v = A[name].rearrange("(r c) -> r c", c=P)
                    sp.dma_start(raw_i[:, a, 0:FULL, :], v[0:FULL * P, :].rearrange("(g p) c -> p g c", p=P)).then_inc(S["e_load"], 16)
                    sp.dma_start(raw_i[0:REST, a, FULL, :], v[FULL * P:ROWS, :]).then_inc(S["e_load"], 16)
                v = A["edge_weight"].rearrange("(r c) -> r c", c=P)
                sp.dma_start(raw[:, 2, 0:FULL, :], v[0:FULL * P, :].rearrange("(g p) c -> p g c", p=P)).then_inc(S["e_load"], 16)
                sp.dma_start(raw[0:REST, 2, FULL, :], v[FULL * P:ROWS, :]).then_inc(S["e_load"], 16)
                for it in turns(sp, UNITS // 2):
                    for u in range(2):
                        n = it * 2 + u
                        sp.wait_ge(S["r_cnt"], n + 3)
                        sp.dma_start(A["cnt"][bass.ds(n, 1), :], cnt_row[:, u, :]).then_inc(S["r_cst"][u], 16)
                for u in range(2):
                    sp.wait_ge(S["r_cst"][u], 16 * (UNITS // 2))
                cv = A["cnt"].rearrange("n (c t) -> (n c) t", t=TILES)
                sp.dma_start(cnt[:, 0:FULL, :], cv[0:FULL * P, :].rearrange("(g p) t -> p g t", p=P)).then_inc(S["r_cld"], 16)
                sp.dma_start(cnt[0:REST, FULL, :], cv[FULL * P:ROWS, :]).then_inc(S["r_cld"], 16)
                sp.wait_ge(S["r_part"], 1)
                for h in range(2):
                    av = A["aux"][h].rearrange("n (c t) -> (n c) t", t=TILES)
                    sp.dma_start(av[0:FULL * P, :].rearrange("(g p) t -> p g t", p=P), part[:, h, 0:FULL, :]).then_inc(S["r_ast"], 16)
                    sp.dma_start(av[FULL * P:ROWS, :], part[0:REST, h, FULL, :]).then_inc(S["r_ast"], 16)
                sp.wait_ge(S["r_ast"], 64)
                for it in turns(sp, UNITS // 2):
                    for u in range(2):
                        n = it * 2 + u
                        sp.wait_ge(S["r_rank"], n + 1)
                        sp.dma_start(aux[:, u, :], A["aux"][:, bass.ds(n, 1), :].rearrange("h o w -> h (o w)")).then_inc(S["r_ald"][u], 16)

            @block.gpsimd
            def _(pool):
                nc.gpsimd.iota(T.iota_i[:, :], pattern=[[1, P]], base=0, channel_multiplier=0).then_inc(S["consts"], 1)
                nc.gpsimd.memset(ones[:, :], 1.0).then_inc(S["consts"], 1)
                nc.gpsimd.memset(onesf[:, :], 1.0).then_inc(S["consts"], 1)
                nc.gpsimd.memset(zeros[:, :], 0.0).then_inc(S["consts"], 1)
                nc.gpsimd.memset(before[:, :], 1.0).then_inc(S["blank"], 1)
                nc.gpsimd.memset(T.ident[:, :], 0.0).then_inc(S["blank"], 1)
                nc.gpsimd.memset(weigh[:, :], 256.0).then_inc(S["blank"], 1)
                pool.wait_ge(S["blank"], 3)
                nc.gpsimd.affine_select(out=before[:, :], in_=before[:, :], compare_op=ALU.is_gt, fill=0.0, base=0,
                                        pattern=[[1, P]], channel_multiplier=-1).then_inc(S["consts"], 1)
                nc.gpsimd.affine_select(out=T.ident[:, :], in_=T.ident[:, :], compare_op=ALU.not_equal, fill=1.0, base=0,
                                        pattern=[[-1, P]], channel_multiplier=1).then_inc(S["consts"], 1)
                nc.gpsimd.affine_select(out=weigh[:, :], in_=weigh[:, :], compare_op=ALU.not_equal, fill=1.0, base=-1,
                                        pattern=[[0, P]], channel_multiplier=1).then_inc(S["consts"], 1)

            @block.scalar
            def _(act):
                for it in turns(act, UNITS // 2):
                    for u in range(2):
                        n = it * 2 + u
                        act.wait_ge(S["r_cps"], n + 1)
                        act.wait_ge(S["r_cst"][u], it * 16)
                        nc.scalar.copy(cnt_row[:, u, :], ps[0:1, u, :]).then_inc(S["r_cnt"], 1)

            @block.vector
            def _(dve):
                def link(ins):
                    T.linked += 1
                    ins.then_inc(S["linked"], 1)
                    dve.wait_ge(S["linked"], T.linked)

                dve.wait_ge(S["consts"], 7)
                nc.vector.tensor_copy(T.iota_f[:, :], T.iota_i[:, :])
                nc.vector.tensor_copy(iota_h[:, :], T.iota_i[:, 0:TILES])
                dve.wait_ge(S["e_load"], 16 * 6)
                for a in range(2):
                    nc.vector.tensor_copy(raw[:, a, 0:FULL, :], raw_i[:, a, 0:FULL, :])
                    link(nc.vector.tensor_copy(raw[0:REST, a, FULL, :], raw_i[0:REST, a, FULL, :]))
                nc.vector.sem_inc(S["r_raw"], 1)
                for a in range(3):
                    dve.wait_ge(S["r_tr"], a + 1)
                    link(nc.vector.tensor_copy(T.rec[:, :, a], ps[:, a % 2, 0:ROWS]))
                    nc.vector.sem_inc(S["r_trfree"], 1)
                link(nc.vector.tensor_copy(src_i[:, :], T.rec[:, :, 0]))
                link(nc.vector.tensor_scalar(src_i[:, :], src_i[:, :], 7, None, ALU.arith_shift_right))
                link(nc.vector.tensor_copy(tile_c[:, :], src_i[:, :]))
                with dve.Fori(0, UNITS) as n:
                    nc.vector.tensor_tensor(hot[:, bass.ds(n * UNIT, UNIT), :],
                                            tile_c[:, bass.ds(n * UNIT, UNIT)].unsqueeze(2).broadcast_to([P, UNIT, TILES]),
                                            iota_h[:, :].unsqueeze(1).broadcast_to([P, UNIT, TILES]),
                                            ALU.is_equal).then_inc(S["r_hot"], 1)
                dve.wait_ge(S["r_tot"], 1)
                link(nc.vector.tensor_copy(total[:, :], ps[:, 0, 0:TILES]))
                link(nc.vector.tensor_tensor_scan(upto[:, :], total[:, :], zeros[:, :], 0.0, ALU.add, ALU.add))
                link(nc.vector.tensor_tensor(start[:, :], upto[:, :], total[:, :], ALU.subtract))
                nc.vector.sem_inc(S["r_start"], 1)
                dve.wait_ge(S["r_carry"], GROUPS)
                for g in range(GROUPS):
                    r = P if g < FULL else REST
                    link(nc.vector.tensor_tensor(carry[0:r, :], start[0:r, :], ps[0:r, 1, g * TILES:(g + 1) * TILES], ALU.add))
                    link(nc.vector.tensor_copy(carry_i[0:r, g, :], carry[0:r, :]))
                    link(nc.vector.tensor_scalar(part_i[0:r, 0, g, :], carry_i[0:r, g, :], 8, None, ALU.arith_shift_right))
                    link(nc.vector.tensor_scalar(part_i[0:r, 1, g, :], carry_i[0:r, g, :], 255, None, ALU.bitwise_and))
                    link(nc.vector.tensor_copy(part[0:r, :, g, :], part_i[0:r, :, g, :]))
                nc.vector.sem_inc(S["r_part"], 1)
                dve.wait_ge(S["r_bound"], 1)
                link(nc.vector.tensor_copy(T.bounds[:, :], ps[0:TILES, 0, 512:514]))
                nc.vector.sem_inc(S["r_bfree"], 1)
                for it in turns(dve, UNITS // 2):
                    for u in range(2):
                        n = it * 2 + u
                        dve.wait_ge(S["r_rps"], n + 1)
                        dve.wait_ge(S["r_place"], n)
                        nc.vector.tensor_tensor(prod[:, :], ps[:, u, :], hot[:, bass.ds(n * UNIT, UNIT), :].rearrange("p c t -> p (c t)"),
                                                ALU.mult).then_inc(S["r_rank"], 1)
                        dve.wait_ge(S["r_rank"], n + 3)
                        nc.vector.reduce_sum(place[:, bass.ds(n * UNIT, UNIT)], prod[:, :].rearrange("p (c t) -> p c t", t=TILES),
                                             AX.X).then_inc(S["r_place"], 1)
                dve.wait_ge(S["r_place"], UNITS)
                nc.vector.tensor_copy(T.place[:, :], place[:, :])

            @block.tensor
            def _(pe):
                pe.sem_inc(S["r_rank"], 2)
                pe.sem_inc(S["r_cnt"], 2)
                pe.wait_ge(S["consts"], 7)
                pe.wait_ge(S["r_raw"], 1)
                for a in range(3):
                    if a == 2:
                        pe.wait_ge(S["r_trfree"], 1)
                    for g in range(GROUPS):
                        r = P if g < FULL else REST
                        ins = nc.tensor.transpose(ps[:, a % 2, g * P:g * P + r], raw[0:r, a, g, :], T.ident[0:r, 0:r])
                    ins.then_inc(S["r_tr"], 1)
                pe.wait_ge(S["r_trfree"], 3)
                for it in turns(pe, UNITS // 2):
                    for u in range(2):
                        n = it * 2 + u
                        pe.wait_ge(S["r_hot"], n + 1)
                        pe.wait_ge(S["r_cnt"], n + 1)
                        for c in range(4):
                            ins = nc.tensor.matmul(ps[:, u, c * 512:(c + 1) * 512], ones[:, :],
                                                   hot[:, bass.ds(n * UNIT + c * 8, 8), :].rearrange("p c t -> p (c t)"),
                                                   start=True, stop=True)
                        ins.then_inc(S["r_cps"], 1)
                pe.wait_ge(S["r_cld"], 32)
                pe.wait_ge(S["r_cnt"], UNITS + 2)
                for g in range(GROUPS):
                    r = P if g < FULL else REST
                    ins = nc.tensor.matmul(ps[:, 0, 0:TILES], ones[0:r, :], cnt[0:r, g, :], start=(g == 0), stop=(g == GROUPS - 1))
                ins.then_inc(S["r_tot"], 1)
                for g in range(GROUPS):
                    r = P if g < FULL else REST
                    ins = nc.tensor.matmul(ps[0:r, 1, g * TILES:(g + 1) * TILES], before[0:r, 0:r], cnt[0:r, g, :],
                                           start=True, stop=(g == 0))
                    for e in range(g):
                        ins = nc.tensor.matmul(ps[0:r, 1, g * TILES:(g + 1) * TILES], ones[:, 0:r], cnt[:, e, :],
                                               start=False, stop=(e == g - 1))
                    ins.then_inc(S["r_carry"], 1)
                pe.wait_ge(S["r_start"], 1)
                nc.tensor.matmul(ps[0:TILES, 0, 512:513], start[0:1, :], onesf[:, :], start=True, stop=True)
                nc.tensor.matmul(ps[0:TILES, 0, 513:514], upto[0:1, :], onesf[:, :], start=True, stop=True).then_inc(S["r_bound"], 1)
                pe.wait_ge(S["r_bfree"], 1)
                for it in turns(pe, UNITS // 2):
                    for u in range(2):
                        n = it * 2 + u
                        pe.wait_ge(S["r_ald"][u], it * 16 + 16)
                        pe.wait_ge(S["r_rank"], n + 1)
                        for c in range(4):
                            w = slice(c * 512, (c + 1) * 512)
                            nc.tensor.matmul(ps[:, u, w], before[:, :], hot[:, bass.ds(n * UNIT + c * 8, 8), :].rearrange("p c t -> p (c t)"),
                                             start=True, stop=False)
                            ins = nc.tensor.matmul(ps[:, u, w], weigh[:, :], aux[:, u, w], start=False, stop=True)
                        ins.then_inc(S["r_rps"], 1)


def edges_stage(nc, A, T, S):
    ctx = ExitStack()
    sb = lambda name, shape, dt=F32: ctx.enter_context(nc.sbuf_tensor(name, shape, dt))
    pb = lambda name, shape: ctx.enter_context(nc.psum_tensor(name, shape, F32))
    with ctx:
        raw = sb("sorted", [P, GROUPS, P, 3])
        step_i = sb("step_i", [P, ALL_STEPS], I32)
        step_f = sb("step_f", [P, ALL_STEPS])
        ones = sb("ones_e", [P, P])
        upper = sb("upper", [TILES, TILES])
        se_i = sb("se_i", [TILES, 3], I32)
        sh_i = sb("sh_i", [TILES, 3], I32)
        sh_f = sb("sh_f", [TILES, 3])
        some = sb("some", [TILES, 1])
        span = sb("span", [TILES, 1])
        past = sb("past", [TILES, ALL_STEPS])
        delta = sb("delta", [TILES, 1])
        delta_w = sb("delta_w", [TILES, P])
        cum = sb("cum", [TILES, 1])
        row_of = sb("row_of", [P, ALL_STEPS, 2])
        chunk = sb("chunk", [P, ALL_STEPS])
        pidx_i = sb("pidx_i", [P, 1], I32)
        pidx = sb("pidx", [P, 1])
        pick = sb("pick", [P, GROUPS, COLS])
        base = sb("base", [P, ALL_STEPS])
        tile_f = sb("tile_f", [1, ALL_STEPS])
        big = pb("big", [P, 3 * 512])
        wide = pb("wide", [P, 4 * 512])
        small = pb("small", [P, 512])

        with nc.Block() as block:
            @block.sync
            def _(sp):
                v = A["recs"].rearrange("(r c) w -> r c w", c=P)
                sp.dma_start(raw[:, 0:FULL, :, :], v[0:FULL * P, :, :].rearrange("(g p) c w -> p g c w", p=P)).then_inc(S["d_load"], 16)
                sp.dma_start(raw[0:REST, FULL, :, :], v[FULL * P:ROWS, :, :]).then_inc(S["d_load"], 16)

            @block.gpsimd
            def _(pool):
                nc.gpsimd.iota(step_i[:, :], pattern=[[1, ALL_STEPS]], base=0, channel_multiplier=0).then_inc(S["consts"], 1)
                nc.gpsimd.iota(pidx_i[:, :], pattern=[[1, 1]], base=0, channel_multiplier=1).then_inc(S["consts"], 1)
                nc.gpsimd.memset(ones[:, :], 1.0).then_inc(S["consts"], 1)
                nc.gpsimd.memset(upper[:, :], 1.0).then_inc(S["blank"], 1)
                pool.wait_ge(S["blank"], 4)
                nc.gpsimd.affine_select(out=upper[:, :], in_=upper[:, :], compare_op=ALU.is_ge, fill=0.0, base=0,
                                        pattern=[[1, TILES]], channel_multiplier=-1).then_inc(S["consts"], 1)

            @block.vector
            def _(dve):
                def link(ins):
                    T.linked += 1
                    ins.then_inc(S["linked"], 1)
                    dve.wait_ge(S["linked"], T.linked)

                nc.vector.tensor_copy(se_i[:, 0:2], T.bounds[:, :])
                link(nc.vector.tensor_scalar(se_i[:, 2:3], T.bounds[:, 1:2], 255.0, None, ALU.add))
                link(nc.vector.tensor_scalar(sh_i[:, :], se_i[:, :], 8, None, ALU.arith_shift_right))
                nc.vector.tensor_tensor(some[:, :], T.bounds[:, 1:2], T.bounds[:, 0:1], ALU.is_gt)
                link(nc.vector.tensor_copy(sh_f[:, :], sh_i[:, :]))
                link(nc.vector.tensor_tensor(span[:, :], sh_f[:, 2:3], sh_f[:, 0:1], ALU.subtract))
                link(nc.vector.tensor_tensor(span[:, :], span[:, :], some[:, :], ALU.mult))
                link(nc.vector.tensor_tensor(delta[:, :], sh_f[:, 1:2], sh_f[:, 0:1], ALU.subtract))
                link(nc.vector.tensor_tensor(delta[:, :], delta[:, :], span[:, :], ALU.subtract))
                link(nc.vector.tensor_copy(delta_w[:, :], delta[:, 0:1].broadcast_to([TILES, P])))
                nc.vector.sem_inc(S["d_dv1"], 1)
                dve.wait_ge(S["consts"], 11)
                nc.vector.tensor_copy(step_f[:, :], step_i[:, :])
                link(nc.vector.tensor_copy(pidx[:, :], pidx_i[:, :]))
                dve.wait_ge(S["d_pe"], 1)
                link(nc.vector.tensor_copy(cum[:, :], small[0:TILES, 4:5]))
                nc.vector.tensor_scalar(past[:, :], step_f[0:TILES, :], cum[:, 0:1], None, ALU.is_ge).then_inc(S["d_dv2"], 1)
                dve.wait_ge(S["d_pe"], 2)
                link(nc.vector.tensor_scalar(base[:, :], wide[:, 0:ALL_STEPS], float(P), None, ALU.mult))
                link(nc.vector.tensor_tensor(chunk[:, :], step_f[:, :], wide[:, 1024:1024 + ALL_STEPS], ALU.add))
                link(nc.vector.tensor_scalar(chunk[:, :], chunk[:, :], 0.0, float(MACRO - 1), ALU.max, ALU.min))
                link(nc.vector.tensor_scalar(tile_f[:, :], wide[0:1, 0:ALL_STEPS], float(TILES - 1), None, ALU.min))
                nc.vector.tensor_copy(T.tile_of[:, :], tile_f[:, :])
                nc.vector.tensor_scalar(row_of[:, :, 0], chunk[:, :], 2.0, None, ALU.mult)
                link(nc.vector.tensor_scalar(row_of[:, :, 1], chunk[:, :], 2.0, 1.0, ALU.mult, ALU.add))
                rows = row_of[:, :, :].rearrange("p s h -> p (s h)")
                for g in range(GROUPS):
                    nc.vector.tensor_scalar(pick[:, g, :], rows, float(g * P), pidx[:, 0:1], ALU.subtract,
                                            ALU.is_equal).then_inc(S["d_pick"], 1)
                dstw = T.dst_w[:, :].rearrange("p (t x c) -> p t x c", x=2, c=CHUNKS)
                dve.wait_ge(S["d_tab"], 1)
                link(nc.vector.tensor_copy(row_of[:, :, :].rearrange("p s h -> p (s h)"), big[:, 0:COLS]))
                nc.vector.sem_inc(S["d_tfree"], 1)
                for h in range(2):
                    link(nc.vector.tensor_tensor(row_of[:, :, h], row_of[:, :, h], base[:, :], ALU.subtract))
                nc.vector.tensor_copy(dstw[:, :, 0, :], rows.rearrange("p (t c) -> p t c", c=CHUNKS))
                dve.wait_ge(S["d_tab"], 2)
                link(nc.vector.tensor_copy(T.src_t[:, :], big[:, 0:COLS]))
                nc.vector.sem_inc(S["d_tfree"], 1)
                dve.wait_ge(S["d_tab"], 3)
                nc.vector.tensor_copy(dstw[:, :, 1, :], big[:, 0:COLS].rearrange("p (t c) -> p t c", c=CHUNKS))

            @block.tensor
            def _(pe):
                pe.wait_ge(S["consts"], 11)
                pe.wait_ge(S["d_dv1"], 1)
                nc.tensor.matmul(small[0:TILES, 4:5], upper[:, :], span[:, :], start=True, stop=True).then_inc(S["d_pe"], 1)
                pe.wait_ge(S["d_dv2"], 1)
                for lhs, off in ((ones[0:TILES, :], 0), (delta_w[:, :], 1024)):
                    for lo in range(0, ALL_STEPS, 512):
                        hi = min(lo + 512, ALL_STEPS)
                        last = nc.tensor.matmul(wide[:, off + lo:off + hi], lhs, past[:, lo:hi], start=True, stop=True)
                last.then_inc(S["d_pe"], 1)
                pe.wait_ge(S["d_load"], 32)
                pe.wait_ge(S["d_pick"], GROUPS)
                for a in range(3):
                    if a:
                        pe.wait_ge(S["d_tfree"], a)
                    for lo in range(0, COLS, 512):
                        hi = min(lo + 512, COLS)
                        for g in range(GROUPS):
                            r = P if g < FULL else REST
                            last = nc.tensor.matmul(big[:, lo:hi], raw[0:r, g, :, a], pick[0:r, g, lo:hi],
                                                    start=(g == 0), stop=(g == GROUPS - 1))
                    last.then_inc(S["d_tab"], 1)


def norm_tiles(nc, dve, rows, stat, mv, n_done, sem, passed):
    for a in range(BLK):
        nc.vector.bn_stats(stat[:, a, :], rows(a)).then_inc(sem, 1)
    wait_apart(dve, passed, sem, n_done + BLK)
    for a in range(BLK):
        nc.vector.bn_aggr(mv[:, a, :], stat[:, a, :]).then_inc(sem, 1)
    dve.wait_ge(sem, n_done + 2 * BLK)


def keys_stage(nc, A, T, S):
    ctx = ExitStack()
    sb = lambda name, shape, dt=F32: ctx.enter_context(nc.sbuf_tensor(name, shape, dt))
    pb = lambda name, shape: ctx.enter_context(nc.psum_tensor(name, shape, F32))
    with ctx:
        w_q = sb("w_q", [P, K, D])
        w_k = sb("w_k", [P, K, D])
        w_v = sb("w_v", [P, K, D])
        w_g = sb("w_g", [P, K, D])
        xin = sb("xin", [P, 2, BLK, D])
        xn = sb("xn", [P, BLK, D])
        xnT = sb("xnT", [P, 2, K, BLK * P])
        neg = sb("neg", [P, K, BLK * P])
        kf = sb("kf", [P, K, BLK * P])
        prob = sb("prob", [P, K, BLK * P])
        probT = sb("probT", [P, BLK, D])
        v_sb = sb("v_sb", [P, BLK, D])
        h_sb = sb("h_sb", [P, 2, BLK, D])
        qs = sb("qs", [P, BLK, D])
        qn = sb("qn", [P, BLK, D])
        qT = sb("qT", [P, 2, K, BLK * P])
        red = sb("red", [P, BLK, 3, HEADS])
        stat = sb("stat", [P, BLK, 6])
        mv = sb("mv", [P, BLK, 2])
        rstd = sb("rstd", [P, BLK])
        half = sb("half", [P, BLK])
        bmax = sb("bmax", [P, K])
        top = sb("top", [P, 2, K])
        dtop = sb("dtop", [P, K])
        ntop = sb("ntop", [P, K])
        corr = sb("corr", [P, K])
        bsum = sb("bsum", [P, K])
        BATCH = ROWS // (2 * BLOCKS)
        ring_i = sb("ring_i", [P, 2, BATCH], I32)
        ring_r = sb("ring_r", [P, 2, BATCH, 3])
        mm = pb("mm", [P, 4, 512])
        tr = pb("tr", [P, 2, 512])
        cps = pb("cps", [P, 512])

        x4 = A["x"].rearrange("(b a p) d -> b p a d", a=BLK, p=P)
        h4 = A["h"].rearrange("(b a p) d -> b p a d", a=BLK, p=P)

        with nc.Block() as block:
            @block.sync
            def _(sp):
                wq = A["w_qkv"].rearrange("(k p) n -> p k n", p=P)
                sp.dma_start(xin[:, 0, :, :], x4[0, :, :, :]).then_inc(S["x_ld"][0], 16)
                sp.dma_start(w_q[:, :, :], wq[:, :, 0:D]).then_inc(S["kw"], 16)
                sp.dma_start(w_k[:, :, :], wq[:, :, D:2 * D]).then_inc(S["kw"], 16)
                sp.dma_start(w_v[:, :, :], wq[:, :, 2 * D:3 * D]).then_inc(S["kw"], 16)
                sp.dma_start(w_g[:, :, :], A["w_gnn"].rearrange("(k p) n -> p k n", p=P)).then_inc(S["kw"], 16)
                for it in turns(sp, BLOCKS // 2):
                    for u in range(2):
                        n = it * 2 + u
                        nxt = (n + 1) % BLOCKS
                        sp.wait_ge(S["xn_done"], n * BLK)
                        sp.dma_start(xin[:, 1 - u, :, :], x4[bass.ds(nxt, 1), :, :, :].rearrange("o p a d -> p (o a) d")).then_inc(S["x_ld"][1 - u], 16)
                        sp.wait_ge(S["tr_free"], n * 12 + 8)
                        sp.dma_start(A["qT"][bass.ds(n, 1), :, :].rearrange("o p f -> p (o f)"), qT[:, u, :, :].rearrange("p k t -> p (k t)")).then_inc(S["xt_st"][u], 16)
                for u in range(2):
                    sp.wait_ge(S["xt_st"][u], 16 * (BLOCKS // 2))

            @block.gpsimd
            def _(pool):
                def power(count):
                    pool.wait_ge(S["var"], count)
                    nc.gpsimd.tensor_tensor(rstd[:, :], mv[:, :, 1], half[:, :], ALU.pow).then_inc(S["rstd"], 1)

                nc.gpsimd.memset(half[:, :], -0.5).then_inc(S["half"], 1)
                pool.wait_ge(S["half"], 1)
                power(1)
                for it in turns(pool, BLOCKS // 2):
                    for u in range(2):
                        n = it * 2 + u
                        for h in range(2):
                            wait_apart(pool, S["pool_passed"], S["scat"][h], n * (16 * BATCH))
                            at = (n * 2 + h) * BATCH
                            nc.gpsimd.tensor_copy(ring_i[:, h, :], T.place[:, bass.ds(at, BATCH)])
                            nc.gpsimd.tensor_copy(ring_r[:, h, :, :], T.rec[:, bass.ds(at, BATCH), :]).then_inc(S["ring"], 1)
                            wait_apart(pool, S["pool_passed"], S["ring"], n * 2 + h + 1)
                            for c in range(BATCH):
                                pool.indirect_dma_start(out=A["recs"][:, :],
                                                        out_offset=bass.IndirectOffsetOnAxis(ap=ring_i[:, h, c:c + 1], axis=0),
                                                        in_=ring_r[:, h, c, :], in_offset=None).then_inc(S["scat"][h], 16)
                            if h == 0:
                                power(n + 2)
                        pool.wait_ge(S["act_free"], n * 8 + 16)
                        pool.dma_start(h4[bass.ds(n, 1), :, :, :].rearrange("o p a d -> p (o a) d"), h_sb[:, u, :, :]).then_inc(S["h_st"][u], 16)
                for u in range(2):
                    pool.wait_ge(S["h_st"][u], 16 * (BLOCKS // 2))
                    pool.wait_ge(S["scat"][u], 16 * BATCH * BLOCKS)

            @block.scalar
            def _(act):
                act.sem_inc(S["act_free"], 8)
                for it in turns(act, BLOCKS // 2):
                    for u in range(2):
                        n = it * 2 + u
                        for a in range(BLK):
                            act.wait_ge(S["q_sub"], n * BLK + a + 1)
                            nc.scalar.activation(qs[:, a, :], qs[:, a, :], ACT.Exp).then_inc(S["q_exp"], 1)
                        for j in range(K):
                            act.wait_ge(S["neg_done"], n * K + j + 1)
                            nc.scalar.activation(neg[:, j, :], neg[:, j, :], ACT.Exp).then_inc(S["e_done"], 1)
                        act.wait_ge(S["top_done"], n + 1)
                        nc.scalar.activation(corr[:, :], dtop[:, :], ACT.Exp).then_inc(S["corr_done"], 1)
                        act.wait_ge(S["tr_done"], n * 12 + 4)
                        for j in range(K):
                            nc.scalar.activation(prob[:, j, :], kf[:, j, :], ACT.Exp, bias=ntop[:, j:j + 1],
                                                 accum_out=bsum[:, j:j + 1]).then_inc(S["p_done"], 1)
                        act.wait_ge(S["ctx_done"], n)
                        for a in range(BLK):
                            act.wait_ge(S["vh_done"], n * 8 + a + 1)
                            nc.scalar.copy(v_sb[:, a, :], mm[:, a, :]).then_inc(S["act_free"], 1)
                        act.wait_ge(S["h_st"][u], it * 16)
                        for a in range(BLK):
                            act.wait_ge(S["vh_done"], n * 8 + BLK + a + 1)
                            nc.scalar.copy(h_sb[:, u, a, :], mm[:, a, :]).then_inc(S["act_free"], 1)

            @block.vector
            def _(dve):
                def prep(m, slot, loads, tr0, between):
                    dve.wait_ge(S["x_ld"][slot], loads)
                    norm_tiles(nc, dve, lambda a: xin[:, slot, a, :], stat, mv, m * 2 * BLK, S["bn"], S["dve_passed"])
                    nc.vector.tensor_scalar(mv[:, :, 1], mv[:, :, 1], EPS, None, ALU.add).then_inc(S["var"], 1)
                    dve.wait_ge(S["rstd"], m + 1)
                    if tr0 is not None:
                        dve.wait_ge(S["tr_done"], tr0 - BLK)
                    for a in range(BLK):
                        nc.vector.tensor_scalar(xn[:, a, :], xin[:, slot, a, :], mv[:, a, 0:1], rstd[:, a:a + 1],
                                                ALU.subtract, ALU.mult).then_inc(S["xn_done"], 1)
                    between()
                    for k in range(K):
                        dve.wait_ge(S["tr_done"], (0 if tr0 is None else tr0) + k + 1)
                        nc.vector.tensor_copy(xnT[:, slot, k, :], tr[:, k % 2, :]).then_inc(S["tr_free"], 1)

                nc.vector.memset(top[:, :, :], 0.0).then_inc(S["k_init"], 1)
                nc.vector.memset(T.ksum[:, :], 0.0).then_inc(S["k_init"], 1)
                nc.vector.memset(T.ctx[:, :, :], 0.0).then_inc(S["k_init"], 1)
                dve.wait_ge(S["k_init"], 3)
                prep(0, 0, 16, None, lambda: None)
                for it in turns(dve, BLOCKS // 2):
                    for u in range(2):
                        n = it * 2 + u

                        def low_half(j):
                            dve.wait_ge(S["k_done"], n * K + j + 1)
                            nc.vector.tensor_scalar(neg[:, j, :], mm[:, j, :], 0.0, None, ALU.min).then_inc(S["neg_done"], 1)

                        def high_half(j):
                            dve.wait_ge(S["e_done"], n * K + j + 1)
                            nc.vector.scalar_tensor_tensor(out=kf[:, j, :], in0=mm[:, j, :], scalar=0.0, in1=neg[:, j, :],
                                                           op0=ALU.max, op1=ALU.add).then_inc(S["kf_done"], 1)
                            dve.wait_ge(S["kf_done"], n * K + j + 1)
                            nc.vector.reduce_max(bmax[:, j:j + 1], kf[:, j, :], AX.X).then_inc(S["bmax_done"], 1)

                        reds = [0]

                        def q_link(ins):
                            reds[0] += 1
                            ins.then_inc(S["q_red"], 1)
                            dve.wait_ge(S["q_red"], n * (3 * BLK) + reds[0])

                        def by_head(t):
                            return t.rearrange("p (h d) -> p h d", h=HEADS)

                        def q_first(a):
                            dve.wait_ge(S["q_done"], n * BLK + a + 1)
                            q_link(nc.vector.reduce_max(red[:, a, 0, :], by_head(mm[:, a, :]), AX.X))
                            nc.vector.tensor_tensor(by_head(qs[:, a, :]), by_head(mm[:, a, :]),
                                                    red[:, a, 0, :].unsqueeze(2).broadcast_to([P, HEADS, HD]),
                                                    ALU.subtract).then_inc(S["q_sub"], 1)

                        def q_second(a):
                            dve.wait_ge(S["q_exp"], n * BLK + a + 1)
                            q_link(nc.vector.reduce_sum(red[:, a, 1, :], by_head(qs[:, a, :]), AX.X))
                            q_link(nc.vector.reciprocal(red[:, a, 2, :], red[:, a, 1, :]))
                            nc.vector.tensor_tensor(by_head(qn[:, a, :]), by_head(qs[:, a, :]),
                                                    red[:, a, 2, :].unsqueeze(2).broadcast_to([P, HEADS, HD]),
                                                    ALU.mult).then_inc(S["qn_done"], 1)

                        def q_turned():
                            dve.wait_ge(S["xt_st"][u], it * 16)
                            for a in range(BLK):
                                dve.wait_ge(S["tr_done"], n * 12 + 4 + a + 1)
                                nc.vector.tensor_copy(qT[:, u, :, a * P:(a + 1) * P],
                                                      tr[:, a % 2, :].rearrange("p (k t) -> p k t", k=K)).then_inc(S["tr_free"], 1)

                        dve.wait_ge(S["qn_done"], n * BLK)
                        q_first(0)
                        for a in range(1, BLK):
                            q_first(a)
                            q_second(a - 1)
                        q_second(BLK - 1)
                        dve.wait_ge(S["p_done"], n * K)
                        low_half(0)
                        low_half(1)
                        high_half(0)
                        low_half(2)
                        high_half(1)
                        low_half(3)
                        high_half(2)
                        high_half(3)
                        dve.wait_ge(S["bmax_done"], n * K + K)
                        nc.vector.tensor_tensor(top[:, 1 - u, :], top[:, u, :], bmax[:, :], ALU.max).then_inc(S["tmax"], 1)
                        dve.wait_ge(S["tmax"], n + 1)
                        nc.vector.tensor_tensor(dtop[:, :], top[:, u, :], top[:, 1 - u, :], ALU.subtract)
                        nc.vector.tensor_scalar(ntop[:, :], top[:, 1 - u, :], -1.0, None, ALU.mult).then_inc(S["top_done"], 1)
                        prep(n + 1, 1 - u, (it + 1 + u) * 16, n * 12 + 8, q_turned)
                        dve.wait_ge(S["corr_done"], n + 1)
                        dve.wait_ge(S["p_done"], n * K + K)
                        dve.wait_ge(S["ks"], n * 2)
                        nc.vector.tensor_tensor(T.ksum[:, :], T.ksum[:, :], corr[:, :], ALU.mult).then_inc(S["ks"], 1)
                        dve.wait_ge(S["ks"], n * 2 + 1)
                        nc.vector.tensor_tensor(T.ksum[:, :], T.ksum[:, :], bsum[:, :], ALU.add).then_inc(S["ks"], 1)
                        dve.wait_ge(S["ctx_done"], n)
                        for a in range(BLK):
                            dve.wait_ge(S["tr_done"], n * 12 + 12 + a + 1)
                            nc.vector.tensor_copy(probT[:, a, :], tr[:, a % 2, :]).then_inc(S["tr_free"], 1)
                        dve.wait_ge(S["ctx_done"], n + 1)
                        for j in range(K):
                            ins = nc.vector.scalar_tensor_tensor(out=T.ctx[:, j, :], in0=T.ctx[:, j, :], scalar=corr[:, j:j + 1],
                                                                 in1=cps[:, j * P:(j + 1) * P], op0=ALU.mult, op1=ALU.add)
                        ins.then_inc(S["ctx_free"], 1)
                        dve.wait_ge(S["ctx_free"], n + 1)

            @block.tensor
            def _(pe):
                def transposes(m, q0):
                    pe.wait_ge(S["xn_done"], m * BLK + BLK)
                    for k in range(K):
                        if q0 is not None:
                            pe.wait_ge(S["tr_free"], q0 + k - 1)
                        elif k >= 2:
                            pe.wait_ge(S["tr_free"], k - 1)
                        for a in range(BLK):
                            ins = nc.tensor.transpose(tr[:, k % 2, a * P:(a + 1) * P], xn[:, a, k * P:(k + 1) * P], T.ident[:, :])
                        ins.then_inc(S["tr_done"], 1)

                transposes(0, None)
                pe.wait_ge(S["kw"], 64)
                for it in turns(pe, BLOCKS // 2):
                    for u in range(2):
                        n = it * 2 + u
                        pe.wait_ge(S["tr_free"], n * 12 + 4)
                        for a in range(BLK):
                            pe.wait_ge(S["act_free"], n * 8 + 4 + a + 1)
                            for k in range(K):
                                ins = nc.tensor.matmul(mm[:, a, :], xnT[:, u, k, a * P:(a + 1) * P], w_q[:, k, :],
                                                       start=(k == 0), stop=(k == K - 1))
                            ins.then_inc(S["q_done"], 1)
                        for j in range(K):
                            pe.wait_ge(S["q_sub"], n * BLK + j + 1)
                            for k in range(K):
                                ins = nc.tensor.matmul(mm[:, j, :], w_k[:, k, j * P:(j + 1) * P], xnT[:, u, k, :],
                                                       start=(k == 0), stop=(k == K - 1))
                            ins.then_inc(S["k_done"], 1)
                        for a in range(BLK):
                            pe.wait_ge(S["kf_done"], n * K + a + 1)
                            for k in range(K):
                                ins = nc.tensor.matmul(mm[:, a, :], xnT[:, u, k, a * P:(a + 1) * P], w_v[:, k, :],
                                                       start=(k == 0), stop=(k == K - 1))
                            ins.then_inc(S["vh_done"], 1)
                        for a in range(BLK):
                            pe.wait_ge(S["qn_done"], n * BLK + a + 1)
                            pe.wait_ge(S["tr_free"], n * 12 + 4 + a - 1)
                            for k in range(K):
                                ins = nc.tensor.transpose(tr[:, a % 2, k * P:(k + 1) * P], qn[:, a, k * P:(k + 1) * P], T.ident[:, :])
                            ins.then_inc(S["tr_done"], 1)
                        transposes(n + 1, n * 12 + 8)
                        for a in range(BLK):
                            pe.wait_ge(S["act_free"], n * 8 + 8 + a + 1)
                            for k in range(K):
                                ins = nc.tensor.matmul(mm[:, a, :], xnT[:, u, k, a * P:(a + 1) * P], w_g[:, k, :],
                                                       start=(k == 0), stop=(k == K - 1))
                            ins.then_inc(S["vh_done"], 1)
                        pe.wait_ge(S["p_done"], n * K + K)
                        for a in range(BLK):
                            pe.wait_ge(S["tr_free"], n * 12 + 12 + a - 1)
                            for j in range(K):
                                ins = nc.tensor.transpose(tr[:, a % 2, j * P:(j + 1) * P], prob[:, j, a * P:(a + 1) * P], T.ident[:, :])
                            ins.then_inc(S["tr_done"], 1)
                        pe.wait_ge(S["tr_free"], n * 12 + 16)
                        pe.wait_ge(S["ctx_free"], n)
                        for j in range(K):
                            for a in range(BLK):
                                ins = nc.tensor.matmul(cps[:, j * P:(j + 1) * P], probT[:, a, j * P:(j + 1) * P],
                                                       v_sb[:, a, j * P:(j + 1) * P], start=(a == 0), stop=(a == BLK - 1))
                        ins.then_inc(S["ctx_done"], 1)


def context_stage(nc, A, T, S):
    ctx = ExitStack()
    sb = lambda name, shape, dt=F32: ctx.enter_context(nc.sbuf_tensor(name, shape, dt))
    with ctx:
        w_p = sb("w_p", [P, K, D])
        inv = sb("inv", [P, K])
        ctxT = sb("ctxT", [P, K, P])
        t_ps = ctx.enter_context(nc.psum_tensor("t_ps", [P, 512], F32))
        m_ps = ctx.enter_context(nc.psum_tensor("m_ps", [P, K, 512], F32))
        with nc.Block() as block:
            @block.sync
            def _(sp):
                sp.dma_start(w_p[:, :, :], A["w_proj"].rearrange("(k p) n -> p k n", p=P)).then_inc(S["c_load"], 16)

            @block.vector
            def _(dve):
                nc.vector.memset(ctxT[:, :, :], 0.0).then_inc(S["c_dve"], 1)
                nc.vector.reciprocal(inv[:, :], T.ksum[:, :]).then_inc(S["c_dve"], 1)
                dve.wait_ge(S["c_dve"], 2)
                for j in range(K):
                    nc.vector.tensor_scalar(T.ctx[:, j, :], T.ctx[:, j, :], inv[:, j:j + 1], None, ALU.mult).then_inc(S["c_dve"], 1)
                dve.wait_ge(S["c_tr"], 1)
                for j in range(K):
                    for h in range(2):
                        s = slice(h * HD, (h + 1) * HD)
                        nc.vector.tensor_copy(ctxT[s, j, s], t_ps[s, j * P + h * HD:j * P + (h + 1) * HD]).then_inc(S["c_dve"], 1)
                for j in range(K):
                    dve.wait_ge(S["c_mm"], j + 1)
                    nc.vector.tensor_copy(T.mix[:, j, :], m_ps[:, j, :]).then_inc(S["c_dve"], 1)

            @block.tensor
            def _(pe):
                pe.wait_ge(S["c_dve"], 2 + K)
                for j in range(K):
                    ins = nc.tensor.transpose(t_ps[:, j * P:(j + 1) * P], T.ctx[:, j, :], T.ident[:, :])
                ins.then_inc(S["c_tr"], 1)
                pe.wait_ge(S["c_load"], 16)
                pe.wait_ge(S["c_dve"], 2 + 3 * K)
                for j in range(K):
                    nc.tensor.matmul(m_ps[:, j, :], ctxT[:, j, :], w_p[:, j, :], start=True, stop=True).then_inc(S["c_mm"], 1)


def nodes_stage(nc, A, T, S):
    ctx = ExitStack()
    sb = lambda name, shape, dt=F32: ctx.enter_context(nc.sbuf_tensor(name, shape, dt))
    pb = lambda name, shape: ctx.enter_context(nc.psum_tensor(name, shape, F32))
    with ctx:
        qT = sb("qT_sb", [P, 2, K, P])
        att = sb("att", [P, D])
        bias = sb("bias", [P, D])
        idx = sb("idx", [P, 2, CHUNKS], I32)
        dw = sb("dw", [P, 2, 2 * CHUNKS])
        rows = sb("rows", [P, GATHERS, D])
        onehot = sb("onehot", [P, BANKS, 2, P])
        sums = pb("sums", [P, BANKS, 512])
        o_ps = pb("o_ps", [P, 512])
        y = T.y
        x3 = A["x"].rearrange("(t p) d -> p t d", p=P)
        PIECES = 8
        W = TILES // PIECES
        qt = A["qT"].rearrange("b p (k a t) -> b a p k t", k=K, a=BLK)
        AHEAD = ARING - 1
        ATT = (4, 11)
        PER = STEPS + 2

        def bank(s):
            return s % ARING if s < STEPS - 1 else ARING

        def later(s):
            return sum(a < s for a in ATT)

        with nc.Block() as block:
            @block.sync
            def _(sp):
                def load_qt(blk, a):
                    sp.dma_start(qT[:, a % 2, :, :], qt[blk, a, :, :, :].rearrange("o p k t -> p (o k) t")).then_inc(S["n_xt"][a % 2], 16)

                load_qt(slice(0, 1), 0)
                sp.dma_start(bias[:, :], A["b_proj"].rearrange("(o d) -> o d", o=1).broadcast_to([P, D])).then_inc(S["n_bias"], 16)
                for c in range(0, PIECES, 2):
                    sp.dma_start(y[:, c * W:(c + 1) * W, :], x3[:, c * W:(c + 1) * W, :]).then_inc(S["n_x"], 16)
                for it in turns(sp, TILES // BLK):
                    for a in range(BLK):
                        sp.wait_ge(S["o_done"], it * BLK + a)
                        if a + 1 < BLK:
                            load_qt(bass.ds(it, 1), a + 1)
                        else:
                            load_qt(bass.ds((it + 1) % BLOCKS, 1), 0)
                sp.wait_ge(S["n_xt"][0], 16 * (TILES // 2 + 1))

            @block.scalar
            def _(act):
                for c in range(1, PIECES, 2):
                    act.dma_start(y[:, c * W:(c + 1) * W, :], x3[:, c * W:(c + 1) * W, :]).then_inc(S["n_x"], 16)

            @block.gpsimd
            def _(pool):
                for it in turns(pool, PAIRS // 2):
                    for u in range(2):
                        n = it * 2 + u
                        nc.gpsimd.tensor_copy(idx[:, u, :], T.src_t[:, bass.ds(n * CHUNKS, CHUNKS)]).then_inc(S["n_idx"], 1)
                        wait_apart(pool, S["pool_passed"], S["n_idx"], n + 1)
                        for c in range(CHUNKS):
                            slot = c % GRING if c < CHUNKS - 2 else GRING + c % 2
                            if c % 2 == 0 and c < CHUNKS - 2:
                                back = (c + 1 - GRING) // 2 if c + 1 >= GRING else c // 2 - GRING // 2 - 1
                                wait_apart(pool, S["pool_passed"], S["agg_done"], n * STEPS + back + 1 + ARING)
                            pool.indirect_dma_start(out=rows[:, slot, :], out_offset=None, in_=A["h"][:, :],
                                                    in_offset=bass.IndirectOffsetOnAxis(ap=idx[:, u, c:c + 1], axis=0)
                                                    ).then_inc(S["gath"][slot], 16)

            @block.vector
            def _(dve):
                def table(m, slot):
                    nc.vector.tensor_copy(dw[:, slot, :], T.dst_w[:, bass.ds(m * 2 * CHUNKS, 2 * CHUNKS)]).then_inc(S["n_dw"], 1)

                def build(n, slot, s):
                    count = n * STEPS + s + (1 if s >= ARING else 0)
                    if not (isinstance(count, int) and count == 0):
                        dve.wait_ge(S["agg_done"], count)
                    for h in range(2):
                        c = 2 * s + h
                        ins = nc.vector.tensor_scalar(onehot[:, bank(s), h, :], T.iota_f[:, :], dw[:, slot, c:c + 1],
                                                      dw[:, slot, CHUNKS + c:CHUNKS + c + 1], ALU.is_equal, ALU.mult)
                    ins.then_inc(S["hot"], 1)

                table(0, 0)
                dve.wait_ge(S["n_dw"], 1)
                for s in range(AHEAD):
                    build(0, 0, s)
                dve.wait_ge(S["n_bias"], 16)
                dve.wait_ge(S["n_x"], 16 * PIECES)
                for it in turns(dve, PAIRS // 2):
                    for u in range(2):
                        n = it * 2 + u

                        def add(s):
                            t = dve.value_load(T.tile_of[0:1, bass.ds(n * STEPS + s, 1)], min_val=0, max_val=TILES - 1)
                            dve.wait_ge(S["agg_done"], n * STEPS + s + 1 + ARING)
                            dve.wait_ge(S["n_y"], n * PER + s + later(s))
                            nc.vector.tensor_tensor(y[:, t, :], y[:, t, :], sums[:, bank(s), :], ALU.add).then_inc(S["n_y"], 1)

                        table((n + 1) % PAIRS, 1 - u)
                        for s in range(STEPS):
                            if s + AHEAD < STEPS:
                                build(n, u, s + AHEAD)
                            else:
                                if s + AHEAD == STEPS:
                                    dve.wait_ge(S["n_dw"], n + 2)
                                build(n + 1, 1 - u, s + AHEAD - STEPS)
                            add(s)
                            if s in ATT:
                                i = ATT.index(s)
                                dve.wait_ge(S["o_done"], n * 2 + i + 1)
                                nc.vector.tensor_tensor(att[:, :], bias[:, :], o_ps[:, :], ALU.add).then_inc(S["o_sb"], 1)
                                dve.wait_ge(S["o_sb"], n * 2 + i + 1)
                                dve.wait_ge(S["n_y"], n * PER + s + 1 + i)
                                yn = y[:, bass.ds(n * 2 + i, 1), :].rearrange("p o d -> p (o d)")
                                nc.vector.tensor_tensor(yn, yn, att[:, :], ALU.add).then_inc(S["n_y"], 1)

            @block.tensor
            def _(pe):
                pe.sem_inc(S["agg_done"], ARING)
                for it in turns(pe, PAIRS // 2):
                    for u in range(2):
                        n = it * 2 + u
                        for s in range(STEPS):
                            if s in ATT:
                                i = ATT.index(s)
                                pe.wait_ge(S["n_xt"][i], n * 16 + 16)
                                pe.wait_ge(S["o_sb"], n * 2 + i)
                                for k in range(K):
                                    ins = nc.tensor.matmul(o_ps[:, :], qT[:, i, k, :], T.mix[:, k, :], start=(k == 0), stop=(k == K - 1))
                                ins.then_inc(S["o_done"], 1)
                            back = s - ARING
                            if 0 <= back and s < STEPS - 1:
                                pe.wait_ge(S["n_y"], n * PER + back + 1 + later(back))
                            elif not (isinstance(n, int) and n == 0):
                                pe.wait_ge(S["n_y"], n * PER + (back if s < ARING else 0))
                            pe.wait_ge(S["hot"], n * STEPS + s + 1)
                            for h in range(2):
                                c = 2 * s + h
                                slot = c % GRING if c < CHUNKS - 2 else GRING + h
                                use = (n * ((CHUNKS - 2) // GRING) + c // GRING if c < CHUNKS - 2 else n) + 1
                                pe.wait_ge(S["gath"][slot], use * 16)
                                ins = nc.tensor.matmul(sums[:, bank(s), :], onehot[:, bank(s), h, :], rows[:, slot, :],
                                                       start=(h == 0), stop=(h == 1))
                            ins.then_inc(S["agg_done"], 1)


def shared_stage(nc, A, T, S):
    ctx = ExitStack()
    sb = lambda name, shape, dt=F32: ctx.enter_context(nc.sbuf_tensor(name, shape, dt))
    pb = lambda name, shape: ctx.enter_context(nc.psum_tensor(name, shape, F32))
    with ctx:
        yn = T.dst_w[:, 0:BLK * D].rearrange("p (a d) -> p a d", a=BLK)
        w1 = T.w_1[:, :, :].rearrange("p k d -> p (k d)").rearrange("p (e k f) -> p e k f", e=SHARED, k=K)
        w2 = T.mix[:, :, :].rearrange("p k d -> p (k d)").rearrange("p (e c d) -> p e c d", e=SHARED, c=FC)
        tT = sb("tT", [P, 2, K, BLK * P])
        hT = sb("hT", [P, SHARED, FC, BLK * P])
        b1 = sb("b1", [P, SHARED, FC])
        gw = sb("gw", [P, K, ROUTED])
        gb = sb("gb", [P, ROUTED])
        stat = sb("stat2", [P, BLK, 6])
        mv = sb("mv2", [P, BLK, 2])
        rstd = sb("rstd2", [P, BLK])
        half = sb("half2", [P, BLK])
        logit = sb("logit", [P, BLK, ROUTED])
        pr = sb("pr", [P, BLK, ROUTED])
        mx = sb("mx", [P, BLK])
        ssum = sb("ssum", [P, BLK])
        best = sb("best", [P, BLK, 8])
        where = sb("where", [P, BLK, 8], U32)
        where_f = sb("where_f", [P, BLK, 8])
        up = pb("up", [P, 2, 512])
        down = pb("down", [P, 3, 512])
        tr = pb("tr2", [P, 2, 512])
        gp = pb("gp", [P, 512])
        y = T.y
        y3 = A["y1"].rearrange("(t p) d -> p t d", p=P)
        n3 = A["yn"].rearrange("(t p) d -> p t d", p=P)
        LINKS = 8

        with nc.Block() as block:
            @block.sync
            def _(sp):
                sp.dma_start(w1[:, :, :, :], A["w1"][0:SHARED].rearrange("e p k f -> p e k f")).then_inc(S["x_par"], 16)
                sp.dma_start(w2[:, :, :, :], A["w2"][0:SHARED].rearrange("e p c d -> p e c d")).then_inc(S["x_par"], 16)
                sp.dma_start(b1[:, :, :], A["b1"][:, 0:SHARED, :]).then_inc(S["x_par"], 16)
                sp.dma_start(gw[:, :, :], A["gate_wT"].rearrange("(k p) e -> p k e", p=P)).then_inc(S["x_par"], 16)
                sp.dma_start(gb[:, :], A["gate_b"].rearrange("(o d) -> o d", o=1).broadcast_to([P, ROUTED])).then_inc(S["x_par"], 16)

                def store_rows(m):
                    for a in range(BLK):
                        sp.wait_ge(S["yn"], m * BLK + a + 1)
                        sp.dma_start(n3[:, bass.ds(m * BLK + a, 1), :], yn[:, a:a + 1, :]).then_inc(S["yn_st"][a], 16)

                store_rows(0)
                for it, last in turns_and_last(sp, BLOCKS // 2):
                    for u in range(2):
                        n = it * 2 + u
                        if not (last and u == 1):
                            store_rows(n + 1)
                        sp.wait_ge(S["y_done"], n * BLK + BLK)
                        sp.dma_start(y3[:, bass.ds(n * BLK, BLK), :], y[:, bass.ds(n * BLK, BLK), :]).then_inc(S["x_out"], 16)
                sp.wait_ge(S["x_out"], 16 * BLOCKS)
                for a in range(BLK):
                    sp.wait_ge(S["yn_st"][a], 16 * BLOCKS)

            @block.gpsimd
            def _(pool):
                nc.gpsimd.memset(half[:, :], -0.5).then_inc(S["half2"], 1)
                pool.wait_ge(S["half2"], 1)
                with pool.Fori(0, BLOCKS) as n:
                    pool.wait_ge(S["var2"], n + 1)
                    nc.gpsimd.tensor_tensor(rstd[:, :], mv[:, :, 1], half[:, :], ALU.pow).then_inc(S["rstd2"], 1)

            @block.scalar
            def _(act):
                act.wait_ge(S["x_par"], 16 * 5)
                for n in turns(act, BLOCKS):
                    act.wait_ge(S["nm"], n + 1)
                    nc.scalar.activation(pr[:, :, :], logit[:, :, :], ACT.Exp).then_inc(S["pr"], 1)
                    act.wait_ge(S["down_done"], n * BLK)
                    for e in range(SHARED):
                        for c in range(FC):
                            act.wait_ge(S["up_done"], n * (SHARED * FC) + e * FC + c + 1)
                            nc.scalar.activation(hT[:, e, c, :], up[:, c, :], ACT.Gelu, bias=b1[:, e, c:c + 1]).then_inc(S["hT"], 1)

            @block.vector
            def _(dve):
                def tile(t):
                    return y[:, bass.ds(t, 1), :].rearrange("p o d -> p (o d)")

                def stats(m):
                    norm_tiles(nc, dve, lambda a: tile(m * BLK + a), stat, mv, m * 2 * BLK, S["bn2"], S["dve_passed"])
                    nc.vector.tensor_scalar(mv[:, :, 1], mv[:, :, 1], EPS, None, ALU.add).then_inc(S["var2"], 1)
                    dve.wait_ge(S["rstd2"], m + 1)

                def norm(m, a):
                    dve.wait_ge(S["yn_st"][a], m * 16)
                    dve.wait_ge(S["tr2_done"], m * BLK + a - 3 if not isinstance(m, int) or m else 0)
                    nc.vector.tensor_scalar(yn[:, a, :], tile(m * BLK + a), mv[:, a, 0:1], rstd[:, a:a + 1],
                                            ALU.subtract, ALU.mult).then_inc(S["yn"], 1)

                def turned(m, slot, a):
                    dve.wait_ge(S["tr2_done"], m * BLK + a + 1)
                    nc.vector.tensor_copy(tT[:, slot, :, a * P:(a + 1) * P],
                                          tr[:, a % 2, :].rearrange("p (k t) -> p k t", k=K)).then_inc(S["tT"], 1)

                def route(m):
                    count = [0]

                    def link(ins):
                        count[0] += 1
                        ins.then_inc(S["r_dve"], 1)
                        wait_apart(dve, S["dve_passed"], S["r_dve"], m * LINKS + count[0])

                    def wide(t):
                        return t.broadcast_to([P, BLK, ROUTED])

                    dve.wait_ge(S["logit"], m + 1)
                    link(nc.vector.tensor_tensor(logit[:, :, :], gp[:, 0:BLK * ROUTED].rearrange("p (a e) -> p a e", e=ROUTED),
                                                 wide(gb[:, :].unsqueeze(1)), ALU.add))
                    link(nc.vector.reduce_max(mx[:, :], logit[:, :, :], AX.X))
                    nc.vector.tensor_tensor(logit[:, :, :], logit[:, :, :], wide(mx[:, :].unsqueeze(2)), ALU.subtract).then_inc(S["nm"], 1)
                    dve.wait_ge(S["pr"], m + 1)
                    link(nc.vector.reduce_sum(mx[:, :], pr[:, :, :], AX.X))
                    link(nc.vector.reciprocal(ssum[:, :], mx[:, :]))
                    link(nc.vector.tensor_tensor(pr[:, :, :], pr[:, :, :], wide(ssum[:, :].unsqueeze(2)), ALU.mult))
                    for a in range(BLK):
                        ins = nc.vector.max(best[:, a, :], pr[:, a, :])
                    link(ins)
                    for a in range(BLK):
                        ins = nc.vector.max_index(where[:, a, :], best[:, a, :], pr[:, a, :])
                    link(ins)
                    link(nc.vector.tensor_copy(where_f[:, :, :], where[:, :, :]))
                    nc.vector.tensor_copy(T.expert[:, bass.ds(m * BLK, BLK), :], where_f[:, :, 0:2])
                    nc.vector.tensor_copy(T.prob[:, bass.ds(m * BLK, BLK), :], best[:, :, 0:2])
                    assert count[0] == LINKS

                dve.wait_ge(S["x_par"], 16 * 5)
                stats(0)
                for a in range(BLK):
                    norm(0, a)
                    turned(0, 0, a)
                for it, last in turns_and_last(dve, BLOCKS // 2):
                    for u in range(2):
                        n = it * 2 + u
                        more = not (last and u == 1)
                        route(n)
                        if more:
                            stats(n + 1)
                            norm(n + 1, 0)
                            norm(n + 1, 1)
                        for a in range(BLK):
                            if more:
                                turned(n + 1, 1 - u, a)
                                if a + 2 < BLK:
                                    norm(n + 1, a + 2)
                            dve.wait_ge(S["down_done"], n * BLK + a + 1)
                            nc.vector.tensor_tensor(tile(n * BLK + a), tile(n * BLK + a), down[:, a % 2, :], ALU.add).then_inc(S["y_done"], 1)

            @block.tensor
            def _(pe):
                def turn(m, a):
                    pe.wait_ge(S["yn"], m * BLK + a + 1)
                    if not (isinstance(m, int) and m == 0 and a < 2):
                        pe.wait_ge(S["tT"], m * BLK + a - 1)
                    for k in range(K):
                        ins = nc.tensor.transpose(tr[:, a % 2, k * P:(k + 1) * P], yn[:, a, k * P:(k + 1) * P], T.ident[:, :])
                    ins.then_inc(S["tr2_done"], 1)

                def logits(m, slot):
                    pe.wait_ge(S["tT"], m * BLK + BLK)
                    pe.wait_ge(S["nm"], m)
                    for a in range(BLK):
                        for k in range(K):
                            ins = nc.tensor.matmul(gp[:, a * ROUTED:(a + 1) * ROUTED], tT[:, slot, k, a * P:(a + 1) * P], gw[:, k, :],
                                                   start=(k == 0), stop=(k == K - 1))
                    ins.then_inc(S["logit"], 1)

                pe.wait_ge(S["x_par"], 16 * 5)
                for a in range(BLK):
                    turn(0, a)
                logits(0, 0)
                for it, last in turns_and_last(pe, BLOCKS // 2):
                    for u in range(2):
                        n = it * 2 + u
                        more = not (last and u == 1)
                        for e in range(SHARED):
                            for c in range(FC):
                                pe.wait_ge(S["hT"], n * (SHARED * FC) + max(e * FC + c - 1, 0))
                                for k in range(K):
                                    ins = nc.tensor.matmul(up[:, c, :], w1[:, e, k, c * P:(c + 1) * P], tT[:, u, k, :],
                                                           start=(k == 0), stop=(k == K - 1))
                                ins.then_inc(S["up_done"], 1)
                        for a in range(BLK):
                            if more:
                                turn(n + 1, a)
                            if a == 0:
                                pe.wait_ge(S["hT"], n * (SHARED * FC) + SHARED * FC)
                            pe.wait_ge(S["y_done"], n * BLK + max(a - 1, 0))
                            for e in range(SHARED):
                                for c in range(FC):
                                    ins = nc.tensor.matmul(down[:, a % 2, :], hT[:, e, c, a * P:(a + 1) * P], w2[:, e, c, :],
                                                           start=(e == 0 and c == 0), stop=(e == SHARED - 1 and c == FC - 1))
                            ins.then_inc(S["down_done"], 1)
                        if more:
                            logits(n + 1, 1 - u)


def places_stage(nc, A, T, S):
    ctx = ExitStack()
    sb = lambda name, shape, dt=F32: ctx.enter_context(nc.sbuf_tensor(name, shape, dt))
    pb = lambda name, shape: ctx.enter_context(nc.psum_tensor(name, shape, F32))
    C = 2 * TILES
    BATCH = 16
    RING = 8
    with ctx:
        hot = sb("hot_e", [P, C, ROUTED], F16)
        ones = sb("ones_p", [P, P], F16)
        before = sb("before_p", [P, P], F16)
        room = T.w_1[:, :, :].rearrange("p k d -> p (k d)")
        W = C * ROUTED
        assert 2 * W <= K * D
        col = room[:, 0:W].rearrange("p (c e) -> p c e", e=ROUTED)
        upto = room[:, W:2 * W].rearrange("p (e c) -> p e c", e=ROUTED)
        zeros = sb("zeros_p", [P, C])
        tiles_i = sb("tiles_i", [P, ROUTED], I32)
        tiles = sb("tiles", [P, ROUTED])
        cum = sb("cum_p", [P, ROUTED])
        base = sb("base_p", [P, ROUTED])
        rank = T.mix[:, :, :].rearrange("p k d -> p (k d)")[:, 0:W].rearrange("p (c e) -> p c e", e=ROUTED)
        place = sb("place_f", [P, C])
        node_i = sb("node_i", [P, C], I32)
        node = sb("node", [P, C])
        slot_i = sb("slot_i", [P, SLOT_TILES], I32)
        slot = sb("slot", [P, SLOT_TILES])
        eof = sb("eof", [1, SLOT_TILES])
        part_i = sb("part_p", [P, 2, C], I32)
        part = sb("part_f", [P, 2, C])
        batch = sb("batch_p", [P, 2, 3, BATCH])
        at_slot = sb("at_slot", [P, RING, P])
        at_tile = sb("at_tile", [P, RING, SLOT_TILES])
        ps = pb("ps_p", [P, 2, 2, 512])
        inv = pb("inv_p", [P, 512])

        with nc.Block() as block:
            @block.gpsimd
            def _(pool):
                nc.gpsimd.memset(ones[:, :], 1.0).then_inc(S["consts"], 1)
                nc.gpsimd.memset(zeros[:, :], 0.0).then_inc(S["consts"], 1)
                nc.gpsimd.memset(before[:, :], 1.0).then_inc(S["blank"], 1)
                nc.gpsimd.iota(node_i[:, :], pattern=[[P, TILES], [0, 2]], base=0, channel_multiplier=1).then_inc(S["consts"], 1)
                nc.gpsimd.iota(slot_i[:, :], pattern=[[1, SLOT_TILES]], base=0, channel_multiplier=0).then_inc(S["consts"], 1)
                pool.wait_ge(S["blank"], 5)
                nc.gpsimd.affine_select(out=before[:, :], in_=before[:, :], compare_op=ALU.is_gt, fill=0.0, base=0,
                                        pattern=[[1, P]], channel_multiplier=-1).then_inc(S["consts"], 1)
                for e in range(ROUTED):
                    for i, (full, high) in enumerate(((T.w1r, T.w1h), (T.w2r, T.w2h))):
                        pool.wait_ge(S["s_high"], 2 * e + i + 1)
                        nc.gpsimd.tensor_tensor(full[:, e, :, :], full[:, e, :, :].bitcast(F32), high[:, e, :, :].bitcast(F32),
                                                ALU.subtract).then_inc(S["s_low"], 1)

            @block.sync
            def _(sp):
                for e in range(ROUTED):
                    sp.dma_start(T.w1r[:, e, :, :].bitcast(F32), A["w1"][SHARED + e]).then_inc(S["s_w"][2 * e // ROUTED], 16)
                sp.dma_start(T.b1r[:, :, :], A["rb1"].rearrange("(o e) f -> o e f", o=1).broadcast_to([P, ROUTED, FF])).then_inc(S["s_par"], 16)
                sp.dma_start(T.b2r[:, :, :], A["rb2"].rearrange("(o e) d -> o e d", o=1).broadcast_to([P, ROUTED, D])).then_inc(S["s_par"], 16)

            @block.scalar
            def _(act):
                for e in range(ROUTED):
                    act.dma_start(T.w2r[:, e, :, :].bitcast(F32), A["w2"][SHARED + e]).then_inc(S["s_w"][2 * e // ROUTED], 16)
                for e in range(ROUTED):
                    if 2 * e % ROUTED == 0:
                        act.wait_ge(S["s_w"][2 * e // ROUTED], 16 * ROUTED)
                    nc.scalar.copy(T.w1h[:, e, :, :], T.w1r[:, e, :, :].bitcast(F32)).then_inc(S["s_high"], 1)
                    nc.scalar.copy(T.w2h[:, e, :, :], T.w2r[:, e, :, :].bitcast(F32)).then_inc(S["s_high"], 1)

            @block.vector
            def _(dve):
                def link(ins):
                    T.linked += 1
                    ins.then_inc(S["linked"], 1)
                    dve.wait_ge(S["linked"], T.linked)

                nc.vector.tensor_tensor(hot[:, :, :], T.expert[:, :, :].rearrange("p t i -> p (t i)").unsqueeze(2).broadcast_to([P, C, ROUTED]),
                                        T.iota_f[:, 0:ROUTED].unsqueeze(1).broadcast_to([P, C, ROUTED]),
                                        ALU.is_equal).then_inc(S["p_hot"], 1)
                dve.wait_ge(S["consts"], 16)
                nc.vector.tensor_copy(node[:, :], node_i[:, :])
                nc.vector.tensor_copy(slot[:, :], slot_i[:, :])
                dve.wait_ge(S["p_mm"], 1)
                link(nc.vector.tensor_copy(col[:, :, :].rearrange("p c e -> p (c e)"), ps[:, 0, :, :].rearrange("p b w -> p (b w)")))
                for e in range(ROUTED):
                    ins = nc.vector.tensor_tensor_scan(upto[:, e, :], col[:, :, e], zeros[:, :], 0.0, ALU.add, ALU.add)
                link(ins)
                link(nc.vector.tensor_scalar(tiles_i[:, :], upto[:, :, C - 1], float(P - 1), None, ALU.add))
                link(nc.vector.tensor_scalar(tiles_i[:, :], tiles_i[:, :], 7, None, ALU.arith_shift_right))
                link(nc.vector.tensor_copy(tiles[:, :], tiles_i[:, :]))
                link(nc.vector.tensor_tensor_scan(cum[:, :], tiles[:, :], zeros[:, 0:ROUTED], 0.0, ALU.add, ALU.add))
                link(nc.vector.tensor_tensor(base[:, :], cum[:, :], tiles[:, :], ALU.subtract))
                link(nc.vector.tensor_scalar(base[:, :], base[:, :], float(P), None, ALU.mult))
                link(nc.vector.tensor_tensor(rank[:, :, :], upto[:, :, :].rearrange("p e c -> p c e"), col[:, :, :], ALU.subtract))
                link(nc.vector.tensor_tensor(rank[:, :, :], rank[:, :, :], base[:, :].unsqueeze(1).broadcast_to([P, C, ROUTED]), ALU.add))
                link(nc.vector.tensor_tensor(rank[:, :, :].rearrange("p c e -> p (c e)"), rank[:, :, :].rearrange("p c e -> p (c e)"),
                                             ps[:, 1, :, :].rearrange("p b w -> p (b w)"), ALU.add))
                link(nc.vector.tensor_tensor(rank[:, :, :], rank[:, :, :], hot[:, :, :], ALU.mult))
                link(nc.vector.reduce_sum(place[:, :], rank[:, :, :], AX.X))
                link(nc.vector.tensor_copy(T.spot[:, :], place[:, :]))
                nc.vector.tensor_scalar(part_i[:, 0, :], T.spot[:, :], P - 1, None, ALU.bitwise_and)
                link(nc.vector.tensor_scalar(part_i[:, 1, :], T.spot[:, :], 7, None, ALU.arith_shift_right))
                link(nc.vector.tensor_copy(part[:, :, :], part_i[:, :, :]))
                link(nc.vector.tensor_scalar(eof[:, :], slot[0:1, :], cum[0:1, 0:1], None, ALU.is_ge))
                for e in range(1, ROUTED - 1):
                    link(nc.vector.scalar_tensor_tensor(out=eof[:, :], in0=slot[0:1, :], scalar=cum[0:1, e:e + 1], in1=eof[:, :],
                                                        op0=ALU.is_ge, op1=ALU.add))
                nc.vector.tensor_copy(T.expert_of[:, :], eof[:, :])
                for it in turns(dve, C // (2 * BATCH)):
                    for u in range(2):
                        n = it * 2 + u
                        dve.wait_ge(S["p_inv"], it * (2 * BATCH) - BATCH + u * BATCH if not isinstance(it, int) else 0)
                        nc.vector.tensor_copy(batch[:, u, 0:2, :], part[:, :, bass.ds(n * BATCH, BATCH)])
                        nc.vector.tensor_copy(batch[:, u, 2, :], node[:, bass.ds(n * BATCH, BATCH)]).then_inc(S["p_ring"], 1)
                        dve.wait_ge(S["p_ring"], n + 1)
                        for c in range(BATCH):
                            if not (isinstance(n, int) and n * BATCH + c < RING):
                                dve.wait_ge(S["p_inv"], n * BATCH + c - RING + 1)
                            nc.vector.tensor_scalar(at_slot[:, c % RING, :], T.iota_f[:, :], batch[:, u, 0, c:c + 1], 1.0,
                                                    ALU.is_equal, ALU.mult)
                            nc.vector.tensor_scalar(at_tile[:, c % RING, :], slot[:, :], batch[:, u, 1, c:c + 1],
                                                    batch[:, u, 2, c:c + 1], ALU.is_equal, ALU.mult).then_inc(S["p_built"], 1)
                dve.wait_ge(S["p_inv"], C)
                nc.vector.tensor_copy(T.ids[:, :], inv[:, 0:SLOT_TILES])

            @block.tensor
            def _(pe):
                pe.wait_ge(S["consts"], 16)
                pe.wait_ge(S["p_hot"], 1)
                flat = hot[:, :, :].rearrange("p c e -> p (c e)")
                for i, lhs in enumerate((ones, before)):
                    for h in range(2):
                        ins = nc.tensor.matmul(ps[:, i, h, :], lhs[:, :], flat[:, h * 512:(h + 1) * 512], start=True, stop=True)
                ins.then_inc(S["p_mm"], 1)
                for it, last in turns_and_last(pe, C // BATCH):
                    for c in range(BATCH):
                        pe.wait_ge(S["p_built"], it * BATCH + c + 1)
                        nc.tensor.matmul(inv[:, 0:SLOT_TILES], at_slot[:, c % RING, :], at_tile[:, c % RING, :],
                                         start=(isinstance(it, int) and it == 0 and c == 0),
                                         stop=(last and c == BATCH - 1)).then_inc(S["p_inv"], 1)


def routed_stage(nc, A, T, S):
    ctx = ExitStack()
    sb = lambda name, shape, dt=F32: ctx.enter_context(nc.sbuf_tensor(name, shape, dt))
    pb = lambda name, shape: ctx.enter_context(nc.psum_tensor(name, shape, F32))
    with ctx:
        w1, w2, b1, b2 = (T.w1h, T.w1r), (T.w2h, T.w2r), T.b1r, T.b2r
        idx = sb("idx_r", [P, 4], I32)
        pre = sb("pre", [P, 2, FF])
        act_h = sb("act_h", [P, 2, FF])
        rT = sb("rT", [P, 2, 2, K, P], F32R)
        hT = sb("hT_r", [P, 2, 2, FC, P], F32R)
        rows = T.w_1
        ob = T.dst_w[:, 0:4 * D].rearrange("p (u d) -> p u d", d=D)
        tr = pb("tr_r", [P, 2, 512])
        up = pb("up_r", [P, 2, 512])
        ht = pb("ht_r", [P, 2, 512])
        down = pb("down_r", [P, 2, 512])
        o3 = A["slots"].rearrange("(j p) d -> p j d", p=P)
        LAST = SLOT_TILES - 1
        PARTS = ((0, 1), (1, 0), (0, 0))

        def four(eng):
            for it, last in turns_and_last(eng, SLOT_TILES // 4):
                for u in range(4):
                    yield it * 4 + u, it, u

        with nc.Block() as block:
            @block.sync
            def _(sp):
                for j, it, u in four(sp):
                    sp.wait_ge(S["s_ob"], j + 1)
                    sp.dma_start(o3[:, bass.ds(j, 1), :], ob[:, u:u + 1, :]).then_inc(S["s_st"][u], 16)
                for u in range(4):
                    sp.wait_ge(S["s_st"][u], 16 * (SLOT_TILES // 4))

            @block.gpsimd
            def _(pool):
                for j, it, u in four(pool):
                    pool.wait_ge(S["s_tr"], it * 4 + u - 3 if not isinstance(it, int) or it else 0)
                    nc.gpsimd.tensor_copy(idx[:, u:u + 1], T.ids[:, bass.ds(j, 1)]).then_inc(S["s_idx"], 1)
                    wait_apart(pool, S["pool_passed"], S["s_idx"], j + 1)
                    pool.indirect_dma_start(out=rows[:, u, :], out_offset=None, in_=A["yn"][:, :],
                                            in_offset=bass.IndirectOffsetOnAxis(ap=idx[:, u:u + 1], axis=0)).then_inc(S["s_rows"][u], 16)

            @block.vector
            def _(dve):
                dve.wait_ge(S["s_par"], 32)

                def rows_low(j, u):
                    dve.wait_ge(S["s_rTh"], j + 1)
                    nc.vector.tensor_tensor(rT[:, 1, u % 2, :, :].rearrange("p k t -> p (k t)"), tr[:, u % 2, :],
                                            rT[:, 0, u % 2, :, :].rearrange("p k t -> p (k t)").bitcast(F32),
                                            ALU.subtract).then_inc(S["s_rT"], 1)

                def h_low(j, u):
                    dve.wait_ge(S["s_hTh"], j + 1)
                    nc.vector.tensor_tensor(hT[:, 1, u % 2, :, :].rearrange("p c t -> p (c t)"), ht[:, u % 2, 0:FF],
                                            hT[:, 0, u % 2, :, :].rearrange("p c t -> p (c t)").bitcast(F32),
                                            ALU.subtract).then_inc(S["s_hT"], 1)

                def expert(j):
                    return dve.value_load(T.expert_of[0:1, bass.ds(j, 1)], min_val=0, max_val=ROUTED - 1)

                def bias(j, u, e):
                    dve.wait_ge(S["s_up"], j + 1)
                    dve.wait_ge(S["s_gelu"], j - 1 if not isinstance(j, int) or j > 0 else 0)
                    nc.vector.tensor_tensor(pre[:, u % 2, :], up[:, u % 2, 0:FF], b1[:, bass.ds(e, 1), :].rearrange("p o f -> p (o f)"),
                                            ALU.add).then_inc(S["s_pre"], 1)

                def sums_out(j, u, e):
                    dve.wait_ge(S["s_down"], j + 1)
                    dve.wait_ge(S["s_st"][u % 4], 16 * (j // 4) if isinstance(j, int) else st_count(j, u))
                    nc.vector.tensor_tensor(ob[:, u % 4, :], down[:, u % 2, :], b2[:, bass.ds(e, 1), :].rearrange("p o d -> p (o d)"),
                                            ALU.add).then_inc(S["s_ob"], 1)

                def st_count(j, u):
                    return (j - (u % 4)) * 4

                rows_low(0, 0)
                for j, it, u in four(dve):
                    if not (isinstance(j, int) and j == 0):
                        h_low(j - 1, u + 3)
                    if not (isinstance(j, int) and j == LAST):
                        rows_low(j + 1, u + 1)
                    if u > 0:
                        before = e
                    elif not (isinstance(j, int) and j == 0):
                        before = expert(j - 1)
                    e = expert(j)
                    bias(j, u, e)
                    if not (isinstance(j, int) and j == 0):
                        sums_out(j - 1, u + 3, before)
                h_low(LAST, 3)
                sums_out(LAST, 3, e)

            @block.scalar
            def _(act):
                def rows_high(j, u):
                    act.wait_ge(S["s_tr"], j + 1)
                    act.wait_ge(S["s_up"], j - 1 if not isinstance(j, int) or j > 0 else 0)
                    nc.scalar.copy(rT[:, 0, u % 2, :, :].rearrange("p k t -> p (k t)"), tr[:, u % 2, :]).then_inc(S["s_rTh"], 1)

                def h_high(j, u):
                    act.wait_ge(S["s_ht"], j + 1)
                    nc.scalar.copy(hT[:, 0, u % 2, :, :].rearrange("p c t -> p (c t)"), ht[:, u % 2, 0:FF]).then_inc(S["s_hTh"], 1)

                rows_high(0, 0)
                for j, it, u in four(act):
                    if not (isinstance(j, int) and j == 0):
                        h_high(j - 1, u + 3)
                    if not (isinstance(j, int) and j == LAST):
                        rows_high(j + 1, u + 1)
                    act.wait_ge(S["s_pre"], j + 1)
                    nc.scalar.activation(act_h[:, u % 2, :], pre[:, u % 2, :], ACT.Gelu).then_inc(S["s_gelu"], 1)
                h_high(LAST, 3)

            @block.tensor
            def _(pe):
                def turn(j, u):
                    pe.wait_ge(S["s_rows"][u % 4], 16 * (j // 4 + 1) if isinstance(j, int) else (j - (u % 4)) * 4 + 16)
                    pe.wait_ge(S["s_rT"], j - 1 if not isinstance(j, int) or j > 0 else 0)
                    for k in range(K):
                        ins = nc.tensor.transpose(tr[:, u % 2, k * P:(k + 1) * P], rows[:, u % 4, k * P:(k + 1) * P], T.ident[:, :])
                    ins.then_inc(S["s_tr"], 1)

                def turn_h(j, u):
                    pe.wait_ge(S["s_gelu"], j + 1)
                    pe.wait_ge(S["s_hT"], j - 1 if not isinstance(j, int) or j > 0 else 0)
                    for c in range(FC):
                        ins = nc.tensor.transpose(ht[:, u % 2, c * P:(c + 1) * P], act_h[:, u % 2, c * P:(c + 1) * P], T.ident[:, :])
                    ins.then_inc(S["s_ht"], 1)

                def expert(j):
                    return pe.value_load(T.expert_of[0:1, bass.ds(j, 1)], min_val=0, max_val=ROUTED - 1)

                def first(j, u, e):
                    pe.wait_ge(S["s_rT"], j + 1)
                    pe.wait_ge(S["s_pre"], j - 1 if not isinstance(j, int) or j > 0 else 0)
                    for i, (l, r) in enumerate(PARTS):
                        for k in range(K):
                            ins = nc.tensor.matmul(up[:, u % 2, 0:FF], rT[:, l, u % 2, k, :],
                                                   w1[r][:, bass.ds(e, 1), k, :].rearrange("p o f -> p (o f)"),
                                                   start=(i == 0 and k == 0), stop=(i == 2 and k == K - 1))
                    ins.then_inc(S["s_up"], 1)

                def second(j, u, e):
                    pe.wait_ge(S["s_hT"], j + 1)
                    pe.wait_ge(S["s_ob"], j - 1 if not isinstance(j, int) or j > 0 else 0)
                    for i, (l, r) in enumerate(PARTS):
                        for c in range(FC):
                            ins = nc.tensor.matmul(down[:, u % 2, :], hT[:, l, u % 2, c, :],
                                                   w2[r][:, bass.ds(e, 1), c, :].rearrange("p o d -> p (o d)"),
                                                   start=(i == 0 and c == 0), stop=(i == 2 and c == FC - 1))
                    ins.then_inc(S["s_down"], 1)

                pe.wait_ge(S["s_low"], 2 * ROUTED)
                turn(0, 0)
                for j, it, u in four(pe):
                    if u > 0:
                        before = e
                    elif not (isinstance(j, int) and j == 0):
                        before = expert(j - 1)
                    e = expert(j)
                    if not (isinstance(j, int) and j == 0):
                        turn_h(j - 1, u + 3)
                    if not (isinstance(j, int) and j == LAST):
                        turn(j + 1, u + 1)
                    first(j, u, e)
                    if not (isinstance(j, int) and j == 0):
                        second(j - 1, u + 3, before)
                turn_h(LAST, 3)
                second(LAST, 3, e)


def combine_stage(nc, A, T, S):
    ctx = ExitStack()
    sb = lambda name, shape, dt=F32: ctx.enter_context(nc.sbuf_tensor(name, shape, dt))
    with ctx:
        RING = 4
        GATHERED = 16 * PAIRS * ((CHUNKS - 2) // GRING)
        STORED = 16 * SLOT_TILES // 4
        idx = sb("idx_c", [P, RING, 2], I32)
        rows = sb("rows_c", [P, RING, 2, D])
        acc = sb("acc_c", [P, RING, D])
        res = sb("res_c", [P, RING, D])
        bias = sb("bias_c", [P, SHARED, D])
        y3 = A["y1"].rearrange("(t p) d -> p t d", p=P)
        out3 = A["out"].rearrange("(t p) d -> p t d", p=P)

        with nc.Block() as block:
            @block.sync
            def _(sp):
                sp.dma_start(bias[:, :, :], A["sb2"].rearrange("(o e) d -> o e d", o=1).broadcast_to([P, SHARED, D])).then_inc(S["f_par"], 16)
                for it in turns(sp, TILES // RING):
                    for u in range(RING):
                        sp.wait_ge(S["f_acc"], it * RING + u - 3 if not isinstance(it, int) or it else 0)
                        sp.dma_start(acc[:, u:u + 1, :], y3[:, bass.ds(it * RING + u, 1), :]).then_inc(S["f_ld"][u], 16)

            @block.gpsimd
            def _(pool):
                for it in turns(pool, TILES // RING):
                    for u in range(RING):
                        t = it * RING + u
                        pool.wait_ge(S["f_acc"], t - 3 if not isinstance(it, int) or it else 0)
                        nc.gpsimd.tensor_copy(idx[:, u, :], T.spot[:, bass.ds(t * 2, 2)]).then_inc(S["f_idx"], 1)
                        wait_apart(pool, S["pool_passed"], S["f_idx"], t + 1)
                        for i in range(2):
                            pool.indirect_dma_start(out=rows[:, u, i, :], out_offset=None, in_=A["slots"][:, :],
                                                    in_offset=bass.IndirectOffsetOnAxis(ap=idx[:, u, i:i + 1], axis=0)).then_inc(S["gath"][u], 16)

            @block.vector
            def _(dve):
                dve.wait_ge(S["f_par"], 16)
                for e in range(1, SHARED):
                    nc.vector.tensor_tensor(bias[:, 0, :], bias[:, 0, :], bias[:, e, :], ALU.add).then_inc(S["f_bias"], 1)
                    dve.wait_ge(S["f_bias"], e)
                for it in turns(dve, TILES // RING):
                    for u in range(RING):
                        t = it * RING + u
                        dve.wait_ge(S["f_ld"][u], it * 16 + 16)
                        nc.vector.tensor_tensor(acc[:, u, :], acc[:, u, :], bias[:, 0, :], ALU.add).then_inc(S["f_bias"], 1)
                        dve.wait_ge(S["f_bias"], t + SHARED)
                        dve.wait_ge(S["gath"][u], GATHERED + it * 32 + 32)
                        p = T.prob[:, bass.ds(t, 1), :].rearrange("p o i -> p (o i)")
                        nc.vector.scalar_tensor_tensor(out=acc[:, u, :], in0=rows[:, u, 0, :], scalar=p[:, 0:1], in1=acc[:, u, :],
                                                       op0=ALU.mult, op1=ALU.add).then_inc(S["f_half"], 1)
                        dve.wait_ge(S["f_half"], t + 1)
                        dve.wait_ge(S["s_st"][u], STORED + it * 16)
                        nc.vector.scalar_tensor_tensor(out=res[:, u, :], in0=rows[:, u, 1, :], scalar=p[:, 1:2], in1=acc[:, u, :],
                                                       op0=ALU.mult, op1=ALU.add).then_inc(S["f_acc"], 1)

            @block.scalar
            def _(act):
                for it in turns(act, TILES // RING):
                    for u in range(RING):
                        t = it * RING + u
                        act.wait_ge(S["f_acc"], t + 1)
                        act.dma_start(out3[:, bass.ds(t, 1), :], res[:, u:u + 1, :]).then_inc(S["s_st"][u], 16)
                for u in range(RING):
                    act.wait_ge(S["s_st"][u], STORED + 16 * (TILES // RING))


class Kept:
    pass


def gps_layer(nc, A):
    ctx = ExitStack()
    T, S = Kept(), {}
    T.linked = 0
    with ctx:
        for name in ("dve_passed pool_passed linked e_load consts blank "
                     "kw xn_done tr_free tr_done var rstd half act_free neg_done e_done top_done corr_done p_done "
                     "ctx_done ctx_free vh_done k_done kf_done bmax_done tmax ks bn k_init "
                     "c_load c_dve c_tr c_mm "
                     "n_bias n_x n_idx n_dw n_y hot agg_done q_done q_red q_sub q_exp qn_done  o_done o_sb "
                     "r_cnt r_cld r_part r_ast r_rank r_cps r_raw r_tr r_trfree r_hot r_tot r_start r_carry r_bound r_bfree r_rps r_place d_load d_dv1 d_dv2 d_pe d_pick d_tab d_tfree ring "
                     "x_par x_out half2 var2 rstd2 bn2 nm pr up_done hT tr2_done yn tT r_dve logit "
                     "down_done y_done "
                     "p_ring p_built p_inv p_hot p_mm "
                     "s_par s_ob s_tr s_idx s_rT s_up s_gelu s_pre s_down s_ht s_hT f_acc f_idx f_half f_par f_bias s_high s_low s_rTh s_hTh").split():
            S[name] = ctx.enter_context(nc.semaphore(name))
        for name, n in (("x_ld", 2), ("r_cst", 2), ("r_ald", 2), ("scat", 2), ("yn_st", BLK),
                        ("s_st", 4), ("s_w", 2), ("s_rows", 4), ("f_ld", 4), ("xt_st", 2), ("h_st", 2), ("n_xt", 2), ("gath", GATHERS)):
            S[name] = [ctx.enter_context(nc.semaphore(f"{name}{i}")) for i in range(n)]
        sb = lambda name, shape, dt=F32: ctx.enter_context(nc.sbuf_tensor(name, shape, dt))
        T.ident = sb("ident", [P, P])
        T.iota_i = sb("iota_i", [P, P], I32)
        T.iota_f = sb("iota_f", [P, P])
        T.bounds = sb("bounds", [TILES, 2])
        T.ctx = sb("ctx", [P, K, P])
        T.ksum = sb("ksum", [P, K])
        with nc.sbuf_tensor("rec", [P, ROWS, 3], F32) as T.rec, nc.sbuf_tensor("place_i", [P, ROWS], I32) as T.place:
            ranks_stage(nc, A, T, S)
            keys_stage(nc, A, T, S)
        T.src_t = sb("src_t", [P, COLS], I32)
        T.dst_w = sb("dst_w", [P, 2 * COLS])
        T.tile_of = sb("tile_of", [1, ALL_STEPS], I32)
        T.w_1 = sb("w_1", [P, K, D])
        T.mix = sb("mix", [P, K, D])
        edges_stage(nc, A, T, S)
        context_stage(nc, A, T, S)
        T.expert = sb("expert", [P, TILES, 2])
        T.prob = sb("prob2", [P, TILES, 2])
        with nc.sbuf_tensor("y", [P, TILES, D], F32) as T.y:
            nodes_stage(nc, A, T, S)
            shared_stage(nc, A, T, S)
        T.spot = sb("spot", [P, 2 * TILES], I32)
        T.expert_of = sb("expert_of", [1, SLOT_TILES], I32)
        T.ids = sb("ids", [P, SLOT_TILES], I32)
        with ExitStack() as weights:
            wb = lambda name, shape, dt=F32: weights.enter_context(nc.sbuf_tensor(name, shape, dt))
            T.w1r = wb("w1r", [P, ROUTED, K, FF], F32R)
            T.w2r = wb("w2r", [P, ROUTED, FC, D], F32R)
            T.w1h = wb("w1h", [P, ROUTED, K, FF], F32R)
            T.w2h = wb("w2h", [P, ROUTED, FC, D], F32R)
            T.b1r = wb("b1r", [P, ROUTED, FF])
            T.b2r = wb("b2r", [P, ROUTED, D])
            places_stage(nc, A, T, S)
            routed_stage(nc, A, T, S)
        combine_stage(nc, A, T, S)


def kernel(**inputs):
    import concourse.bacc as _bacc
    import numpy as _np
    from concourse import mybir as _mybir
    from concourse.bass_utils import run_bass_kernel_spmd as _run

    g = {k: _np.asarray(v) for k, v in inputs.items()}
    w1 = _np.concatenate([g["L0_ffn_sw1"], g["L0_ffn_rw1"]])
    w2 = _np.concatenate([g["L0_ffn_sw2"], g["L0_ffn_rw2"]])
    b1 = _np.concatenate([g["L0_ffn_sb1"], g["L0_ffn_rb1"]])
    arrays = {
        "x": g["x"], "src": g["src"], "dst": g["dst"], "edge_weight": g["edge_weight"],
        "w_gnn": g["L0_gnn_weight"].T,
        "w_qkv": g["L0_mix_w_qkv"], "w_proj": g["L0_mix_w_proj"], "b_proj": g["L0_mix_b_proj"],
        "gate_wT": g["L0_ffn_gate_w"].T, "gate_b": g["L0_ffn_gate_b"],
        "w1": w1.transpose(0, 2, 1).reshape(EXPERTS, K, P, FF).transpose(0, 2, 1, 3),
        "w2": w2.transpose(0, 2, 1).reshape(EXPERTS, FC, P, D).transpose(0, 2, 1, 3),
        "b1": b1.reshape(EXPERTS, FC, P).transpose(2, 0, 1),
        "rb1": g["L0_ffn_rb1"], "rb2": g["L0_ffn_rb2"], "sb2": g["L0_ffn_sb2"],
    }
    arrays = {k: _np.ascontiguousarray(v) for k, v in arrays.items()}
    nc = _bacc.Bacc("TRN2", target_bir_lowering=False, num_devices=1)
    A = {k: nc.dram_tensor(f"in_{k}", a.shape, _mybir.dt.from_np(a.dtype), kind="ExternalInput").ap() for k, a in arrays.items()}
    A["qT"] = nc.dram_tensor("qT_dram", (BLOCKS, P, K * BLK * P), F32).ap()
    A["h"] = nc.dram_tensor("h_dram", (N, D), F32).ap()
    A["cnt"] = nc.dram_tensor("cnt_dram", (ROWS // 32, 32 * TILES), F16).ap()
    A["aux"] = nc.dram_tensor("aux_dram", (2, ROWS // 32, 32 * TILES), F16).ap()
    A["recs"] = nc.dram_tensor("recs_dram", (E, 3), F32).ap()
    A["y1"] = nc.dram_tensor("y_dram", (N, D), F32).ap()
    A["yn"] = nc.dram_tensor("yn_dram", (N, D), F32).ap()
    A["slots"] = nc.dram_tensor("slots_dram", (SLOT_TILES * P, D), F32).ap()
    A["out"] = nc.dram_tensor("out_0", (N, D), F32, kind="ExternalOutput").ap()
    gps_layer(nc, A)
    r = _run(nc, [{f"in_{k}": a for k, a in arrays.items()}], core_ids=[0])
    return r.results[0]["out_0"]
```
